# Optimizing a Trainium2 kernel written in Bass

```python
import numpy as np
import jax
import jax.numpy as jnp

def _softmax(x, axis=-1):
    return jax.nn.softmax(x, axis=axis)

def _gelu(x):
    return jax.nn.gelu(x, approximate=True)

def _silu(x):
    return jax.nn.silu(x)

def _sigmoid(x):
    return jax.nn.sigmoid(x)

def _layernorm(x, axis=-1, eps=1e-05):
    m = jnp.mean(x, axis=axis, keepdims=True)
    v = jnp.var(x, axis=axis, keepdims=True)
    return (x - m) / jnp.sqrt(v + eps)

def _scatter_add(tgt, idx, src, axis=0):
    return tgt.at[idx].add(src)

def _segment_sum(src, seg, n):
    return jax.ops.segment_sum(src, seg, n)
kernel_name = 'mk_prb_d4_jaxref_r8_526540'

def setup_inputs(seed: int=0):
    np.random.seed(seed)
    _w = jnp.asarray

    def _L0_attn_setup():
        import jax, jax.numpy as jnp
        import numpy as np
        DIM = 256
        NUM_HEADS = 16
        HEAD_DIM = 128
        T_LEN = 256
        W_MAX = 1.0

        def _init_linear(key, out_f, in_f):
            std = 0.5 * in_f ** (-0.5)
            bound = 3.0 ** 0.5 * std
            return jax.random.uniform(key, (out_f, in_f), jnp.float32, -bound, bound)

        def _rope_tables(T, dh, dtype):
            af = (1.0 / 1024.0) ** jnp.linspace(0.0, 1.0, dh // 4, dtype=jnp.float32)
            af = jnp.concatenate([af, jnp.zeros(dh // 4, jnp.float32)])
            theta = jnp.arange(T, dtype=jnp.float32)[:, None] * af[None, :]
            return (jnp.cos(theta), jnp.sin(theta))

        def _apply_rope(x_BTHD, cos, sin):
            x = x_BTHD.astype(jnp.float32)
            x1, x2 = jnp.split(x, 2, axis=-1)
            c = cos[None, :, None, :]
            s = sin[None, :, None, :]
            y1 = x1 * c + x2 * s
            y2 = -x1 * s + x2 * c
            return jnp.concatenate([y1, y2], axis=-1).astype(x_BTHD.dtype)
        key = jax.random.key(seed)
        kx, kq, kk, kv, ko = jax.random.split(key, 5)
        hdim = NUM_HEADS * HEAD_DIM
        return {'x': jax.random.normal(kx, (1, T_LEN, DIM), jnp.float32), 'Wq': _init_linear(kq, hdim, DIM), 'Wk': _init_linear(kk, hdim, DIM), 'Wv': _init_linear(kv, hdim, DIM), 'Wo': _init_linear(ko, DIM, hdim)}
    _L0_attn_in = _L0_attn_setup()

    def _L0_ffn_setup():
        import jax, jax.numpy as jnp
        import numpy as np
        TOP_K = 4
        key = jax.random.key(seed)
        ks = jax.random.split(key, 5)
        H, I, E = (256, 96, 32)
        s = 0.02
        return {'hidden_states': jax.random.normal(ks[0], (1, 128, H), jnp.float32), 'router_w': jax.random.normal(ks[1], (E, H), jnp.float32) * s, 'gate_w': jax.random.normal(ks[2], (E, I, H), jnp.float32) * s, 'up_w': jax.random.normal(ks[3], (E, I, H), jnp.float32) * s, 'down_w': jax.random.normal(ks[4], (E, H, I), jnp.float32) * s}
    _L0_ffn_in = _L0_ffn_setup()

    def _L1_attn_setup():
        import jax, jax.numpy as jnp
        import numpy as np
        D_MODEL = 256
        D_INNER = 512
        D_STATE = 16
        DT_RANK = 128
        D_CONV = 4
        EPS = 1e-05

        def _rmsnorm(x, w):
            return x * jax.lax.rsqrt(jnp.mean(jnp.square(x), axis=-1, keepdims=True) + EPS) * w

        def _depthwise_causal_conv(x, conv_w, conv_b):
            k = conv_w[:, None, :]
            y = jax.lax.conv_general_dilated(x, k, window_strides=(1,), padding=((D_CONV - 1, 0),), dimension_numbers=('NWC', 'WIO', 'NWC'), feature_group_count=D_INNER)
            return y + conv_b

        def _selective_scan(u, delta, A, B, C, D):
            deltaA = jnp.exp(jnp.einsum('bld,dn->bldn', delta, A))
            deltaBu = jnp.einsum('bld,bln,bld->bldn', delta, B, u)
            dA = jnp.moveaxis(deltaA, 1, 0)
            dBu = jnp.moveaxis(deltaBu, 1, 0)
            Ct = jnp.moveaxis(C, 1, 0)
            b, l, d = u.shape
            n = A.shape[1]

            def step(h, inputs):
                dA_t, dBu_t, C_t = inputs
                h = h * dA_t + dBu_t
                y = jnp.einsum('bdn,bn->bd', h, C_t)
                return (h, y)
            h0 = jnp.zeros((b, d, n), u.dtype)
            _, ys = jax.lax.scan(step, h0, (dA, dBu, Ct))
            y = jnp.moveaxis(ys, 0, 1)
            return y + u * D
        key = jax.random.key(seed)
        ks = jax.random.split(key, 10)
        b, l = (1, 128)
        s = 0.02
        x = jax.random.normal(ks[0], (b, l, D_MODEL), jnp.float32)
        w_norm = jnp.ones((D_MODEL,), jnp.float32)
        W_in = jax.random.normal(ks[1], (D_MODEL, 2 * D_INNER), jnp.float32) * s
        conv_w = jax.random.normal(ks[2], (D_CONV, D_INNER), jnp.float32) * 0.3
        conv_b = jnp.zeros((D_INNER,), jnp.float32)
        W_xp = jax.random.normal(ks[3], (D_INNER, DT_RANK + 2 * D_STATE), jnp.float32) * s
        W_dt = jax.random.normal(ks[4], (DT_RANK, D_INNER), jnp.float32) * s
        b_dt = jnp.full((D_INNER,), -4.0, jnp.float32)
        A_log = jnp.log(jnp.tile(jnp.arange(1, D_STATE + 1, dtype=jnp.float32), (D_INNER, 1)))
        D = jnp.ones((D_INNER,), jnp.float32)
        W_out = jax.random.normal(ks[5], (D_INNER, D_MODEL), jnp.float32) * s
        return dict(x=x, w_norm=w_norm, W_in=W_in, conv_w=conv_w, conv_b=conv_b, W_xp=W_xp, W_dt=W_dt, b_dt=b_dt, A_log=A_log, D=D, W_out=W_out)
    _L1_attn_in = _L1_attn_setup()

    def _L1_ffn_setup():
        import jax, jax.numpy as jnp
        import numpy as np
        HIDDEN = 256
        INTER = 1024
        COMPRESSION = 128.9

        def _n_ctrl(out_size, in_size):
            return max(16, int(out_size * in_size / COMPRESSION))

        def _catmull_rom_grid(n_ctrl, n_samples):
            t = np.linspace(0.0, n_ctrl - 1.0, n_samples, dtype=np.float64)
            i = np.clip(np.floor(t).astype(np.int64), 0, n_ctrl - 2)
            f = (t - i).astype(np.float32)
            idx = np.stack([np.clip(i + k, 0, n_ctrl - 1) for k in (-1, 0, 1, 2)], axis=0)
            return (jnp.asarray(idx.astype(np.int32)), jnp.asarray(f))

        def spline_reconstruct(control_points, out_size, in_size):
            n = out_size * in_size
            idx, f = _catmull_rom_grid(control_points.shape[0], n)
            p0, p1, p2, p3 = (control_points[idx[0]], control_points[idx[1]], control_points[idx[2]], control_points[idx[3]])
            f2 = f * f
            f3 = f2 * f
            w = 0.5 * (2.0 * p1 + (p2 - p0) * f + (2.0 * p0 - 5.0 * p1 + 4.0 * p2 - p3) * f2 + (3.0 * p1 - p0 - 3.0 * p2 + p3) * f3)
            return w.reshape(out_size, in_size)
        key = jax.random.key(seed)
        k0, k1, k2, k3 = jax.random.split(key, 4)
        hidden_states = jax.random.normal(k0, (4, 256, HIDDEN), dtype=jnp.float32)
        gate_cp = jax.random.normal(k1, (_n_ctrl(INTER, HIDDEN),), dtype=jnp.float32) * 0.02
        up_cp = jax.random.normal(k2, (_n_ctrl(INTER, HIDDEN),), dtype=jnp.float32) * 0.02
        down_cp = jax.random.normal(k3, (_n_ctrl(HIDDEN, INTER),), dtype=jnp.float32) * 0.02
        return {'hidden_states': hidden_states, 'gate_cp': gate_cp, 'up_cp': up_cp, 'down_cp': down_cp}
    _L1_ffn_in = _L1_ffn_setup()

    def _L2_attn_setup():
        import jax, jax.numpy as jnp
        import numpy as np
        import math
        D_MODEL = 256
        D_STATE = 32
        R_MIN = 0.0
        R_MAX = 0.9
        MAX_PHASE = 6.283185307179586
        B_SZ = 4
        T_LEN = 256
        key = jax.random.key(seed)
        k_x, k_bre, k_bim, k_cre, k_cim = jax.random.split(key, 5)
        x = jax.random.normal(k_x, (B_SZ, T_LEN, D_MODEL), dtype=jnp.float32)
        u = np.linspace(0.0, 1.0, D_STATE, dtype=np.float64)
        mag_init = np.clip(R_MIN + (R_MAX - R_MIN) * u, 1e-06, 1.0 - 1e-06)
        nu_init = -np.log(mag_init)
        nu_log = jnp.asarray(np.log(np.clip(np.expm1(nu_init), 1e-06, None)), dtype=jnp.float32)
        theta_log = jnp.asarray(np.linspace(math.log(0.0001), math.log(MAX_PHASE), D_STATE), dtype=jnp.float32)
        B_re = jax.random.normal(k_bre, (D_STATE, D_MODEL), dtype=jnp.float32) / math.sqrt(D_MODEL)
        B_im = jax.random.normal(k_bim, (D_STATE, D_MODEL), dtype=jnp.float32) / math.sqrt(D_MODEL)
        C_re = jax.random.normal(k_cre, (D_MODEL, D_STATE), dtype=jnp.float32) / math.sqrt(D_STATE)
        C_im = jax.random.normal(k_cim, (D_MODEL, D_STATE), dtype=jnp.float32) / math.sqrt(D_STATE)
        D = jnp.ones((D_MODEL,), dtype=jnp.float32)
        return {'x': x, 'nu_log': nu_log, 'theta_log': theta_log, 'B_re': B_re, 'B_im': B_im, 'C_re': C_re, 'C_im': C_im, 'D': D}
    _L2_attn_in = _L2_attn_setup()

    def _L2_ffn_setup():
        import jax, jax.numpy as jnp
        import numpy as np
        HIDDEN = 256
        INTER = 688
        LUT_SIZE = 16

        def _ghost_linear(x, idx, lut):
            w = lut[idx]
            return jnp.einsum('bsh,oh->bso', x, w)
        key = jax.random.key(seed)
        k_x, k_lut, k_g, k_u, k_d = jax.random.split(key, 5)
        x = jax.random.normal(k_x, (2, 512, HIDDEN), dtype=jnp.float32)
        lut = jax.random.normal(k_lut, (LUT_SIZE,), dtype=jnp.float32) * 0.02
        gate_idx = jax.random.randint(k_g, (INTER, HIDDEN), 0, LUT_SIZE, dtype=jnp.int32)
        up_idx = jax.random.randint(k_u, (INTER, HIDDEN), 0, LUT_SIZE, dtype=jnp.int32)
        down_idx = jax.random.randint(k_d, (HIDDEN, INTER), 0, LUT_SIZE, dtype=jnp.int32)
        return {'x': x, 'lut': lut, 'gate_idx': gate_idx, 'up_idx': up_idx, 'down_idx': down_idx}
    _L2_ffn_in = _L2_ffn_setup()

    def _L3_attn_setup():
        import jax, jax.numpy as jnp
        import numpy as np
        B, T, D_MODEL = (4, 256, 256)
        NUM_HEADS, HEAD_SIZE = (16, 128)
        MODEL_SIZE = 256
        key = jax.random.key(seed)
        ks = jax.random.split(key, 9)
        s = 0.02 / np.sqrt(D_MODEL)
        so = 0.02 / np.sqrt(NUM_HEADS * HEAD_SIZE)
        return {'query': jax.random.normal(ks[0], (B, T, D_MODEL), jnp.float32), 'w_q': jax.random.normal(ks[1], (D_MODEL, NUM_HEADS * HEAD_SIZE), jnp.float32) * s, 'b_q': jnp.zeros((NUM_HEADS * HEAD_SIZE,), jnp.float32), 'w_k': jax.random.normal(ks[2], (D_MODEL, NUM_HEADS * HEAD_SIZE), jnp.float32) * s, 'b_k': jnp.zeros((NUM_HEADS * HEAD_SIZE,), jnp.float32), 'w_v': jax.random.normal(ks[3], (D_MODEL, NUM_HEADS * HEAD_SIZE), jnp.float32) * s, 'b_v': jnp.zeros((NUM_HEADS * HEAD_SIZE,), jnp.float32), 'w_o': jax.random.normal(ks[4], (NUM_HEADS * HEAD_SIZE, MODEL_SIZE), jnp.float32) * so, 'b_o': jnp.zeros((MODEL_SIZE,), jnp.float32)}
    _L3_attn_in = _L3_attn_setup()

    def _L3_ffn_setup():
        import jax, jax.numpy as jnp
        import numpy as np
        TOP_K = 2
        EPS = 1e-06
        key = jax.random.key(seed)
        ks = jax.random.split(key, 4)
        B, L, D, E, ED = (2, 256, 256, 8, 256)
        scale_gu = (6.0 / D) ** 0.5
        scale_dn = (6.0 / ED) ** 0.5
        return {'x': jax.random.normal(ks[0], (B, L, D), jnp.float32), 'router_scale': jnp.ones((D,), jnp.float32), 'gate_w': jax.random.normal(ks[1], (D, E), jnp.float32) * D ** (-0.5), 'gate_up': jax.random.uniform(ks[2], (E, D, 2 * ED), jnp.float32, -scale_gu, scale_gu), 'down': jax.random.uniform(ks[3], (E, ED, D), jnp.float32, -scale_dn, scale_dn), 'per_expert_scale': jnp.ones((E,), jnp.float32)}
    _L3_ffn_in = _L3_ffn_setup()
    _d = {'L0_attn_x': _L0_attn_in['x'], 'L0_attn_Wq': _L0_attn_in['Wq'], 'L0_attn_Wk': _L0_attn_in['Wk'], 'L0_attn_Wv': _L0_attn_in['Wv'], 'L0_attn_Wo': _L0_attn_in['Wo'], 'L0_ffn_router_w': _L0_ffn_in['router_w'], 'L0_ffn_gate_w': _L0_ffn_in['gate_w'], 'L0_ffn_up_w': _L0_ffn_in['up_w'], 'L0_ffn_down_w': _L0_ffn_in['down_w'], 'L1_attn_w_norm': _L1_attn_in['w_norm'], 'L1_attn_W_in': _L1_attn_in['W_in'], 'L1_attn_conv_w': _L1_attn_in['conv_w'], 'L1_attn_conv_b': _L1_attn_in['conv_b'], 'L1_attn_W_xp': _L1_attn_in['W_xp'], 'L1_attn_W_dt': _L1_attn_in['W_dt'], 'L1_attn_b_dt': _L1_attn_in['b_dt'], 'L1_attn_A_log': _L1_attn_in['A_log'], 'L1_attn_D': _L1_attn_in['D'], 'L1_attn_W_out': _L1_attn_in['W_out'], 'L1_ffn_gate_cp': _L1_ffn_in['gate_cp'], 'L1_ffn_up_cp': _L1_ffn_in['up_cp'], 'L1_ffn_down_cp': _L1_ffn_in['down_cp'], 'L2_attn_nu_log': _L2_attn_in['nu_log'], 'L2_attn_theta_log': _L2_attn_in['theta_log'], 'L2_attn_B_re': _L2_attn_in['B_re'], 'L2_attn_B_im': _L2_attn_in['B_im'], 'L2_attn_C_re': _L2_attn_in['C_re'], 'L2_attn_C_im': _L2_attn_in['C_im'], 'L2_attn_D': _L2_attn_in['D'], 'L2_ffn_lut': _L2_ffn_in['lut'], 'L2_ffn_gate_idx': _L2_ffn_in['gate_idx'], 'L2_ffn_up_idx': _L2_ffn_in['up_idx'], 'L2_ffn_down_idx': _L2_ffn_in['down_idx'], 'L3_attn_w_q': _L3_attn_in['w_q'], 'L3_attn_b_q': _L3_attn_in['b_q'], 'L3_attn_w_k': _L3_attn_in['w_k'], 'L3_attn_b_k': _L3_attn_in['b_k'], 'L3_attn_w_v': _L3_attn_in['w_v'], 'L3_attn_b_v': _L3_attn_in['b_v'], 'L3_attn_w_o': _L3_attn_in['w_o'], 'L3_attn_b_o': _L3_attn_in['b_o'], 'L3_ffn_router_scale': _L3_ffn_in['router_scale'], 'L3_ffn_gate_w': _L3_ffn_in['gate_w'], 'L3_ffn_gate_up': _L3_ffn_in['gate_up'], 'L3_ffn_down': _L3_ffn_in['down'], 'L3_ffn_per_expert_scale': _L3_ffn_in['per_expert_scale']}
    _x0 = _d['L0_attn_x']
    _d['L0_attn_x'] = jax.random.normal(jax.random.fold_in(jax.random.key(seed), 1), (2, 512, 256), dtype=_x0.dtype)
    del _x0
    return _d

def reference(L0_attn_x, L0_attn_Wq, L0_attn_Wk, L0_attn_Wv, L0_attn_Wo, L0_ffn_router_w, L0_ffn_gate_w, L0_ffn_up_w, L0_ffn_down_w, L1_attn_w_norm, L1_attn_W_in, L1_attn_conv_w, L1_attn_conv_b, L1_attn_W_xp, L1_attn_W_dt, L1_attn_b_dt, L1_attn_A_log, L1_attn_D, L1_attn_W_out, L1_ffn_gate_cp, L1_ffn_up_cp, L1_ffn_down_cp, L2_attn_nu_log, L2_attn_theta_log, L2_attn_B_re, L2_attn_B_im, L2_attn_C_re, L2_attn_C_im, L2_attn_D, L2_ffn_lut, L2_ffn_gate_idx, L2_ffn_up_idx, L2_ffn_down_idx, L3_attn_w_q, L3_attn_b_q, L3_attn_w_k, L3_attn_b_k, L3_attn_w_v, L3_attn_b_v, L3_attn_w_o, L3_attn_b_o, L3_ffn_router_scale, L3_ffn_gate_w, L3_ffn_gate_up, L3_ffn_down, L3_ffn_per_expert_scale):

    def _L0_attn_ref(x, Wq, Wk, Wv, Wo):
        import jax, jax.numpy as jnp
        import numpy as np
        DIM = 256
        NUM_HEADS = 16
        HEAD_DIM = 128
        T_LEN = 256
        W_MAX = 1.0

        def _init_linear(key, out_f, in_f):
            std = 0.5 * in_f ** (-0.5)
            bound = 3.0 ** 0.5 * std
            return jax.random.uniform(key, (out_f, in_f), jnp.float32, -bound, bound)

        def _rope_tables(T, dh, dtype):
            af = (1.0 / 1024.0) ** jnp.linspace(0.0, 1.0, dh // 4, dtype=jnp.float32)
            af = jnp.concatenate([af, jnp.zeros(dh // 4, jnp.float32)])
            theta = jnp.arange(T, dtype=jnp.float32)[:, None] * af[None, :]
            return (jnp.cos(theta), jnp.sin(theta))

        def _apply_rope(x_BTHD, cos, sin):
            x = x_BTHD.astype(jnp.float32)
            x1, x2 = jnp.split(x, 2, axis=-1)
            c = cos[None, :, None, :]
            s = sin[None, :, None, :]
            y1 = x1 * c + x2 * s
            y2 = -x1 * s + x2 * c
            return jnp.concatenate([y1, y2], axis=-1).astype(x_BTHD.dtype)
        B, T, _ = x.shape
        H, Dh = (NUM_HEADS, HEAD_DIM)
        scale = Dh ** 0.5 / W_MAX ** 2 / Dh
        q = (x @ Wq.T).reshape(B, T, H, Dh)
        k = (x @ Wk.T).reshape(B, T, H, Dh)
        v = (x @ Wv.T).reshape(B, T, H, Dh)
        cos, sin = _rope_tables(T, Dh, x.dtype)
        q = _apply_rope(q, cos, sin)
        k = _apply_rope(k, cos, sin)
        scores = jnp.einsum('bthd,bshd->bhts', q, k) * scale
        causal = jnp.tril(jnp.ones((T, T), bool))
        scores = jnp.where(causal[None, None], scores, -jnp.inf)
        attn = jax.nn.softmax(scores, axis=-1)
        y = jnp.einsum('bhts,bshd->bthd', attn, v).reshape(B, T, H * Dh)
        return y / 3.0 @ Wo.T

    def _L0_ffn_ref(hidden_states, router_w, gate_w, up_w, down_w):
        import jax, jax.numpy as jnp
        import numpy as np
        TOP_K = 4
        B, S, H = hidden_states.shape
        E = router_w.shape[0]
        x = hidden_states.reshape(-1, H)
        logits = x @ router_w.T
        probs = jax.nn.softmax(logits.astype(jnp.float32), axis=-1)
        rw, sel = jax.lax.top_k(probs, TOP_K)
        rw = rw / jnp.sum(rw, axis=-1, keepdims=True)
        rw = rw.astype(x.dtype)

        def body(acc, expert):
            gw, uw, dw, e = expert
            w_tok = jnp.sum(jnp.where(sel == e, rw, 0.0), axis=-1)
            h = jax.nn.silu(x @ gw.T) * (x @ uw.T)
            y = h @ dw.T
            return (acc + w_tok[:, None] * y, None)
        acc0 = jnp.zeros_like(x)
        out, _ = jax.lax.scan(body, acc0, (gate_w, up_w, down_w, jnp.arange(E)))
        return out.reshape(B, S, H)

    def _L1_attn_ref(x, w_norm, W_in, conv_w, conv_b, W_xp, W_dt, b_dt, A_log, D, W_out):
        import jax, jax.numpy as jnp
        import numpy as np
        D_MODEL = 256
        D_INNER = 512
        D_STATE = 16
        DT_RANK = 128
        D_CONV = 4
        EPS = 1e-05

        def _rmsnorm(x, w):
            return x * jax.lax.rsqrt(jnp.mean(jnp.square(x), axis=-1, keepdims=True) + EPS) * w

        def _depthwise_causal_conv(x, conv_w, conv_b):
            k = conv_w[:, None, :]
            y = jax.lax.conv_general_dilated(x, k, window_strides=(1,), padding=((D_CONV - 1, 0),), dimension_numbers=('NWC', 'WIO', 'NWC'), feature_group_count=D_INNER)
            return y + conv_b

        def _selective_scan(u, delta, A, B, C, D):
            deltaA = jnp.exp(jnp.einsum('bld,dn->bldn', delta, A))
            deltaBu = jnp.einsum('bld,bln,bld->bldn', delta, B, u)
            dA = jnp.moveaxis(deltaA, 1, 0)
            dBu = jnp.moveaxis(deltaBu, 1, 0)
            Ct = jnp.moveaxis(C, 1, 0)
            b, l, d = u.shape
            n = A.shape[1]

            def step(h, inputs):
                dA_t, dBu_t, C_t = inputs
                h = h * dA_t + dBu_t
                y = jnp.einsum('bdn,bn->bd', h, C_t)
                return (h, y)
            h0 = jnp.zeros((b, d, n), u.dtype)
            _, ys = jax.lax.scan(step, h0, (dA, dBu, Ct))
            y = jnp.moveaxis(ys, 0, 1)
            return y + u * D
        xn = _rmsnorm(x, w_norm)
        xz = xn @ W_in
        xs, res = jnp.split(xz, 2, axis=-1)
        xs = _depthwise_causal_conv(xs, conv_w, conv_b)
        xs = jax.nn.silu(xs)
        A = -jnp.exp(A_log)
        xdbc = xs @ W_xp
        dt_r = xdbc[..., :DT_RANK]
        B = xdbc[..., DT_RANK:DT_RANK + D_STATE]
        C = xdbc[..., DT_RANK + D_STATE:]
        delta = jax.nn.softplus(dt_r @ W_dt + b_dt)
        y = _selective_scan(xs, delta, A, B, C, D)
        y = y * jax.nn.silu(res)
        out = y @ W_out + x
        return out

    def _L1_ffn_ref(hidden_states, gate_cp, up_cp, down_cp):
        import jax, jax.numpy as jnp
        import numpy as np
        HIDDEN = 256
        INTER = 1024
        COMPRESSION = 128.9

        def _n_ctrl(out_size, in_size):
            return max(16, int(out_size * in_size / COMPRESSION))

        def _catmull_rom_grid(n_ctrl, n_samples):
            t = np.linspace(0.0, n_ctrl - 1.0, n_samples, dtype=np.float64)
            i = np.clip(np.floor(t).astype(np.int64), 0, n_ctrl - 2)
            f = (t - i).astype(np.float32)
            idx = np.stack([np.clip(i + k, 0, n_ctrl - 1) for k in (-1, 0, 1, 2)], axis=0)
            return (jnp.asarray(idx.astype(np.int32)), jnp.asarray(f))

        def spline_reconstruct(control_points, out_size, in_size):
            n = out_size * in_size
            idx, f = _catmull_rom_grid(control_points.shape[0], n)
            p0, p1, p2, p3 = (control_points[idx[0]], control_points[idx[1]], control_points[idx[2]], control_points[idx[3]])
            f2 = f * f
            f3 = f2 * f
            w = 0.5 * (2.0 * p1 + (p2 - p0) * f + (2.0 * p0 - 5.0 * p1 + 4.0 * p2 - p3) * f2 + (3.0 * p1 - p0 - 3.0 * p2 + p3) * f3)
            return w.reshape(out_size, in_size)
        gate_w = spline_reconstruct(gate_cp, INTER, HIDDEN)
        up_w = spline_reconstruct(up_cp, INTER, HIDDEN)
        down_w = spline_reconstruct(down_cp, HIDDEN, INTER)
        gate = jnp.einsum('bsh,ih->bsi', hidden_states, gate_w)
        up = jnp.einsum('bsh,ih->bsi', hidden_states, up_w)
        inter = jax.nn.silu(gate) * up
        return jnp.einsum('bsi,hi->bsh', inter, down_w)

    def _L2_attn_ref(x, nu_log, theta_log, B_re, B_im, C_re, C_im, D):
        import jax, jax.numpy as jnp
        import numpy as np
        import math
        D_MODEL = 256
        D_STATE = 32
        R_MIN = 0.0
        R_MAX = 0.9
        MAX_PHASE = 6.283185307179586
        B_SZ = 4
        T_LEN = 256
        nu = jax.nn.softplus(nu_log)
        mag = jnp.exp(-jnp.exp(nu))
        theta = jnp.exp(theta_log)
        A_re = mag * jnp.cos(theta)
        A_im = mag * jnp.sin(theta)
        gamma = jnp.sqrt(jnp.clip(1.0 - mag * mag, 0.0))
        gB_re = gamma[:, None] * B_re
        gB_im = gamma[:, None] * B_im
        Bu_re = jnp.einsum('btd,nd->btn', x, gB_re)
        Bu_im = jnp.einsum('btd,nd->btn', x, gB_im)

        def step(h, bu):
            h_re, h_im = h
            bu_re, bu_im = bu
            new_re = A_re * h_re - A_im * h_im + bu_re
            new_im = A_re * h_im + A_im * h_re + bu_im
            return ((new_re, new_im), (new_re, new_im))
        Bsz = x.shape[0]
        h0 = jnp.zeros((Bsz, A_re.shape[0]), dtype=x.dtype)
        _, (H_re, H_im) = jax.lax.scan(step, (h0, h0), (jnp.swapaxes(Bu_re, 0, 1), jnp.swapaxes(Bu_im, 0, 1)))
        H_re = jnp.swapaxes(H_re, 0, 1)
        H_im = jnp.swapaxes(H_im, 0, 1)
        y = jnp.einsum('btn,dn->btd', H_re, C_re) - jnp.einsum('btn,dn->btd', H_im, C_im) + D * x
        return y

    def _L2_ffn_ref(x, lut, gate_idx, up_idx, down_idx):
        import jax, jax.numpy as jnp
        import numpy as np
        HIDDEN = 256
        INTER = 688
        LUT_SIZE = 16

        def _ghost_linear(x, idx, lut):
            w = lut[idx]
            return jnp.einsum('bsh,oh->bso', x, w)
        gate = _ghost_linear(x, gate_idx, lut)
        up = _ghost_linear(x, up_idx, lut)
        h = jax.nn.silu(gate) * up
        return _ghost_linear(h, down_idx, lut)

    def _L3_attn_ref(query, w_q, b_q, w_k, b_k, w_v, b_v, w_o, b_o):
        import jax, jax.numpy as jnp
        import numpy as np
        B, T, D_MODEL = (4, 256, 256)
        NUM_HEADS, HEAD_SIZE = (16, 128)
        MODEL_SIZE = 256
        B_, T_, _ = query.shape
        q = (query @ w_q + b_q).reshape(B_, T_, NUM_HEADS, HEAD_SIZE)
        k = (query @ w_k + b_k).reshape(B_, T_, NUM_HEADS, HEAD_SIZE)
        v = (query @ w_v + b_v).reshape(B_, T_, NUM_HEADS, HEAD_SIZE)
        logits = jnp.einsum('bthd,bThd->bhtT', q, k) * jax.lax.rsqrt(jnp.float32(HEAD_SIZE))
        i = jnp.arange(T_, dtype=jnp.int32)[:, None]
        j = jnp.arange(T_, dtype=jnp.int32)
        mask = (i >= j).astype(logits.dtype)
        logits = logits - 10000000000.0 * (1.0 - mask)
        weights = jax.nn.softmax(logits, axis=-1)
        attn = jnp.einsum('bhtT,bThd->bthd', weights, v).reshape(B_, T_, NUM_HEADS * HEAD_SIZE)
        out = attn @ w_o + b_o
        return out

    def _L3_ffn_ref(x, router_scale, gate_w, gate_up, down, per_expert_scale):
        import jax, jax.numpy as jnp
        import numpy as np
        TOP_K = 2
        EPS = 1e-06
        B, L, D = x.shape
        E = gate_up.shape[0]
        h = x * jax.lax.rsqrt(jnp.mean(x * x, axis=-1, keepdims=True) + EPS)
        h = h * D ** (-0.5) * router_scale
        logits = (h @ gate_w).astype(jnp.float32)
        probs = jax.nn.softmax(logits, axis=-1)
        w, idx = jax.lax.top_k(probs, TOP_K)
        w = w / jnp.clip(jnp.sum(w, axis=-1, keepdims=True), 1e-12)
        w = w.astype(x.dtype)
        N = B * L
        xf = x.reshape(N, D)
        idxf = idx.reshape(N, TOP_K)
        wf = w.reshape(N, TOP_K)
        combine = jnp.zeros((N, E), x.dtype).at[jnp.arange(N)[:, None], idxf].add(wf)
        hh = jnp.einsum('nd,edf->nef', xf, gate_up)
        gate, up = jnp.split(hh, 2, axis=-1)
        act = jax.nn.gelu(gate, approximate=False) * up
        y = jnp.einsum('nef,efd->ned', act, down)
        out = jnp.einsum('ne,ned->nd', combine * per_expert_scale, y)
        return out.reshape(B, L, D)
    x = L0_attn_x
    xn = _layernorm(x, axis=-1)
    x = x + _L0_attn_ref(xn, L0_attn_Wq, L0_attn_Wk, L0_attn_Wv, L0_attn_Wo) + _L0_ffn_ref(xn, L0_ffn_router_w, L0_ffn_gate_w, L0_ffn_up_w, L0_ffn_down_w)
    xn = _layernorm(x, axis=-1)
    x = x + _L1_attn_ref(xn, L1_attn_w_norm, L1_attn_W_in, L1_attn_conv_w, L1_attn_conv_b, L1_attn_W_xp, L1_attn_W_dt, L1_attn_b_dt, L1_attn_A_log, L1_attn_D, L1_attn_W_out) + _L1_ffn_ref(xn, L1_ffn_gate_cp, L1_ffn_up_cp, L1_ffn_down_cp)
    xn = _layernorm(x, axis=-1)
    x = x + _L2_attn_ref(xn, L2_attn_nu_log, L2_attn_theta_log, L2_attn_B_re, L2_attn_B_im, L2_attn_C_re, L2_attn_C_im, L2_attn_D) + _L2_ffn_ref(xn, L2_ffn_lut, L2_ffn_gate_idx, L2_ffn_up_idx, L2_ffn_down_idx)
    xn = _layernorm(x, axis=-1)
    x = x + _L3_attn_ref(xn, L3_attn_w_q, L3_attn_b_q, L3_attn_w_k, L3_attn_b_k, L3_attn_w_v, L3_attn_b_v, L3_attn_w_o, L3_attn_b_o) + _L3_ffn_ref(xn, L3_ffn_router_scale, L3_ffn_gate_w, L3_ffn_gate_up, L3_ffn_down, L3_ffn_per_expert_scale)
    return x

_drawn_inputs = setup_inputs


def setup_inputs(seed=0):
    import zlib

    import numpy as np

    out = dict(_drawn_inputs(seed))
    spreads = {'L1_attn_w_norm': (1.0, 0.6),
     'L1_attn_conv_b': (0.0, 0.8),
     'L1_attn_b_dt': (-4.0, 0.6),
     'L1_attn_D': (1.0, 0.6),
     'L2_attn_D': (1.0, 0.2),
     'L3_attn_b_q': (0.0, 2.0),
     'L3_attn_b_k': (0.0, 2.0),
     'L3_attn_b_v': (0.0, 2.0),
     'L3_attn_b_o': (0.0, 0.3),
     'L3_ffn_router_scale': (1.0, 0.2),
     'L3_ffn_per_expert_scale': (1.0, 0.2)}
    factors = {'L0_attn_Wq': 3.295,
     'L1_attn_conv_w': 2.672,
     'L1_attn_W_xp': 8.0,
     'L1_attn_W_dt': 8.0,
     'L1_attn_A_log': 8.0,
     'L3_attn_w_q': 199.029,
     'L3_attn_w_k': 64.0,
     'L3_attn_w_v': 64.0,
     'L3_attn_w_o': 8.0}
    for name, (base, spread) in spreads.items():
        noise = np.random.default_rng([zlib.crc32(name.encode()), seed]).standard_normal(out[name].shape)
        drawn = base * np.exp(spread * noise) if base else spread * noise
        out[name] = jnp.asarray(drawn.astype(out[name].dtype))
    for name, factor in factors.items():
        out[name] = (out[name] * factor).astype(out[name].dtype)
    return out
```

```python
from contextlib import ExitStack

import numpy as np

import concourse.bass as bass
from concourse import mybir

FP32 = mybir.dt.float32
BF16 = mybir.dt.bfloat16
INT32 = mybir.dt.int32
ACT = mybir.ActivationFunctionType
ALU = mybir.AluOpType
AXIS = mybir.AxisListType

P = 128
BATCH, T, D = 2, 512, 256
NT = T // P
KD = D // P
HEADS, HD = 16, 128
QK_SCALE = float(HD) ** -0.5
MASKED = -1e30

E0, TOP0, I0 = 32, 4, 96
E3, TOP3, I3 = 8, 2, 256
GROUPS = 8
F0 = E0 * I0 // GROUPS
F3 = E3 * I3 // GROUPS

CH, NS, RANK, TAPS = 512, 16, 128, 4
KC = CH // P
INTER1 = 1024
NCTRL = max(16, int(INTER1 * D / 128.9))
WINDOW = 6
STATES = 32
INTER2 = 688
F2 = INTER2 // 2
F2_ROWS = (P, P, F2 - 2 * P)
LUT = 16
LUT_COLS = KD * 2 * INTER2 + 6 * D
LUT_CHUNK = LUT_COLS // 8
TWO_PI = 2.0 * np.pi


class Signal:

    def __init__(self, nc, ctx, name):
        self.sem = ctx.enter_context(nc.semaphore(name))
        self.base = 0

    def at(self, n):
        return self.base + n

    def close(self, n):
        self.base = self.base + n


class Chain:

    def __init__(self, eng, count, start=0):
        self.eng, self.count, self.start, self.n = eng, count, start, 0

    def link(self, instruction):
        instruction.then_inc(self.count.sem, 1)
        self.n += 1

    def wait(self):
        self.eng.wait_ge(self.count.sem, self.count.at(self.start + self.n))

    def all(self, instruction):
        self.link(instruction)
        self.wait()


class Machine:

    def __init__(self, nc, ctx, dram):
        self.nc, self.ctx, self.dram = nc, ctx, dram
        self.signals = {}
        sb = lambda name, shape, dt=FP32: ctx.enter_context(nc.sbuf_tensor(name, shape, dt))
        self.x = sb("x", [P, NT, D])
        self.xn = sb("xn", [P, NT, D])
        self.xnT = sb("xnT", [P, KD, T])
        self.stats = sb("stats", [P, NT, 6])
        self.mv = sb("mv", [P, NT, 2])
        self.rs = sb("rs", [P, 6, NT])
        self.ident = sb("ident", [P, P])
        self.ident_bf = sb("ident_bf", [P, P], BF16)
        self.mask_bf = sb("mask_bf", [P, P], BF16)
        self.zero_row = sb("zero_row", [1, T])
        self.one_row = sb("one_row", [1, P])
        self.bo_row = sb("bo_row", [1, 2, D])
        self.spline_gu = sb("spline_gu", [P, KD, 2, INTER1])
        self.spline_down = sb("spline_down", [P, INTER1 // P, D])
        self.lut_w = sb("lut_w", [P, LUT_COLS])
        self.lru_step = sb("lru_step", [2 * STATES, 9, 2 * STATES])
        self.lru_gamma = sb("lru_gamma", [2 * STATES, 1])
        self.acc = ctx.enter_context(nc.psum_tensor("acc", [P, 2, 512], FP32))
        self.banks = ctx.enter_context(nc.psum_tensor("banks", [P, 6, 512], FP32))

    def sig(self, name):
        if name not in self.signals:
            self.signals[name] = Signal(self.nc, self.ctx, name)
        return self.signals[name]

    def local(self, stage_ctx):
        self.n_local = 1 + (self.n_local if hasattr(self, "n_local") else 0)
        tag = self.n_local
        return lambda name, shape, dt=FP32: stage_ctx.enter_context(
            self.nc.sbuf_tensor(f"{name}_{tag}", shape, dt))

    def acc_tile(self, t):
        return self.acc[:, t // 2, (t % 2) * D:(t % 2 + 1) * D]


def reciprocal_root(nc, chain, rs):
    chain.all(nc.vector.reciprocal(rs[:, 2], rs[:, 1]))
    chain.all(nc.vector.tensor_tensor(rs[:, 4], rs[:, 2], rs[:, 2], ALU.mult))
    chain.all(nc.vector.tensor_tensor(rs[:, 4], rs[:, 4], rs[:, 0], ALU.mult))
    chain.all(nc.vector.tensor_scalar(rs[:, 4], rs[:, 4], -0.5, 1.5, ALU.mult, ALU.add))
    chain.all(nc.vector.tensor_tensor(rs[:, 3], rs[:, 2], rs[:, 4], ALU.mult))


def prepare(m):
    nc, dram = m.nc, m.dram
    with ExitStack() as local_ctx:
        sb = m.local(local_ctx)
        coef = sb("coef", [P, 2, WINDOW, D])
        points = sb("points", [P, 8, 3, WINDOW])
        spline_rows = sb("spline_rows", [P, 2, 3, D])
        term = sb("term", [P, 2, 3, D])
        idx = sb("idx", [P, 2, LUT_CHUNK], INT32)
        bits = sb("bits", [P, 4, LUT_CHUNK], INT32)
        leaves = sb("leaves", [P, 7, LUT_CHUNK])
        table = sb("table", [P, LUT])
        delta = sb("delta", [P, LUT // 2])
        lru_in = sb("lru_in", [2 * STATES, 2])
        lru_sign = sb("lru_sign", [2 * STATES, 4])
        lru_fold = sb("lru_fold", [2 * STATES, STATES])
        lru = sb("lru", [2 * STATES, 24])
        turns = sb("turns", [2 * STATES, 1], INT32)
        power = sb("power", [2 * STATES, 2, 9])
        blend = sb("blend", [2 * STATES, 4, 9])
        loaded = m.sig("constants_loaded")
        coef_loaded = [m.sig(f"coef_loaded{i}") for i in range(2)]
        idx_loaded = [m.sig(f"idx_loaded{i}") for i in range(2)]
        rows_made, rows_turned, turned_stored = m.sig("rows_made"), m.sig("rows_turned"), m.sig("turned_stored")
        chunk_read = m.sig("chunk_read")
        dve_chain, act_chain, pool_chain = m.sig("dve_chain"), m.sig("act_chain"), m.sig("pool_chain")
        lru_act, lru_dve = m.sig("lru_act"), m.sig("lru_dve")
        constants = [
            (m.ident[:], dram["ident"]), (m.ident_bf[:], dram["ident_bf"]), (m.mask_bf[:], dram["mask_bf"]),
            (m.bo_row[:, 0, :], dram["bo"]), (m.bo_row[:, 1, :], dram["bo"]),
            (points[:], dram["spline_points"]), (table[:], dram["lut"].broadcast_to([P, LUT])),
            (lru_in[:], dram["lru_in"]), (lru_sign[:], dram["lru_sign"]), (lru_fold[:], dram["lru_fold"]),
        ]

        with nc.Block() as block:
            @block.sync
            def _(sp):
                for dst, src in constants:
                    sp.dma_start(dst, src).then_inc(loaded.sem, 16)
                for n in range(8):
                    if n >= 2:
                        sp.wait_ge(chunk_read.sem, chunk_read.at(n - 1))
                        sp.wait_ge(rows_made.sem, rows_made.at(n - 1))
                    sp.dma_start(idx[:, n % 2], dram["lut_idx"][:, n * LUT_CHUNK:(n + 1) * LUT_CHUNK])\
                      .then_inc(idx_loaded[n % 2].sem, 16)
                    sp.dma_start(coef[:, n % 2], dram["spline_coef"][n]).then_inc(coef_loaded[n % 2].sem, 16)

            @block.gpsimd
            def _(pool):
                pool.wait_ge(loaded.sem, loaded.at(16 * len(constants)))
                chain = Chain(pool, pool_chain)
                for n in range(8):
                    pool.wait_ge(coef_loaded[n % 2].sem, coef_loaded[n % 2].at(16 * (n // 2 + 1)))
                    if n >= 2:
                        pool.wait_ge(rows_turned.sem, rows_turned.at(n - 1))
                    rows = spline_rows[:, n % 2]
                    for j in range(WINDOW):
                        for w in range(3):
                            out = term[:, j % 2, w] if j else rows[:, w]
                            chain.link(nc.gpsimd.tensor_scalar(out, coef[:, n % 2, j], points[:, n, w, j:j + 1], 1.0,
                                                               ALU.mult, ALU.mult))
                        chain.wait()
                        if j:
                            last = nc.gpsimd.tensor_tensor(rows, rows, term[:, j % 2], ALU.add)
                            if j < WINDOW - 1:
                                chain.link(last)
                    last.then_inc(rows_made.sem, 1)
                pool_chain.close(chain.n)

            @block.tensor
            def _(pe):
                pe.wait_ge(loaded.sem, loaded.at(16 * len(constants)))
                for n in range(8):
                    pe.wait_ge(rows_made.sem, rows_made.at(n + 1))
                    if n >= 2:
                        pe.wait_ge(turned_stored.sem, turned_stored.at(n - 1))
                    for w in range(3):
                        for k in range(KD):
                            b = 2 * (n % 2) + w // 2
                            at = ((w % 2) * 2 + k) * P
                            last = nc.tensor.transpose(m.banks[:, b, at:at + P],
                                                       spline_rows[:, n % 2, w, k * P:(k + 1) * P], m.ident[:])
                    last.then_inc(rows_turned.sem, 1)

            @block.scalar
            def _(act):
                act.wait_ge(loaded.sem, loaded.at(16 * len(constants)))
                chain = Chain(act, act_chain)
                chain.all(nc.scalar.activation(lru[:, 0:1], lru_in[:, 0:1], ACT.Abs))
                chain.all(nc.scalar.activation(lru[:, 1:2], lru[:, 0:1], ACT.Exp, scale=-1.0))
                nc.scalar.activation(lru[:, 3:4], lru_in[:, 1:2], ACT.Exp).then_inc(lru_act.sem, 1)
                chain.all(nc.scalar.activation(lru[:, 2:3], lru[:, 1:2], ACT.Ln, bias=1.0))
                act.wait_ge(lru_dve.sem, lru_dve.at(1))
                chain.all(nc.scalar.activation(lru[:, 5:6], lru[:, 4:5], ACT.Identity, bias=lru[:, 2:3]))
                chain.all(nc.scalar.activation(lru[:, 6:7], lru[:, 5:6], ACT.Exp))
                nc.scalar.activation(lru[:, 7:8], lru[:, 6:7], ACT.Exp, scale=-1.0).then_inc(lru_act.sem, 1)
                act.wait_ge(lru_dve.sem, lru_dve.at(2))
                nc.scalar.activation(lru[:, 14:15], lru[:, 12:13], ACT.Sin)
                nc.scalar.activation(lru[:, 15:16], lru[:, 13:14], ACT.Sin).then_inc(lru_act.sem, 1)
                act.wait_ge(lru_dve.sem, lru_dve.at(3))
                nc.scalar.activation(m.lru_gamma[:], lru[:, 17:18], ACT.Sqrt)
                act_chain.close(chain.n)
                for n in range(8):
                    act.wait_ge(rows_turned.sem, rows_turned.at(n + 1))
                    half, q = divmod(n, 4)
                    b = 2 * (n % 2)
                    for w in range(2):
                        out = m.spline_gu[:, :, w, half * 512:(half + 1) * 512]
                        out = out.rearrange("p k (c q) -> p k q c", q=4)[:, :, q, :]
                        src = m.banks[:, b, w * 2 * P:(w + 1) * 2 * P].rearrange("p (k c) -> p k c", k=KD)
                        nc.scalar.activation(out, src, ACT.Copy)
                    src = m.banks[:, b + 1, 0:2 * P].rearrange("p (k c) -> p k c", k=KD)
                    nc.scalar.activation(m.spline_down[:, 2 * q:2 * q + 2, half * P:(half + 1) * P], src, ACT.Copy)\
                      .then_inc(turned_stored.sem, 1)

            @block.vector
            def _(dve):
                chain = Chain(dve, dve_chain)
                nc.vector.memset(m.zero_row[:], 0.0)
                nc.vector.memset(m.one_row[:], 1.0)
                dve.wait_ge(loaded.sem, loaded.at(16 * len(constants)))
                nc.vector.tensor_scalar(lru[:, 4:5], lru_in[:, 0:1], 0.0, None, ALU.max).then_inc(lru_dve.sem, 1)
                dve.wait_ge(lru_act.sem, lru_act.at(1))
                chain.all(nc.vector.tensor_scalar(turns[:], lru[:, 3:4], float(1.0 / TWO_PI), None, ALU.mult))
                chain.all(nc.vector.tensor_copy(lru[:, 8:9], turns[:]))
                c1 = 6.28125
                c2 = float(np.float32(TWO_PI - c1))
                c2 = float(np.frombuffer(np.uint32(np.float32(c2).view(np.uint32) & 0xFFFFF000).tobytes(), np.float32)[0])
                c3 = float(TWO_PI - c1 - c2)
                chain.all(nc.vector.scalar_tensor_tensor(lru[:, 9:10], lru[:, 8:9], -c1, lru[:, 3:4], ALU.mult, ALU.add))
                chain.all(nc.vector.scalar_tensor_tensor(lru[:, 10:11], lru[:, 8:9], -c2, lru[:, 9:10], ALU.mult, ALU.add))
                chain.all(nc.vector.scalar_tensor_tensor(lru[:, 11:12], lru[:, 8:9], -c3, lru[:, 10:11], ALU.mult, ALU.add))
                fold_turn(nc, chain, lru, 11, 16, 18)
                chain.all(nc.vector.tensor_scalar(lru[:, 19:20], lru[:, 16:17], float(np.pi / 2), None, ALU.add))
                fold_turn(nc, chain, lru, 19, 20, 18)
                limit = float(np.nextafter(np.float32(np.pi), np.float32(0)))
                chain.all(nc.vector.tensor_scalar(lru[:, 12:13], lru[:, 16:17], -limit, limit, ALU.max, ALU.min))
                nc.vector.tensor_scalar(lru[:, 13:14], lru[:, 20:21], -limit, limit, ALU.max, ALU.min)\
                  .then_inc(lru_dve.sem, 1)
                dve.wait_ge(lru_act.sem, lru_act.at(3))
                chain.all(nc.vector.tensor_tensor(lru[:, 21:22], lru[:, 7:8], lru[:, 7:8], ALU.mult))
                chain.all(nc.vector.tensor_scalar(lru[:, 22:23], lru[:, 21:22], -1.0, 1.0, ALU.mult, ALU.add))
                nc.vector.tensor_scalar(lru[:, 17:18], lru[:, 22:23], 0.0, None, ALU.max).then_inc(lru_dve.sem, 1)
                nc.vector.tensor_tensor(power[:, 0, 0:1], lru[:, 7:8], lru[:, 15:16], ALU.mult)
                chain.all(nc.vector.tensor_tensor(power[:, 1, 0:1], lru[:, 7:8], lru[:, 14:15], ALU.mult))
                for s in range(1, 9):
                    re, im = power[:, 0, s - 1:s], power[:, 1, s - 1:s]
                    nc.vector.tensor_tensor(blend[:, 0, 0:1], re, re, ALU.mult)
                    nc.vector.tensor_tensor(blend[:, 1, 0:1], im, im, ALU.mult)
                    chain.all(nc.vector.scalar_tensor_tensor(power[:, 1, s:s + 1], re, 2.0, im, ALU.mult, ALU.mult))
                    chain.all(nc.vector.tensor_tensor(power[:, 0, s:s + 1], blend[:, 0, 0:1], blend[:, 1, 0:1],
                                                      ALU.subtract))
                for c in range(2):
                    nc.vector.tensor_scalar(blend[:, 0], power[:, 0], lru_sign[:, 2 * c:2 * c + 1], None, ALU.mult)
                    chain.all(nc.vector.tensor_scalar(blend[:, 1], power[:, 1], lru_sign[:, 2 * c + 1:2 * c + 2],
                                                      None, ALU.mult))
                    chain.all(nc.vector.tensor_tensor(blend[:, 2 + c], blend[:, 0], blend[:, 1], ALU.add))
                for s in range(9):
                    for c in range(2):
                        nc.vector.tensor_scalar(m.lru_step[:, s, c * STATES:(c + 1) * STATES], lru_fold[:],
                                                blend[:, 2 + c, s:s + 1], None, ALU.mult)
                low, high = (table[:].rearrange("p (j e) -> p e j", e=2)[:, e] for e in range(2))
                chain.all(nc.vector.tensor_tensor(delta[:], high, low, ALU.subtract))
                for n in range(8):
                    dve.wait_ge(idx_loaded[n % 2].sem, idx_loaded[n % 2].at(16 * (n // 2 + 1)))
                    for b in range(4):
                        chain.link(nc.vector.tensor_scalar(bits[:, b], idx[:, n % 2], 1 << b, None, ALU.bitwise_and))
                    chain.wait()
                    tree = [m.lut_w[:, n * LUT_CHUNK:(n + 1) * LUT_CHUNK]] + [leaves[:, j] for j in range(7)]
                    for j in range(LUT // 2):
                        chain.link(nc.vector.tensor_scalar(tree[j], bits[:, 0], delta[:, j:j + 1],
                                                           table[:, 2 * j:2 * j + 1], ALU.mult, ALU.add))
                    chain.wait()
                    nc.vector.copy_predicated(tree[0], bits[:, 1], tree[1]).then_inc(chunk_read.sem, 1)
                    for a in (2, 4, 6):
                        chain.link(nc.vector.copy_predicated(tree[a], bits[:, 1], tree[a + 1]))
                    chain.wait()
                    dve.wait_ge(chunk_read.sem, chunk_read.at(n + 1))
                    chain.link(nc.vector.copy_predicated(tree[0], bits[:, 2], tree[2]))
                    chain.all(nc.vector.copy_predicated(tree[4], bits[:, 2], tree[6]))
                    chain.all(nc.vector.copy_predicated(tree[0], bits[:, 3], tree[4]))
                dve_chain.close(chain.n)

        for s, n in ((loaded, 16 * len(constants)), (rows_made, 8), (rows_turned, 8), (turned_stored, 8),
                     (chunk_read, 8), (lru_act, 3), (lru_dve, 3)):
            s.close(n)
        for s in coef_loaded + idx_loaded:
            s.close(64)


def fold_turn(nc, chain, v, src, dst, tmp):
    chain.all(nc.vector.tensor_scalar(v[:, tmp:tmp + 1], v[:, src:src + 1], float(np.pi), -TWO_PI,
                                      ALU.is_gt, ALU.mult))
    chain.all(nc.vector.tensor_tensor(v[:, dst:dst + 1], v[:, src:src + 1], v[:, tmp:tmp + 1], ALU.add))
    chain.all(nc.vector.tensor_scalar(v[:, tmp:tmp + 1], v[:, dst:dst + 1], -float(np.pi), TWO_PI,
                                      ALU.is_lt, ALU.mult))
    chain.all(nc.vector.tensor_tensor(v[:, dst:dst + 1], v[:, dst:dst + 1], v[:, tmp:tmp + 1], ALU.add))


def normalise(m, b, layer):
    nc = m.nc
    stepped, rooted, normed = m.sig("ln_var"), m.sig("ln_root"), m.sig("ln_normed")
    turned, loaded = m.sig("ln_turned"), m.sig("x_loaded")
    dve_chain = m.sig("dve_chain")
    with ExitStack() as local_ctx:
        sb = m.local(local_ctx)
        extra = sb("extra", [P, NT, D])
        skip = sb("skip", [P, D])
        with nc.Block() as block:
            @block.sync
            def _(sp):
                if layer == 0:
                    sp.dma_start(m.x[:], m.dram["x"][b].rearrange("(t p) d -> p t d", p=P)).then_inc(loaded.sem, 16)
                if layer == 3:
                    sp.dma_start(skip[:], m.dram["lru_d"].broadcast_to([P, D])).then_inc(loaded.sem, 16)

            @block.vector
            def _(dve):
                chain = Chain(dve, dve_chain)
                if layer in (0, 3):
                    dve.wait_ge(loaded.sem, loaded.at(16))
                if layer:
                    for h in range(2):
                        x_pair = m.x[:, 2 * h:2 * h + 2].rearrange("p t d -> p (t d)")
                        chain.link(nc.vector.tensor_tensor(x_pair, x_pair, m.acc[:, h, :], ALU.add))
                    if layer == 2:
                        chain.wait()
                        chain.link(nc.vector.tensor_tensor(m.x[:], m.x[:], m.xn[:], ALU.add))
                    if layer == 3:
                        chain.link(nc.vector.tensor_tensor(extra[:], m.xn[:],
                                                           skip[:].unsqueeze(1).broadcast_to([P, NT, D]), ALU.mult))
                        chain.wait()
                        chain.link(nc.vector.tensor_tensor(m.x[:], m.x[:], extra[:], ALU.add))
                    chain.wait()
                for t in range(NT):
                    chain.link(nc.vector.bn_stats(m.stats[:, t], m.x[:, t]))
                chain.wait()
                for t in range(NT):
                    chain.link(nc.vector.bn_aggr(m.mv[:, t], m.stats[:, t]))
                chain.wait()
                nc.vector.tensor_scalar(m.rs[:, 0], m.mv[:, :, 1], 1e-5, None, ALU.add).then_inc(stepped.sem, 1)
                dve.wait_ge(stepped.sem, stepped.at(1))
                dve.wait_ge(rooted.sem, rooted.at(1))
                reciprocal_root(nc, chain, m.rs)
                for t in range(NT):
                    last = nc.vector.tensor_scalar(m.xn[:, t], m.x[:, t], m.mv[:, t, 0:1], m.rs[:, 3, t:t + 1],
                                                   ALU.subtract, ALU.mult)
                    last.then_inc(normed.sem, 1)
                dve_chain.close(chain.n)

            @block.scalar
            def _(act):
                act.wait_ge(stepped.sem, stepped.at(1))
                nc.scalar.activation(m.rs[:, 1], m.rs[:, 0], ACT.Sqrt).then_inc(rooted.sem, 1)
                for k in range(KD):
                    act.wait_ge(turned.sem, turned.at(k + 1))
                    nc.scalar.activation(m.xnT[:, k], m.banks[:, k, :], ACT.Copy)

            @block.tensor
            def _(pe):
                for k in range(KD):
                    for t in range(NT):
                        pe.wait_ge(normed.sem, normed.at(t + 1))
                        last = nc.tensor.transpose(m.banks[:, k, t * P:(t + 1) * P],
                                                   m.xn[:, t, k * P:(k + 1) * P], m.ident[:])
                    last.then_inc(turned.sem, 1)
        for s, n in ((stepped, 1), (rooted, 1), (normed, NT), (turned, KD)):
            s.close(n)
        if layer in (0, 3):
            loaded.close(16)


SCORE_AT = {3: (0, 0), 2: (1, 0), 1: (2, 0), 0: (2, 2 * P)}
PROB_AT = {3: 0, 2: T, 1: T + 3 * P, 0: T + 5 * P}
PROB_COLS = 10 * P


def attention(m, layer):
    nc = m.nc
    rotary = layer == 0
    qkv_dram, wo_dram = m.dram[f"qkv{layer}"], m.dram[f"wo{layer}"]
    qkv_cols, wo_cols = qkv_dram.shape[2], wo_dram.shape[2]
    qkv_loaded = [m.sig(f"qkv_loaded{i}") for i in range(2)]
    wo_loaded = [m.sig(f"wo_loaded{i}") for i in range(2)]
    qk_projected, v_projected, scored = m.sig("qk_projected"), m.sig("v_projected"), m.sig("scored")
    turned, attended, added = m.sig("turned"), m.sig("attended"), m.sig("head_added")
    qk_ready, qk_rest_ready, max_ready = m.sig("qk_ready"), m.sig("qk_rest_ready"), m.sig("max_ready")
    exp_ready, probs_ready, v_ready = m.sig("exp_ready"), m.sig("probs_ready"), m.sig("v_ready")
    probsT_ready, y_ready, dve_chain = m.sig("probsT_ready"), m.sig("y_ready"), m.sig("dve_chain")
    rope_loaded = m.sig("rope_loaded")
    CHAIN_QK = 3 if rotary else 0
    CHAIN_SOFTMAX = 5

    with ExitStack() as local_ctx:
        sb = m.local(local_ctx)
        qkv = [sb(f"qkv{i}", [P, qkv_cols]) for i in range(2)]
        wo = [sb(f"wo{i}", [P, wo_cols]) for i in range(2)]
        qkT = sb("qkT", [P, 2, T])
        v = [sb(f"v{i}", [P, NT, HD]) for i in range(2)]
        rot = sb("rot", [64, 2, 2, T])
        rope_cos, rope_sin = sb("rope_cos", [64, T]), sb("rope_sin", [64, T])
        probs = sb("probs", [P, PROB_COLS])
        probsT = sb("probsT", [P, PROB_COLS])
        yT = sb("yT", [P, T])
        row_max, neg_max = sb("row_max", [P, NT]), sb("neg_max", [P, NT])
        row_sum, row_inv = sb("row_sum", [P, NT]), sb("row_inv", [P, NT])
        qk_psum, v_psum = m.banks[:, 3:5, :], m.banks[:, 5, :]

        def score_tile(i):
            b, at = SCORE_AT[i]
            return m.banks[:, b, at:at + (i + 1) * P]

        def prob_tile(i):
            return probs[:, PROB_AT[i]:PROB_AT[i] + (i + 1) * P]

        def turned_tile(k):
            return probsT[:, PROB_AT[3 - k]:PROB_AT[3 - k] + (NT - k) * P]

        with nc.Block() as block:
            @block.sync
            def _(sp):
                def load_qkv(h, par):
                    sp.dma_start(qkv[par][:], head_rows(qkv_dram, h)).then_inc(qkv_loaded[par].sem, 16)

                def load_wo(h, par):
                    sp.dma_start(wo[par][:], head_rows(wo_dram, h)).then_inc(wo_loaded[par].sem, 16)

                load_qkv(0, 0)
                if rotary:
                    sp.dma_start(rope_cos[:], m.dram["rope_cos"]).then_inc(rope_loaded.sem, 16)
                    sp.dma_start(rope_sin[:], m.dram["rope_sin"]).then_inc(rope_loaded.sem, 16)
                load_qkv(1, 1)
                load_wo(0, 0)
                load_wo(1, 1)
                with sp.Fori(0, HEADS // 2 - 1) as i:
                    for par in range(2):
                        h = 2 * i + par
                        sp.wait_ge(v_projected.sem, v_projected.at(h + 1))
                        if not rotary:
                            sp.wait_ge(qk_ready.sem, qk_ready.at(h + 1))
                        load_qkv(h + 2, par)
                        sp.wait_ge(added.sem, added.at(h + 1))
                        load_wo(h + 2, par)

            @block.tensor
            def _(pe):
                def project_qk(par):
                    for which in range(2):
                        for k in range(KD):
                            at = (which * KD + k) * HD
                            last = nc.tensor.matmul(qk_psum[:, which], qkv[par][:, at:at + HD], m.xnT[:, k],
                                                    start=k == 0, stop=k == KD - 1)
                    last.then_inc(qk_projected.sem, 1)

                def project_v(par):
                    for t in range(NT):
                        for k in range(KD):
                            at = (2 * KD + k) * HD
                            last = nc.tensor.matmul(v_psum[:, t * P:(t + 1) * P], m.xnT[:, k, t * P:(t + 1) * P],
                                                    qkv[par][:, at:at + HD], start=k == 0, stop=k == KD - 1)
                    last.then_inc(v_projected.sem, 1)

                def project(h, par, use):
                    pe.wait_ge(qkv_loaded[par].sem, qkv_loaded[par].at(use))
                    project_qk(par)

                def score():
                    for i in (3, 2, 1, 0):
                        out = score_tile(i)
                        nc.tensor.matmul(out, qkT[:, 0, i * P:(i + 1) * P], qkT[:, 1, 0:(i + 1) * P],
                                         start=True, stop=False)
                        last = nc.tensor.matmul(out[:, i * P:(i + 1) * P], m.ident_bf[:], m.mask_bf[:],
                                                start=False, stop=True)
                        if i != 1:
                            last.then_inc(scored.sem, 1)

                def turn():
                    for k in range(NT):
                        out = score_tile(3 - k)
                        for i in range(k, NT):
                            last = nc.tensor.transpose(out[:, (i - k) * P:(i - k + 1) * P],
                                                       prob_tile(i)[:, k * P:(k + 1) * P], m.ident[:])
                        if k != 2:
                            last.then_inc(turned.sem, 1)

                def add_head(par):
                    for t in range(NT):
                        last = nc.tensor.matmul(m.acc_tile(t), yT[:, t * P:(t + 1) * P], wo[par][:, 0:D],
                                                start=False, stop=False, skip_group_check=True)
                    last.then_inc(added.sem, 1)

                def attend(par):
                    for k in range(NT):
                        last = nc.tensor.matmul(v_psum[:, k * P:T], v[par][:, k], turned_tile(k),
                                                start=k == 0, stop=k == NT - 1)
                    last.then_inc(attended.sem, 1)

                def step(h, par, pair, first=False, final=False):
                    pe.wait_ge(qk_ready.sem, qk_ready.at(h + 1))
                    if rotary:
                        pe.wait_ge(qk_rest_ready.sem, qk_rest_ready.at(h + 1))
                    if not first:
                        pe.wait_ge(probsT_ready.sem, probsT_ready.at(3 * h))
                    score()
                    if not final:
                        project(h + 1, 1 - par, 16 * (pair + (1 if par == 0 else 2)))
                        if first:
                            pe.wait_ge(v_ready.sem, v_ready.at(1))
                        else:
                            pe.wait_ge(y_ready.sem, y_ready.at(h))
                        project_v(1 - par)
                    pe.wait_ge(probs_ready.sem, probs_ready.at(h + 1))
                    turn()
                    if not first:
                        if final:
                            pe.wait_ge(y_ready.sem, y_ready.at(h))
                        pe.wait_ge(wo_loaded[1 - par].sem, wo_loaded[1 - par].at(16 * (pair + (1 if par else 0))))
                        add_head(1 - par)
                    pe.wait_ge(v_ready.sem, v_ready.at(h + (1 if final else 2)))
                    pe.wait_ge(probsT_ready.sem, probsT_ready.at(3 * h + 3))
                    attend(par)

                seed = m.bo_row[:].rearrange("o a d -> o (a d)") if not rotary else m.zero_row[:]
                for h in range(2):
                    nc.tensor.matmul(m.acc[:, h, :], m.one_row[:], seed, start=True, stop=False,
                                     skip_group_check=True)
                project(0, 0, 16)
                project_v(0)
                step(0, 0, 0, first=True)
                with pe.Fori(0, HEADS // 2 - 1) as i:
                    step(2 * i + 1, 1, i)
                    step(2 * i + 2, 0, i + 1)
                step(HEADS - 1, 1, HEADS // 2 - 1, final=True)
                pe.wait_ge(y_ready.sem, y_ready.at(HEADS))
                pe.wait_ge(wo_loaded[1].sem, wo_loaded[1].at(16 * HEADS // 2))
                add_head(1)

            @block.vector
            def _(dve):
                def spread_qk(h, par, at):
                    dve.wait_ge(qk_projected.sem, qk_projected.at(h + 1))
                    if not rotary:
                        for which in range(2):
                            last = nc.vector.tensor_scalar(qkT[:, which], qk_psum[:, which],
                                                           qkv[par][:, 6 * HD + which:6 * HD + which + 1], None,
                                                           ALU.add)
                        last.then_inc(qk_ready.sem, 1)
                        return
                    chain = Chain(dve, dve_chain, at)
                    sin = lambda a: rope_sin[a:a + 32].unsqueeze(1).broadcast_to([32, 2, T])
                    chain.link(nc.vector.tensor_tensor(rot[0:32, 0], qk_psum[32:64], sin(32), ALU.mult))
                    chain.link(nc.vector.tensor_tensor(rot[32:64, 0], qk_psum[0:32], sin(0), ALU.mult))
                    cos = rope_cos[:].unsqueeze(1).broadcast_to([64, 2, T])
                    chain.link(nc.vector.tensor_tensor(rot[:, 1], qk_psum[0:64], cos, ALU.mult))
                    chain.wait()
                    nc.vector.tensor_tensor(qkT[0:64], rot[:, 0], rot[:, 1], ALU.add).then_inc(qk_ready.sem, 1)

                def softmax(h, at):
                    chain = Chain(dve, dve_chain, at)
                    for n, i in enumerate((3, 2, 1, 0)):
                        if n < 3:
                            dve.wait_ge(scored.sem, scored.at(3 * h + n + 1))
                        chain.link(nc.vector.reduce_max(row_max[:, i:i + 1], score_tile(i), AXIS.X))
                    chain.wait()
                    nc.vector.tensor_scalar(neg_max[:], row_max[:], -QK_SCALE, None, ALU.mult)\
                      .then_inc(max_ready.sem, 1)
                    dve.wait_ge(exp_ready.sem, exp_ready.at(h + 1))
                    chain.all(nc.vector.reciprocal(row_inv[:], row_sum[:]))
                    for i in (3, 2, 1, 0):
                        last = nc.vector.tensor_scalar(prob_tile(i), prob_tile(i), row_inv[:, i:i + 1], None,
                                                       ALU.mult)
                    last.then_inc(probs_ready.sem, 1)

                per = CHAIN_QK + CHAIN_SOFTMAX
                if rotary:
                    dve.wait_ge(rope_loaded.sem, rope_loaded.at(32))
                spread_qk(0, 0, 0)
                with dve.Fori(0, HEADS // 2 - 1) as i:
                    for par in range(2):
                        h = 2 * i + par
                        at = CHAIN_QK + per * h
                        softmax(h, at)
                        spread_qk(h + 1, 1 - par, at + CHAIN_SOFTMAX)
                softmax(HEADS - 2, CHAIN_QK + per * (HEADS - 2))
                spread_qk(HEADS - 1, 1, CHAIN_QK + per * (HEADS - 2) + CHAIN_SOFTMAX)
                softmax(HEADS - 1, CHAIN_QK + per * (HEADS - 1))

            @block.scalar
            def _(act):
                def spread_rest(h, par):
                    if rotary:
                        act.wait_ge(qk_projected.sem, qk_projected.at(h + 1))
                        nc.scalar.activation(qkT[64:P], qk_psum[64:P], ACT.Copy).then_inc(qk_rest_ready.sem, 1)
                    act.wait_ge(v_projected.sem, v_projected.at(h + 1))
                    nc.scalar.activation(v[par][:].rearrange("p t c -> p (t c)"), v_psum, ACT.Copy)\
                      .then_inc(v_ready.sem, 1)

                def exponentials(h):
                    act.wait_ge(max_ready.sem, max_ready.at(h + 1))
                    for i in (3, 2, 1, 0):
                        last = nc.scalar.activation(prob_tile(i), score_tile(i), ACT.Exp, bias=neg_max[:, i:i + 1],
                                                    scale=QK_SCALE, accum_out=row_sum[:, i:i + 1])
                    last.then_inc(exp_ready.sem, 1)

                def store_turned(h):
                    for k, (at, cols) in enumerate(((0, 4 * P), (T, 3 * P), (T + 3 * P, 3 * P))):
                        act.wait_ge(turned.sem, turned.at(3 * h + k + 1))
                        nc.scalar.activation(probsT[:, at:at + cols], m.banks[:, k, 0:cols], ACT.Copy)\
                          .then_inc(probsT_ready.sem, 1)

                def store_y(h, par, use):
                    if not rotary:
                        act.wait_ge(wo_loaded[par].sem, wo_loaded[par].at(16 * use))
                    act.wait_ge(attended.sem, attended.at(h + 1))
                    if rotary:
                        nc.scalar.activation(yT[:], v_psum, ACT.Copy, scale=1.0 / 3.0).then_inc(y_ready.sem, 1)
                    else:
                        nc.scalar.activation(yT[:], v_psum, ACT.Identity, bias=wo[par][:, D:D + 1])\
                          .then_inc(y_ready.sem, 1)

                spread_rest(0, 0)
                with act.Fori(0, HEADS // 2 - 1) as i:
                    for par in range(2):
                        h = 2 * i + par
                        exponentials(h)
                        spread_rest(h + 1, 1 - par)
                        store_turned(h)
                        store_y(h, par, i + 1)
                exponentials(HEADS - 2)
                spread_rest(HEADS - 1, 1)
                store_turned(HEADS - 2)
                store_y(HEADS - 2, 0, HEADS // 2)
                exponentials(HEADS - 1)
                store_turned(HEADS - 1)
                store_y(HEADS - 1, 1, HEADS // 2)

        for s, n in ((qk_projected, HEADS), (v_projected, HEADS), (scored, 3 * HEADS), (turned, 3 * HEADS),
                     (attended, HEADS), (added, HEADS), (qk_ready, HEADS), (max_ready, HEADS), (exp_ready, HEADS),
                     (probs_ready, HEADS), (v_ready, HEADS), (probsT_ready, 3 * HEADS), (y_ready, HEADS),
                     (dve_chain, HEADS * (CHAIN_QK + CHAIN_SOFTMAX))):
            s.close(n)
        if rotary:
            qk_rest_ready.close(HEADS)
            rope_loaded.close(32)
        for s in qkv_loaded + wo_loaded:
            s.close(16 * HEADS // 2)


def head_rows(dram, h):
    return dram[bass.ds(h, 1)].rearrange("a p f -> (a p) f")


class Hidden:

    def __init__(self, groups, cols, rows, experts, act):
        self.groups, self.cols, self.rows, self.experts, self.act = groups, cols, rows, experts, act
        self.one_bank = 2 * cols <= 512


def gated_mlp_engines(m, shape, sb, first_bank, gate_up, down, scale_of, waits):
    nc = m.nc
    gate_done, gated, hidden_ready = m.sig("gate_up_done"), m.sig("gated"), m.sig("hidden_ready")
    hidden_turned, hiddenT_ready, added = m.sig("hidden_turned"), m.sig("hiddenT_ready"), m.sig("group_added")
    F, R = shape.cols, len(shape.rows)
    act_out = [sb(f"act_out{i}", [P, F]) for i in range(2)]
    hidden = [sb(f"hidden{i}", [P, F]) for i in range(2)]
    hiddenT = [sb(f"hiddenT{i}", [P, R, P]) for i in range(2)]
    per_item = 1 if shape.one_bank else 2
    m.last_mlp = act_out, hidden

    def gate_up_psum(par):
        if shape.one_bank:
            b = m.banks[:, first_bank + par, :]
            return b[:, 0:F], b[:, F:2 * F], b[:, 0:2 * F].rearrange("p (w f) -> p w f", w=2)
        b = first_bank + 2 * par
        return m.banks[:, b, 0:F], m.banks[:, b + 1, 0:F], None

    def turned_psum(par):
        return m.banks[:, first_bank + 2 * per_item + par, 0:R * P].rearrange("p (r c) -> p r c", r=R)

    def multiply(t, par, gpar):
        gate, up, both = gate_up_psum(par)
        if both is not None:
            for k in range(KD):
                last = nc.tensor.matmul(both, m.xnT[:, k, t * P:(t + 1) * P], gate_up(gpar, k),
                                        start=k == 0, stop=k == KD - 1)
        else:
            for w, out in enumerate((gate, up)):
                for k in range(KD):
                    last = nc.tensor.matmul(out, m.xnT[:, k, t * P:(t + 1) * P], gate_up(gpar, k)[:, w],
                                            start=k == 0, stop=k == KD - 1)
        last.then_inc(gate_done.sem, 1)

    def turn(pe, n, par):
        pe.wait_ge(hidden_ready.sem, hidden_ready.at(n + 1))
        for r, rows in enumerate(shape.rows):
            last = nc.tensor.transpose(turned_psum(par)[0:rows, r], hidden[par][:, r * P:r * P + rows], m.ident[:])
        last.then_inc(hidden_turned.sem, 1)

    def add(pe, n, t, par, gpar):
        pe.wait_ge(hiddenT_ready.sem, hiddenT_ready.at(n + 1))
        for r, rows in enumerate(shape.rows):
            last = nc.tensor.matmul(m.acc_tile(t), hiddenT[par][0:rows, r], down(gpar, r)[0:rows],
                                    start=False, stop=False, skip_group_check=True)
        last.then_inc(added.sem, 1)

    def activate(act, n, par):
        act.wait_ge(gate_done.sem, gate_done.at(n + 1))
        nc.scalar.activation(act_out[par][:], gate_up_psum(par)[0], shape.act).then_inc(gated.sem, 1)

    def store_turned(act, n, par):
        act.wait_ge(hidden_turned.sem, hidden_turned.at(n + 1))
        whole = sum(r == P for r in shape.rows)
        last = nc.scalar.activation(hiddenT[par][:, 0:whole], turned_psum(par)[:, 0:whole], ACT.Copy)
        if whole < R:
            rows = shape.rows[-1]
            last = nc.scalar.activation(hiddenT[par][0:rows, whole], turned_psum(par)[0:rows, whole], ACT.Copy)
        last.then_inc(hiddenT_ready.sem, 1)

    def gate(dve, n, g, t, par):
        dve.wait_ge(gated.sem, gated.at(n + 1))
        up = gate_up_psum(par)[1]
        if scale_of is None:
            last = nc.vector.tensor_tensor(hidden[par][:], act_out[par][:], up, ALU.mult)
        else:
            cols = F // shape.experts
            for e in range(shape.experts):
                at = slice(e * cols, (e + 1) * cols)
                last = nc.vector.scalar_tensor_tensor(hidden[par][:, at], up[:, at], scale_of(g, t, e),
                                                      act_out[par][:, at], ALU.mult, ALU.mult)
        last.then_inc(hidden_ready.sem, 1)

    def close():
        n = NT * shape.groups
        for s in (gate_done, gated, hidden_ready, hidden_turned, hiddenT_ready, added):
            s.close(n)

    return multiply, turn, add, activate, store_turned, gate, close, gate_done, added


def mixture(m, layer):
    nc = m.nc
    E, TOP = (E0, TOP0) if layer == 0 else (E3, TOP3)
    shape = Hidden(GROUPS, F0, (P, P, P), 4, ACT.Silu) if layer == 0 else Hidden(GROUPS, F3, (P, P), 1, ACT.Gelu)
    F, R = shape.cols, len(shape.rows)
    gu_dram, down_dram, router_dram = m.dram[f"gate_up{layer}"], m.dram[f"down{layer}"], m.dram[f"router{layer}"]
    gu_loaded = [m.sig(f"gu_loaded{i}") for i in range(2)]
    down_loaded = [m.sig(f"down_loaded{i}") for i in range(2)]
    loaded, routed, logits_in, exp_in = m.sig("router_loaded"), m.sig("routed"), m.sig("logits_in"), m.sig("route_exp")
    stepped, rooted = m.sig("ln_var"), m.sig("ln_root")
    scaled_router, square_step = m.sig("scaled_router"), m.sig("square_step")
    dve_chain = m.sig("dve_chain")
    ITEMS = NT * GROUPS
    UNROLL = 2 * NT
    EP = E + 8 - TOP

    with ExitStack() as local_ctx:
        sb = m.local(local_ctx)
        gu = [sb(f"gu{i}", [P, KD, 2, F]) for i in range(2)]
        dn = [sb(f"dn{i}", [P, R, D]) for i in range(2)]
        router = sb("router", [P, KD, E])
        router_scale = sb("router_scale", [P, KD])
        per_expert = sb("per_expert", [P, E])
        logits, replaced = sb("logits", [P, NT, EP]), sb("replaced", [P, NT, EP])
        top = sb("top", [P, NT, 8])
        chosen, expd = sb("chosen", [P, NT, E]), sb("expd", [P, NT, E])
        weight = sb("weight", [P, NT, E])
        sums = sb("sums", [P, 4, NT])
        squares, square_sum = sb("squares", [P, D]), sb("square_sum", [P, NT])
        scale_of = lambda g, t, e: weight[:, t, bass.ds(g * shape.experts + e, 1)]
        multiply, turn, add, activate, store_turned, gate, close, gate_done, added = gated_mlp_engines(
            m, shape, sb, 0, lambda gpar, k: gu[gpar][:, k], lambda gpar, r: dn[gpar][:, r], scale_of, None)
        per_token = lambda a: a.unsqueeze(2).broadcast_to([P, NT, E])
        n_loads = 1 if layer == 0 else 3

        with nc.Block() as block:
            @block.sync
            def _(sp):
                def load_gu(g, gpar):
                    sp.dma_start(gu[gpar][:].rearrange("p k w f -> p (k w f)"), head_rows(gu_dram, g))\
                      .then_inc(gu_loaded[gpar].sem, 16)

                def load_down(g, gpar):
                    sp.dma_start(dn[gpar][:].rearrange("p r d -> p (r d)"), head_rows(down_dram, g))\
                      .then_inc(down_loaded[gpar].sem, 16)

                sp.dma_start(router[:], router_dram).then_inc(loaded.sem, 16)
                if layer == 3:
                    sp.dma_start(router_scale[:], m.dram["router_scale"]).then_inc(loaded.sem, 16)
                    sp.dma_start(per_expert[:], m.dram["per_expert"].broadcast_to([P, E])).then_inc(loaded.sem, 16)
                for g in range(2):
                    load_gu(g, g)
                    load_down(g, g)
                with sp.Fori(0, GROUPS // 2 - 1) as i:
                    for gpar in range(2):
                        g = 2 * i + gpar
                        sp.wait_ge(gate_done.sem, gate_done.at(NT * g + NT))
                        load_gu(g + 2, gpar)
                        sp.wait_ge(added.sem, added.at(NT * g + NT))
                        load_down(g + 2, gpar)

            @block.tensor
            def _(pe):
                if layer == 0:
                    pe.wait_ge(loaded.sem, loaded.at(16))
                else:
                    pe.wait_ge(scaled_router.sem, scaled_router.at(1))
                for t in range(NT):
                    for k in range(KD):
                        last = nc.tensor.matmul(m.banks[:, 5, t * E:(t + 1) * E], m.xnT[:, k, t * P:(t + 1) * P],
                                                router[:, k], start=k == 0, stop=k == KD - 1)
                last.then_inc(routed.sem, 1)

                def step(n, c, pair):
                    if c < UNROLL:
                        gpar, t, nxt = c // NT, c % NT, (c + 1) % UNROLL
                    if n is not None and not (isinstance(n, int) and n == ITEMS - 1):
                        if nxt % NT == 0:
                            use = pair + (2 if nxt == 0 else 1)
                            pe.wait_ge(gu_loaded[nxt // NT].sem, gu_loaded[nxt // NT].at(16 * use))
                        multiply(nxt % NT, nxt % 2, nxt // NT)
                    turn(pe, n, c % 2)
                    if not (isinstance(n, int) and n == 0):
                        prev = (c - 1) % UNROLL
                        if prev % NT == 0:
                            use = pair + (1 if c else 0)
                            pe.wait_ge(down_loaded[prev // NT].sem, down_loaded[prev // NT].at(16 * use))
                        add(pe, n - 1, prev % NT, prev % 2, prev // NT)

                pe.wait_ge(gu_loaded[0].sem, gu_loaded[0].at(16))
                multiply(0, 0, 0)
                step(0, 0, 0)
                with pe.Fori(0, GROUPS // 2 - 1) as i:
                    for c in range(1, UNROLL + 1):
                        step(UNROLL * i + c, c % UNROLL, i + c // UNROLL)
                for n in range(ITEMS - UNROLL + 1, ITEMS):
                    step(n, n % UNROLL, n // UNROLL)
                add(pe, ITEMS - 1, NT - 1, 1, 1)

            @block.vector
            def _(dve):
                chain = Chain(dve, dve_chain)
                chain.link(nc.vector.memset(logits[:, :, E:], -3e38))
                dve.wait_ge(loaded.sem, loaded.at(16 * n_loads))
                if layer == 3:
                    for k in range(KD):
                        last = nc.vector.tensor_scalar(router[:, k], router[:, k], router_scale[:, k:k + 1],
                                                       float(D) ** -0.5, ALU.mult, ALU.mult)
                    last.then_inc(scaled_router.sem, 1)
                    dve.wait_ge(square_step.sem, square_step.at(NT))
                    nc.vector.tensor_scalar(m.rs[:, 0], square_sum[:], 1.0 / D, 1e-6, ALU.mult, ALU.add)\
                      .then_inc(stepped.sem, 1)
                    dve.wait_ge(stepped.sem, stepped.at(1))
                    dve.wait_ge(rooted.sem, rooted.at(1))
                    reciprocal_root(nc, chain, m.rs)
                dve.wait_ge(routed.sem, routed.at(1))
                src = m.banks[:, 5, 0:NT * E].rearrange("p (t e) -> p t e", t=NT)
                if layer == 0:
                    chain.all(nc.vector.tensor_copy(logits[:, :, 0:E], src))
                else:
                    chain.all(nc.vector.tensor_tensor(logits[:, :, 0:E], src, per_token(m.rs[:, 3]), ALU.mult))
                for t in range(NT):
                    chain.link(nc.vector.max(top[:, t], logits[:, t]))
                chain.wait()
                chain.link(nc.vector.tensor_tensor(expd[:], logits[:, :, 0:E],
                                                   top[:, :, 0:1].broadcast_to([P, NT, E]), ALU.subtract))
                chain.wait()
                chain.all(nc.vector.memset(top[:, :, TOP:], -3e38))
                for t in range(NT):
                    chain.link(nc.vector.match_replace(replaced[:, t], top[:, t], logits[:, t], 3e38))
                chain.wait()
                nc.vector.tensor_tensor(chosen[:], replaced[:, :, 0:E], logits[:, :, 0:E], ALU.not_equal)\
                  .then_inc(logits_in.sem, 1)
                dve.wait_ge(exp_in.sem, exp_in.at(1))
                dve.wait_ge(logits_in.sem, logits_in.at(1))
                if layer == 3:
                    chain.all(nc.vector.reduce_sum(sums[:, 0], expd[:], AXIS.X))
                    chain.all(nc.vector.reciprocal(sums[:, 1], sums[:, 0]))
                    chain.all(nc.vector.tensor_tensor(expd[:], expd[:], per_token(sums[:, 1]), ALU.mult))
                chain.all(nc.vector.tensor_tensor(chosen[:], chosen[:], expd[:], ALU.mult))
                chain.all(nc.vector.reduce_sum(sums[:, 0], chosen[:], AXIS.X))
                if layer == 3:
                    chain.all(nc.vector.tensor_scalar(sums[:, 0], sums[:, 0], 1e-12, None, ALU.max))
                chain.all(nc.vector.reciprocal(sums[:, 1], sums[:, 0]))
                chain.all(nc.vector.tensor_tensor(weight[:], chosen[:], per_token(sums[:, 1]), ALU.mult))
                if layer == 3:
                    chain.all(nc.vector.tensor_tensor(weight[:], weight[:],
                                                      per_expert[:].unsqueeze(1).broadcast_to([P, NT, E]), ALU.mult))
                with dve.Fori(0, GROUPS // 2) as i:
                    for c in range(UNROLL):
                        gate(dve, UNROLL * i + c, 2 * i + c // NT, c % NT, c % 2)
                dve_chain.close(chain.n)

            @block.scalar
            def _(act):
                if layer == 3:
                    for t in range(NT):
                        last = nc.scalar.activation(squares[:], m.xn[:, t], ACT.Square,
                                                    accum_out=square_sum[:, t:t + 1])
                        last.then_inc(square_step.sem, 1)
                        act.wait_ge(square_step.sem, square_step.at(t + 1))
                    act.wait_ge(stepped.sem, stepped.at(1))
                    nc.scalar.activation(m.rs[:, 1], m.rs[:, 0], ACT.Sqrt).then_inc(rooted.sem, 1)
                act.wait_ge(logits_in.sem, logits_in.at(1))
                nc.scalar.activation(expd[:], expd[:], ACT.Exp).then_inc(exp_in.sem, 1)

                activate(act, 0, 0)
                with act.Fori(0, GROUPS // 2 - 1) as i:
                    for c in range(UNROLL):
                        activate(act, UNROLL * i + c + 1, (c + 1) % 2)
                        store_turned(act, UNROLL * i + c, c % 2)
                for n in range(ITEMS - UNROLL, ITEMS):
                    if n + 1 < ITEMS:
                        activate(act, n + 1, (n + 1) % 2)
                    store_turned(act, n, n % 2)

        close()
        loaded.close(16 * n_loads)
        for s in (routed, logits_in, exp_in):
            s.close(1)
        if layer == 3:
            stepped.close(1)
            rooted.close(1)
            scaled_router.close(1)
            square_step.close(NT)
        for s in gu_loaded + down_loaded:
            s.close(16 * GROUPS // 2)


def state_space(m):
    nc, dram = m.nc, m.dram
    loaded, in_weights = m.sig("ss_loaded"), m.sig("ss_in_loaded")
    square_step, stepped, rooted = m.sig("square_step"), m.sig("ln_var"), m.sig("ln_root")
    scaled, turned, xmT_ready = m.sig("ln_normed"), m.sig("ln_turned"), m.sig("xmT_ready")
    projected, xs_ready, z_ready = m.sig("ss_projected"), m.sig("xs_ready"), m.sig("z_ready")
    conv_ready, u_ready = m.sig("conv_ready"), m.sig("u_ready")
    low_rank, dt_in, bc_split = m.sig("low_rank"), m.sig("dt_in"), m.sig("bc_split")
    spread, b_stored, c_stored = m.sig("bc_spread"), m.sig("b_stored"), m.sig("c_stored")
    dt_done, dt_parts = m.sig("dt_done"), m.sig("dt_parts")
    softplus_step, delta_ready = m.sig("softplus_step"), m.sig("delta_ready")
    decay_ready, scanned, product_ready, summed = (m.sig("decay_ready"), m.sig("scanned"), m.sig("product_ready"),
                                                   m.sig("summed"))
    y_taken, gated_y, joined = m.sig("y_taken"), m.sig("gated_y"), m.sig("joined")
    dve_chain = m.sig("dve_chain")
    shape = Hidden(KC, D, (P, P), 1, ACT.Tanh)
    CHAIN_TILE = NS + NT

    with ExitStack() as local_ctx:
        sb = m.local(local_ctx)
        xp = sb("xp", [P, KC, T + TAPS - 1])
        u, silu_z, delta = sb("u", [P, KC, T]), sb("silu_z", [P, KC, T]), sb("delta", [P, KC, T])
        Bs, Cs = sb("Bs", [P, NS, T]), sb("Cs", [P, NS, T])
        decay, inflow = sb("decay", [P, 2, T]), sb("inflow", [P, 2, T])
        state, product = sb("state", [P, 2, T]), sb("product", [P, 2, T])
        yg = sb("yg", [P, T])
        w_xp, w_dt, w_out = sb("w_xp", [P, KC, RANK + 2 * NS]), sb("w_dt", [P, CH]), sb("w_out", [P, KC, D])
        select = sb("select", [3 * 2 * NS, 2 * NS, P], BF16)
        split = sb("split", [3 * 2 * NS, T], BF16)
        mid = sb("mid", [2 * NS, T], BF16)
        rank_in = sb("rank_in", [P, T])
        rest = sb("rest", [2 * NS, T])
        vec = sb("vec", [P, KC, 7])
        w_norm, A = sb("w_norm", [P, KD]), sb("A", [P, KC, NS])
        squares, square_sum = sb("squares", [P, D]), sb("square_sum", [P, NT])
        blended = [sb(f"blended{i}", [P, D]) for i in range(2)]
        xm = decay[:].rearrange("p a t -> p (a t)").rearrange("p (t d) -> p t d", t=NT)
        xmT = inflow
        w_in = Cs[:, NS - 4:].rearrange("p a t -> p (a t)").rearrange("p (k c) -> p k c", k=KD)
        du = xp[:, :, 0:T]
        multiply, turn, add, activate, store_turned, _, close, gate_done, _ = gated_mlp_engines(
            m, shape, sb, 0, lambda g, k: m.spline_gu[:, k, :, bass.ds(g * D, D)],
            lambda g, r: m.spline_down[:, bass.ds(2 * g + r, 1), :].rearrange("p a d -> p (a d)"), None, None)
        gated, hidden_ready = m.sig("gated"), m.sig("hidden_ready")
        act_out, hidden = m.last_mlp
        y_psum = m.banks[:, 4, :]
        loads = [(w_xp[:], dram["w_xp"]), (w_dt[:], dram["w_dt"]), (w_out[:], dram["w_out"]),
                 (select[:], dram["select"]), (vec[:], dram["ss_vec"]), (w_norm[:], dram["w_norm"]),
                 (A[:], dram["a_log"])]

        with nc.Block() as block:
            @block.sync
            def _(sp):
                sp.dma_start(w_in, dram["w_in"]).then_inc(in_weights.sem, 16)
                for dst, src in loads:
                    sp.dma_start(dst, src).then_inc(loaded.sem, 16)

            @block.tensor
            def _(pe):
                for k in range(KD):
                    for t in range(NT):
                        pe.wait_ge(scaled.sem, scaled.at(t + 1))
                        last = nc.tensor.transpose(m.banks[:, k, t * P:(t + 1) * P], xm[:, t, k * P:(k + 1) * P],
                                                   m.ident[:])
                    last.then_inc(turned.sem, 1)
                pe.wait_ge(in_weights.sem, in_weights.at(16))
                pe.wait_ge(xmT_ready.sem, xmT_ready.at(KD))
                for c in range(2 * KC):
                    if c >= 2:
                        if c - 2 < KC:
                            pe.wait_ge(xs_ready.sem, xs_ready.at(c - 1))
                        else:
                            pe.wait_ge(z_ready.sem, z_ready.at(c - 1 - KC))
                    for k in range(KD):
                        last = nc.tensor.matmul(m.banks[:, 4 + c % 2, :], w_in[:, k, c * P:(c + 1) * P], xmT[:, k],
                                                start=k == 0, stop=k == KD - 1)
                    last.then_inc(projected.sem, 1)
                pe.wait_ge(loaded.sem, loaded.at(16 * len(loads)))
                for k in range(KC):
                    pe.wait_ge(u_ready.sem, u_ready.at(k + 1))
                    nc.tensor.matmul(m.banks[:, 0, :], w_xp[:, k, 0:RANK], u[:, k], start=k == 0, stop=k == KC - 1)
                    last = nc.tensor.matmul(m.banks[0:2 * NS, 1, :], w_xp[:, k, RANK:], u[:, k],
                                            start=k == 0, stop=k == KC - 1)
                last.then_inc(low_rank.sem, 1)
                pe.wait_ge(dt_in.sem, dt_in.at(1))
                pe.wait_ge(z_ready.sem, z_ready.at(KC))
                for c in range(KC):
                    if c >= 2:
                        pe.wait_ge(dt_parts.sem, dt_parts.at(c - 1))
                    nc.tensor.matmul(m.banks[:, 4 + c % 2, :], w_dt[:, c * P:(c + 1) * P], rank_in[:],
                                     start=True, stop=True).then_inc(dt_done.sem, 1)
                pe.wait_ge(bc_split.sem, bc_split.at(1))
                for n in range(NS):
                    for which, stored in ((0, b_stored), (1, c_stored)):
                        if n >= 2:
                            pe.wait_ge(stored.sem, stored.at(n - 1))
                        nc.tensor.matmul(m.banks[:, 2 * which + n % 2, :], select[:, which * NS + n, :], split[:],
                                         start=True, stop=True).then_inc(spread.sem, 1)
                pe.wait_ge(b_stored.sem, b_stored.at(NS))
                pe.wait_ge(c_stored.sem, c_stored.at(NS))
                pe.wait_ge(dt_parts.sem, dt_parts.at(KC))
                pe.sem_inc(summed.sem, 2)
                with pe.Fori(0, KC) as c:
                    pe.wait_ge(y_taken.sem, y_taken.at(c + 1))
                    for n in range(NS):
                        pe.wait_ge(product_ready.sem, product_ready.at(NS * c + n + 1))
                        nc.tensor.matmul(y_psum, m.ident[:], product[:, n % 2], start=n == 0, stop=n == NS - 1)\
                          .then_inc(summed.sem, 1)
                        item = NT * c
                        if n in (0, 2, 6, 10):
                            t = (0, 2, 6, 10).index(n)
                            multiply(t, t % 2, c)
                        if n in (3, 7, 11, 13):
                            t = (3, 7, 11, 13).index(n)
                            turn(pe, item + t, t % 2)
                        if n in (5, 9, 12, 14):
                            t = (5, 9, 12, 14).index(n)
                            add(pe, item + t, t, t % 2, c)
                    pe.wait_ge(gated_y.sem, gated_y.at(c + 1))
                    for t in range(NT):
                        last = nc.tensor.matmul(m.acc_tile(t), yg[:, t * P:(t + 1) * P],
                                                w_out[:, bass.ds(c, 1), :].rearrange("p a d -> p (a d)"),
                                                start=False, stop=False, skip_group_check=True)
                    last.then_inc(joined.sem, 1)

            @block.scalar
            def _(act):
                for t in range(NT):
                    nc.scalar.activation(squares[:], m.xn[:, t], ACT.Square, accum_out=square_sum[:, t:t + 1])\
                      .then_inc(square_step.sem, 1)
                    act.wait_ge(square_step.sem, square_step.at(t + 1))
                act.wait_ge(stepped.sem, stepped.at(1))
                nc.scalar.activation(m.rs[:, 1], m.rs[:, 0], ACT.Sqrt).then_inc(rooted.sem, 1)
                act.wait_ge(loaded.sem, loaded.at(16 * len(loads)))
                for k in range(KD):
                    act.wait_ge(turned.sem, turned.at(k + 1))
                    nc.scalar.activation(xmT[:, k], m.banks[:, k, :], ACT.Copy, scale=w_norm[:, k:k + 1])\
                      .then_inc(xmT_ready.sem, 1)
                for c in range(KC):
                    act.wait_ge(projected.sem, projected.at(c + 1))
                    nc.scalar.activation(xp[:, c, TAPS - 1:], m.banks[:, 4 + c % 2, :], ACT.Copy)\
                      .then_inc(xs_ready.sem, 1)
                for c in range(KC):
                    act.wait_ge(projected.sem, projected.at(KC + c + 1))
                    nc.scalar.activation(silu_z[:, c], m.banks[:, 4 + c % 2, :], ACT.Silu).then_inc(z_ready.sem, 1)
                for c in range(KC):
                    act.wait_ge(conv_ready.sem, conv_ready.at(c + 1))
                    nc.scalar.activation(u[:, c], delta[:, c], ACT.Silu).then_inc(u_ready.sem, 1)
                act.wait_ge(low_rank.sem, low_rank.at(1))
                nc.scalar.activation(rank_in[:], m.banks[:, 0, :], ACT.Copy).then_inc(dt_in.sem, 1)
                for c in range(KC):
                    act.wait_ge(dt_done.sem, dt_done.at(c + 1))
                    v = m.banks[:, 4 + c % 2, :]
                    nc.scalar.activation(delta[:, c], v, ACT.Relu, bias=vec[:, c, 5:6])
                    nc.scalar.activation(du[:, c], v, ACT.Abs, bias=vec[:, c, 5:6]).then_inc(dt_parts.sem, 1)
                act.wait_ge(dt_parts.sem, dt_parts.at(KC))
                nc.scalar.activation(du, du, ACT.Exp, scale=-1.0).then_inc(softplus_step.sem, 1)
                nc.scalar.activation(A[:], A[:], ACT.Exp).then_inc(softplus_step.sem, 1)
                act.wait_ge(softplus_step.sem, softplus_step.at(2))
                nc.scalar.activation(du, du, ACT.Ln, bias=1.0).then_inc(softplus_step.sem, 1)
                for n in range(NS):
                    act.wait_ge(spread.sem, spread.at(2 * n + 1))
                    nc.scalar.activation(Bs[:, n], m.banks[:, n % 2, :], ACT.Copy).then_inc(b_stored.sem, 1)
                act.wait_ge(delta_ready.sem, delta_ready.at(1))
                with act.Fori(0, KC) as c:
                    for n in range(NS):
                        act.wait_ge(scanned.sem, scanned.at(NS * c + n + 1))
                        nc.scalar.activation(decay[:, n % 2],
                                             delta[:, bass.ds(c, 1), :].rearrange("p a t -> p (a t)"), ACT.Exp,
                                             scale=A[:, bass.ds(c, 1), n:n + 1].rearrange("p a n -> p (a n)"))\
                          .then_inc(decay_ready.sem, 1)
                        if n in (1, 3, 7, 11):
                            t = (1, 3, 7, 11).index(n)
                            act.wait_ge(gate_done.sem, gate_done.at(NT * c + t + 1))
                            nc.scalar.activation(act_out[t % 2][:], m.banks[:, t % 2, 0:D], ACT.Tanh, scale=0.5)\
                              .then_inc(gated.sem, 1)
                        if n in (4, 8, 12, 14):
                            t = (4, 8, 12, 14).index(n)
                            store_turned(act, NT * c + t, t % 2)

            @block.vector
            def _(dve):
                chain = Chain(dve, dve_chain)
                dve.wait_ge(square_step.sem, square_step.at(NT))
                nc.vector.tensor_scalar(m.rs[:, 0], square_sum[:], 1.0 / D, 1e-5, ALU.mult, ALU.add)\
                  .then_inc(stepped.sem, 1)
                dve.wait_ge(stepped.sem, stepped.at(1))
                dve.wait_ge(rooted.sem, rooted.at(1))
                reciprocal_root(nc, chain, m.rs)
                for t in range(NT):
                    nc.vector.tensor_scalar(xm[:, t], m.xn[:, t], m.rs[:, 3, t:t + 1], None, ALU.mult)\
                      .then_inc(scaled.sem, 1)
                dve.wait_ge(loaded.sem, loaded.at(16 * len(loads)))
                chain.all(nc.vector.memset(xp[:, :, 0:TAPS - 1], 0.0))
                conv = delta
                for c in range(KC):
                    dve.wait_ge(xs_ready.sem, xs_ready.at(c + 1))
                    chain.all(nc.vector.tensor_scalar(conv[:, c], xp[:, c, 0:T], vec[:, c, 0:1], vec[:, c, 4:5],
                                                      ALU.mult, ALU.add))
                    for j in range(1, TAPS):
                        last = nc.vector.scalar_tensor_tensor(conv[:, c], xp[:, c, j:j + T], vec[:, c, j:j + 1],
                                                              conv[:, c], ALU.mult, ALU.add)
                        if j < TAPS - 1:
                            chain.all(last)
                    last.then_inc(conv_ready.sem, 1)
                dve.wait_ge(low_rank.sem, low_rank.at(1))
                bc = m.banks[0:2 * NS, 1, :]
                chain.all(nc.vector.tensor_copy(split[0:2 * NS], bc))
                chain.all(nc.vector.tensor_tensor(rest[:], bc, split[0:2 * NS], ALU.subtract))
                chain.all(nc.vector.tensor_copy(mid[:], rest[:]))
                chain.link(nc.vector.tensor_copy(split[2 * NS:4 * NS], mid[:]))
                chain.link(nc.vector.tensor_tensor(split[4 * NS:6 * NS], rest[:], mid[:], ALU.subtract))
                chain.wait()
                nc.vector.memset(rest[:, 0:1], 0.0).then_inc(bc_split.sem, 1)
                dve.wait_ge(softplus_step.sem, softplus_step.at(3))
                chain.link(nc.vector.tensor_scalar(A[:], A[:], -1.0, None, ALU.mult))
                chain.all(nc.vector.tensor_tensor(delta[:], delta[:], du, ALU.add))
                chain.all(nc.vector.tensor_tensor(du, delta[:], u[:], ALU.mult))
                nc.vector.memset(rest[:, 0:1], 0.0).then_inc(delta_ready.sem, 1)
                for n in range(NS):
                    dve.wait_ge(spread.sem, spread.at(2 * n + 2))
                    nc.vector.tensor_copy(Cs[:, n], m.banks[:, 2 + n % 2, :]).then_inc(c_stored.sem, 1)
                dve.wait_ge(c_stored.sem, c_stored.at(NS))
                dve.wait_ge(b_stored.sem, b_stored.at(NS))
                dve.sem_inc(scanned.sem, 2)
                dve.sem_inc(y_taken.sem, 1)
                ahead = chain.n
                with dve.Fori(0, KC) as c:
                    tile = Chain(dve, dve_chain, ahead + CHAIN_TILE * c)
                    row = lambda a: a[:, bass.ds(c, 1), :].rearrange("p a t -> p (a t)")
                    scalar = lambda j: vec[:, bass.ds(c, 1), j:j + 1].rearrange("p a n -> p (a n)")
                    du_c = xp[:, bass.ds(c, 1), 0:T].rearrange("p a t -> p (a t)")
                    tile.link(nc.vector.tensor_tensor(inflow[:, 0], du_c, Bs[:, 0], ALU.mult))
                    for n in range(NS):
                        tile.wait()
                        dve.wait_ge(decay_ready.sem, decay_ready.at(NS * c + n + 1))
                        nc.vector.tensor_tensor_scan(state[:, n % 2], decay[:, n % 2], inflow[:, n % 2], 0.0,
                                                     ALU.mult, ALU.add).then_inc(scanned.sem, 1)
                        if n + 1 < NS:
                            tile.link(nc.vector.tensor_tensor(inflow[:, (n + 1) % 2], du_c, Bs[:, n + 1], ALU.mult))
                        dve.wait_ge(scanned.sem, scanned.at(NS * c + n + 3))
                        dve.wait_ge(summed.sem, summed.at(NS * c + n + 1))
                        nc.vector.tensor_tensor(product[:, n % 2], state[:, n % 2], Cs[:, n], ALU.mult)\
                          .then_inc(product_ready.sem, 1)
                        if n in (2, 4, 8, 12):
                            t = (2, 4, 8, 12).index(n)
                            dve.wait_ge(gated.sem, gated.at(NT * c + t + 1))
                            tile.all(nc.vector.scalar_tensor_tensor(blended[t % 2][:], act_out[t % 2][:], 1.0,
                                                                    m.banks[:, t % 2, D:2 * D], ALU.add, ALU.mult))
                            nc.vector.scalar_tensor_tensor(hidden[t % 2][:], blended[t % 2][:], 0.5,
                                                           m.banks[:, t % 2, 0:D], ALU.mult, ALU.mult)\
                              .then_inc(hidden_ready.sem, 1)
                    dve.wait_ge(summed.sem, summed.at(NS * c + NS + 2))
                    nc.vector.scalar_tensor_tensor(state[:, 0], row(u), scalar(6), y_psum, ALU.mult, ALU.add)\
                      .then_inc(y_taken.sem, 1)
                    dve.wait_ge(y_taken.sem, y_taken.at(c + 2))
                    nc.vector.tensor_tensor(yg[:], state[:, 0], row(silu_z), ALU.mult).then_inc(gated_y.sem, 1)
                dve_chain.close(ahead + KC * CHAIN_TILE)

        close()
        for s, n in ((in_weights, 16), (loaded, 16 * len(loads)), (square_step, NT), (stepped, 1), (rooted, 1),
                     (scaled, NT), (turned, KD), (xmT_ready, KD), (projected, 2 * KC), (xs_ready, KC),
                     (z_ready, KC), (conv_ready, KC), (u_ready, KC), (low_rank, 1), (dt_in, 1), (bc_split, 1),
                     (spread, 2 * NS), (b_stored, NS), (c_stored, NS), (dt_done, KC), (dt_parts, KC),
                     (softplus_step, 3), (delta_ready, 1), (decay_ready, KC * NS), (scanned, KC * NS + 2),
                     (product_ready, KC * NS), (summed, KC * NS + 2), (y_taken, KC + 1), (gated_y, KC),
                     (joined, KC)):
            s.close(n)


def clear_acc(m, pe):
    for h in range(2):
        m.nc.tensor.matmul(m.acc[:, h, :], m.one_row[:], m.zero_row[:], start=True, stop=False,
                           skip_group_check=True)


def linear_recurrence(m):
    nc, dram = m.nc, m.dram
    loaded, projected, h_ready, stepped = m.sig("lru_loaded"), m.sig("lru_projected"), m.sig("h_ready"), m.sig("lru_stepped")
    shape = Hidden(2, F2, F2_ROWS, 1, ACT.Silu)
    ITEMS = 2 * NT
    N2 = 2 * STATES
    STEPS = 9
    with ExitStack() as local_ctx:
        sb = m.local(local_ctx)
        w_b, w_c = sb("w_b", [P, KD, N2]), sb("w_c", [N2, D])
        h = sb("h", [N2, T])
        gu_w = m.lut_w[:, 0:KD * 2 * INTER2].rearrange("p (k w f) -> p k w f", k=KD, w=2)
        down_w = m.lut_w[:, KD * 2 * INTER2:].rearrange("p (r d) -> p r d", d=D)
        multiply, turn, add, activate, store_turned, gate, close, gate_done, _ = gated_mlp_engines(
            m, shape, sb, 0, lambda g, k: gu_w[:, k, :, g * F2:(g + 1) * F2],
            lambda g, r: down_w[:, 3 * g + r], None, None)
        lru_psum = m.banks[0:N2, 4 + 1, :]

        with nc.Block() as block:
            @block.sync
            def _(sp):
                sp.dma_start(w_b[:], dram["lru_b"]).then_inc(loaded.sem, 16)
                sp.dma_start(w_c[:], dram["lru_c"]).then_inc(loaded.sem, 16)

            @block.tensor
            def _(pe):
                clear_acc(m, pe)
                pe.wait_ge(loaded.sem, loaded.at(32))
                for k in range(KD):
                    last = nc.tensor.matmul(lru_psum, w_b[:, k], m.xnT[:, k], start=k == 0, stop=k == KD - 1)
                last.then_inc(projected.sem, 1)
                for s in range(STEPS):
                    pe.wait_ge(h_ready.sem, h_ready.at(s + 1))
                    shift = 1 << s
                    nc.tensor.matmul(lru_psum[:, shift:], m.lru_step[:, s], h[:, 0:T - shift], start=True, stop=True)\
                      .then_inc(stepped.sem, 1)
                pe.wait_ge(h_ready.sem, h_ready.at(STEPS + 1))
                for t in range(NT):
                    nc.tensor.matmul(m.acc_tile(t), h[:, t * P:(t + 1) * P], w_c[:], start=False, stop=False,
                                     skip_group_check=True)
                multiply(0, 0, 0)
                for n in range(ITEMS):
                    if n + 1 < ITEMS:
                        multiply((n + 1) % NT, (n + 1) % 2, (n + 1) // NT)
                    turn(pe, n, n % 2)
                    if n:
                        add(pe, n - 1, (n - 1) % NT, (n - 1) % 2, (n - 1) // NT)
                add(pe, ITEMS - 1, NT - 1, 1, 1)

            @block.vector
            def _(dve):
                dve.wait_ge(loaded.sem, loaded.at(32))
                dve.wait_ge(projected.sem, projected.at(1))
                nc.vector.tensor_scalar(w_c[STATES:], w_c[STATES:], -1.0, None, ALU.mult)
                nc.vector.tensor_scalar(h[:], lru_psum, m.lru_gamma[:], None, ALU.mult).then_inc(h_ready.sem, 1)
                for s in range(STEPS):
                    dve.wait_ge(h_ready.sem, h_ready.at(s + 1))
                    dve.wait_ge(stepped.sem, stepped.at(s + 1))
                    shift = 1 << s
                    nc.vector.tensor_tensor(h[:, shift:], h[:, shift:], lru_psum[:, shift:], ALU.add)\
                      .then_inc(h_ready.sem, 1)
                for n in range(ITEMS):
                    gate(dve, n, None, n % NT, n % 2)

            @block.scalar
            def _(act):
                for n in range(ITEMS):
                    activate(act, n, n % 2)
                    if n:
                        store_turned(act, n - 1, (n - 1) % 2)
                store_turned(act, ITEMS - 1, 1)
        close()
        loaded.close(32)
        for s, n in ((projected, 1), (h_ready, STEPS + 1), (stepped, STEPS)):
            s.close(n)


def finish(m, b, out, add_mixer=True):
    nc = m.nc
    joined, stored = m.sig("sequence_joined"), m.sig("sequence_stored")
    with nc.Block() as block:
        @block.vector
        def _(dve):
            for h in range(2):
                x_pair = m.x[:, 2 * h:2 * h + 2].rearrange("p t d -> p (t d)")
                nc.vector.tensor_tensor(x_pair, x_pair, m.acc[:, h, :], ALU.add).then_inc(joined.sem, 1)

        @block.sync
        def _(sp):
            for h in range(2):
                sp.wait_ge(joined.sem, joined.at(h + 1))
                sp.dma_start(out[b, h * 2 * P:(h + 1) * 2 * P].rearrange("(t p) d -> p t d", p=P),
                             m.x[:, 2 * h:2 * h + 2]).then_inc(stored.sem, 16)
            sp.wait_ge(stored.sem, stored.at(32))
    joined.close(2)
    stored.close(32)


def clear_stage(m):
    with m.nc.Block() as block:
        @block.tensor
        def _(pe):
            clear_acc(m, pe)


STOP = 4


def hybrid_stack_kernel(nc, dram, out):
    with ExitStack() as ctx:
        m = Machine(nc, ctx, dram)
        prepare(m)
        for b in range(BATCH):
            normalise(m, b, 0)
            attention(m, 0)
            mixture(m, 0)
            if STOP >= 2:
                normalise(m, b, 1)
                clear_stage(m)
                state_space(m)
            if STOP >= 3:
                normalise(m, b, 2)
                linear_recurrence(m)
            if STOP >= 4:
                normalise(m, b, 3)
                attention(m, 3)
                mixture(m, 3)
            finish(m, b, out)



def shape_constants():
    f32, bf16 = np.float32, np.dtype("bfloat16")
    out = {"ident": np.eye(P, dtype=f32), "ident_bf": np.eye(P).astype(bf16)}
    i = np.arange(P)
    out["mask_bf"] = np.where(i[None, :] > i[:, None], MASKED, 0.0).astype(bf16)
    freq = (f32(1.0 / 1024.0) ** np.linspace(0.0, 1.0, HD // 4, dtype=f32)).astype(f32)
    theta = np.arange(T, dtype=f32)[None, :] * freq[:, None]
    cos, sin = np.cos(theta.astype(np.float64)), np.sin(theta.astype(np.float64))
    out["rope_cos"] = np.concatenate([cos, cos]).astype(f32)
    out["rope_sin"] = np.concatenate([-sin, sin]).astype(f32)
    rows = np.arange(6 * NS)[:, None, None] % (2 * NS) == np.arange(2 * NS)[None, :, None]
    out["select"] = np.broadcast_to(rows, (6 * NS, 2 * NS, P)).astype(bf16)
    p = np.arange(2 * STATES)
    out["lru_fold"] = (p[:, None] % STATES == np.arange(STATES)[None, :]).astype(f32)
    re, im = (p < STATES).astype(f32), (p >= STATES).astype(f32)
    out["lru_sign"] = np.stack([re, -im, im, re], 1)
    base, frac, at = spline_grid()
    coef = np.zeros((P * 8, WINDOW, D), np.float64)
    f = frac.astype(np.float64)
    blend = (0.5 * (-f + 2 * f ** 2 - f ** 3), 0.5 * (2 - 5 * f ** 2 + 3 * f ** 3),
             0.5 * (f + 4 * f ** 2 - 3 * f ** 3), 0.5 * (-f ** 2 + f ** 3))
    r, c = np.arange(P * 8)[:, None], np.arange(D)[None, :]
    for k in range(4):
        coef[r, at + k, c] += blend[k]
    out["spline_coef"] = coef.astype(f32)[spline_rows_of()]
    return out


def spline_grid():
    n = INTER1 * D
    t = np.linspace(0.0, NCTRL - 1.0, n, dtype=np.float64)
    i = np.clip(np.floor(t).astype(np.int64), 0, NCTRL - 2)
    frac = (t - i).astype(np.float32).reshape(P * 8, D)
    i = i.reshape(P * 8, D)
    base = i[:, 0] - 1
    at = i - 1 - base[:, None]
    assert at.max() + 3 < WINDOW
    return base, frac, at


def spline_rows_of():
    half, q, p = np.meshgrid(np.arange(2), np.arange(4), np.arange(P), indexing="ij")
    return (4 * (half * P + p) + q).reshape(8, P)


def by_rows(w, rows=P):
    return np.ascontiguousarray(w.reshape(-1, rows, w.shape[-1]).transpose(1, 0, 2))


def laid_out(v):
    out = {"x": v["L0_attn_x"]}
    order = np.concatenate([np.arange(0, 32), np.arange(64, 96), np.arange(32, 64), np.arange(96, 128)])

    def qkv_heads(mats, biases):
        parts = []
        for w in mats:
            parts.append(w.reshape(KD, P, HEADS, HD).transpose(2, 1, 0, 3).reshape(HEADS, P, KD * HD))
        for b in biases:
            parts.append(b.reshape(HEADS, HD, 1))
        return np.ascontiguousarray(np.concatenate(parts, 2))

    q, k, w = (v[f"L0_attn_W{c}"].T.reshape(D, HEADS, HD) for c in "qkv")
    out["qkv0"] = qkv_heads([q[..., order], k[..., order], w], [])
    out["wo0"] = np.ascontiguousarray(v["L0_attn_Wo"].T.reshape(HEADS, HD, D))
    q, k, w = (v[f"L3_attn_w_{c}"].reshape(D, HEADS, HD) for c in "qkv")
    out["qkv3"] = qkv_heads([q, k, w], [v["L3_attn_b_q"], v["L3_attn_b_k"]])
    out["wo3"] = np.ascontiguousarray(np.concatenate([v["L3_attn_w_o"].reshape(HEADS, HD, D),
                                                      v["L3_attn_b_v"].reshape(HEADS, HD, 1)], 2))
    out["bo"] = v["L3_attn_b_o"].reshape(1, D)

    def gate_up(gate, up):
        both = np.stack([gate, up], 1).reshape(KD, P, 2, GROUPS, -1)
        return np.ascontiguousarray(both.transpose(3, 1, 0, 2, 4).reshape(GROUPS, P, -1))

    def down(w):
        w = w.reshape(GROUPS, -1, P, D)
        return np.ascontiguousarray(w.transpose(0, 2, 1, 3).reshape(GROUPS, P, -1))

    out["router0"] = by_rows(v["L0_ffn_router_w"].T)
    out["gate_up0"] = gate_up(*(v[f"L0_ffn_{c}_w"].transpose(2, 0, 1).reshape(D, -1) for c in ("gate", "up")))
    out["down0"] = down(v["L0_ffn_down_w"].transpose(0, 2, 1).reshape(E0 * I0, D))
    gu = v["L3_ffn_gate_up"].transpose(1, 0, 2).reshape(D, E3, 2, I3)
    out["router3"] = by_rows(v["L3_ffn_gate_w"])
    out["gate_up3"] = gate_up(gu[:, :, 0].reshape(D, -1), gu[:, :, 1].reshape(D, -1))
    out["down3"] = down(v["L3_ffn_down"].reshape(E3 * I3, D))
    out["router_scale"] = np.ascontiguousarray(v["L3_ffn_router_scale"].reshape(KD, P).T)
    out["per_expert"] = v["L3_ffn_per_expert_scale"].reshape(1, E3)

    out["w_norm"] = np.ascontiguousarray(v["L1_attn_w_norm"].reshape(KD, P).T)
    out["w_in"] = by_rows(v["L1_attn_W_in"])
    out["w_xp"] = by_rows(v["L1_attn_W_xp"])
    out["w_dt"] = v["L1_attn_W_dt"]
    out["w_out"] = by_rows(v["L1_attn_W_out"])
    vec = np.concatenate([v["L1_attn_conv_w"], v["L1_attn_conv_b"][None], v["L1_attn_b_dt"][None],
                          v["L1_attn_D"][None]])
    out["ss_vec"] = np.ascontiguousarray(vec.reshape(7, KC, P).transpose(2, 1, 0))
    out["a_log"] = by_rows(v["L1_attn_A_log"])
    base, _, _ = spline_grid()
    window = np.clip(base[:, None] + np.arange(WINDOW), 0, NCTRL - 1)[spline_rows_of()]
    points = np.stack([v[f"L1_ffn_{c}_cp"][window] for c in ("gate", "up", "down")], 2)
    out["spline_points"] = np.ascontiguousarray(points.transpose(1, 0, 2, 3))

    out["lru_in"] = np.stack([np.tile(v["L2_attn_nu_log"], 2), np.tile(v["L2_attn_theta_log"], 2)], 1)
    out["lru_b"] = by_rows(np.concatenate([v["L2_attn_B_re"], v["L2_attn_B_im"]]).T)
    out["lru_c"] = np.ascontiguousarray(np.concatenate([v["L2_attn_C_re"].T, v["L2_attn_C_im"].T]))
    out["lru_d"] = v["L2_attn_D"].reshape(1, D)
    out["lut"] = v["L2_ffn_lut"].reshape(1, LUT)
    gu = np.stack([v["L2_ffn_gate_idx"].T, v["L2_ffn_up_idx"].T], 1)
    gu = gu.reshape(KD, P, 2 * INTER2).transpose(1, 0, 2).reshape(P, -1)
    dn = np.zeros((2, 3 * P, D), v["L2_ffn_down_idx"].dtype)
    dn[:, :F2] = v["L2_ffn_down_idx"].T.reshape(2, F2, D)
    dn = dn.reshape(6, P, D).transpose(1, 0, 2).reshape(P, -1)
    out["lut_idx"] = np.ascontiguousarray(np.concatenate([gu, dn], 1))
    return out


def kernel(**inputs):
    import concourse.bacc as bacc
    from concourse.bass_utils import run_bass_kernel_spmd

    arrays = laid_out({name: np.asarray(a) for name, a in inputs.items()})
    arrays.update(shape_constants())
    arrays = {f"in_{name}": np.ascontiguousarray(a) for name, a in arrays.items()}
    nc = bacc.Bacc("TRN2", target_bir_lowering=False, num_devices=1)
    dram = {name[3:]: nc.dram_tensor(name, a.shape, mybir.dt.from_np(a.dtype), kind="ExternalInput").ap()
            for name, a in arrays.items()}
    out = nc.dram_tensor("out", (BATCH, T, D), FP32, kind="ExternalOutput").ap()
    hybrid_stack_kernel(nc, dram, out)
    result = run_bass_kernel_spmd(nc, [arrays], core_ids=[0])
    return result.results[0]["out"]
```

```python
from contextlib import ExitStack

import numpy as np

import concourse.bass as bass
from concourse import mybir

FP32 = mybir.dt.float32
FP32R = mybir.dt.float32r
BF16 = mybir.dt.bfloat16
INT32 = mybir.dt.int32
ACT = mybir.ActivationFunctionType
ALU = mybir.AluOpType
AXIS = mybir.AxisListType

P = 128
BATCH, T, D = 2, 512, 256
NT = T // P
KD = D // P
HEADS, HD = 16, 128
QK_SCALE = float(HD) ** -0.5
MASKED = -1e30

E0, TOP0, I0 = 32, 4, 96
E3, TOP3, I3 = 8, 2, 256
GROUPS = 8
F0 = E0 * I0 // GROUPS
F3 = E3 * I3 // GROUPS

CH, NS, RANK, TAPS = 512, 16, 128, 4
KC = CH // P
INTER1 = 1024
NCTRL = max(16, int(INTER1 * D / 128.9))
WINDOW = 6
STATES = 32
INTER2 = 688
F2 = INTER2 // 2
F2_ROWS = (P, P, F2 - 2 * P)
LUT = 16
LUT_COLS = KD * 2 * INTER2 + 6 * D
LUT_CHUNK = LUT_COLS // GROUPS
TWO_PI = 2.0 * np.pi


class Signal:

    def __init__(self, nc, ctx, name):
        self.sem = ctx.enter_context(nc.semaphore(name))
        self.base = 0

    def at(self, n):
        return self.base + n

    def close(self, n):
        self.base = self.base + n


class Chain:

    def __init__(self, eng, count, start=0):
        self.eng, self.count, self.start, self.n = eng, count, start, 0

    def link(self, instruction):
        instruction.then_inc(self.count.sem, 1)
        self.n += 1

    def wait(self):
        self.eng.wait_ge(self.count.sem, self.count.at(self.start + self.n))

    def all(self, instruction):
        self.link(instruction)
        self.wait()


class Machine:

    def __init__(self, nc, ctx, dram):
        self.nc, self.ctx, self.dram = nc, ctx, dram
        self.signals = {}
        sb = lambda name, shape, dt=FP32: ctx.enter_context(nc.sbuf_tensor(name, shape, dt))
        self.x = sb("x", [P, NT, D])
        self.xn = sb("xn", [P, NT, D])
        self.xnT = sb("xnT", [P, KD, T])
        self.xnT_parts = [sb(f"xnT_{part}", [P, KD, T], FP32R) for part in ("high", "low")]
        self.stats = sb("stats", [P, NT, 6])
        self.mv = sb("mv", [P, NT, 2])
        self.rs = sb("rs", [P, 6, NT])
        self.ident = sb("ident", [P, P])
        self.ident_bf = sb("ident_bf", [P, P], BF16)
        self.mask_bf = sb("mask_bf", [P, P], BF16)
        self.zero_row = sb("zero_row", [1, T])
        self.one_row = sb("one_row", [1, P])
        self.bo_row = sb("bo_row", [1, 2, D])
        self.spline_gu = sb("spline_gu", [P, KD, 2, INTER1])
        self.spline_down = sb("spline_down", [P, INTER1 // P, D])
        self.lut_w = sb("lut_w", [P, LUT_COLS])
        self.lru_step = sb("lru_step", [2 * STATES, 9, 2 * STATES])
        self.lru_gamma = sb("lru_gamma", [2 * STATES, 1])
        self.acc = ctx.enter_context(nc.psum_tensor("acc", [P, 2, 512], FP32))
        self.banks = ctx.enter_context(nc.psum_tensor("banks", [P, 6, 512], FP32))

    def sig(self, name):
        if name not in self.signals:
            self.signals[name] = Signal(self.nc, self.ctx, name)
        return self.signals[name]

    def local(self, stage_ctx):
        self.n_local = 1 + (self.n_local if hasattr(self, "n_local") else 0)
        tag = self.n_local
        return lambda name, shape, dt=FP32: stage_ctx.enter_context(
            self.nc.sbuf_tensor(f"{name}_{tag}", shape, dt))

    def acc_tile(self, t):
        return self.acc[:, t // 2, (t % 2) * D:(t % 2 + 1) * D]


def exact_product(nc, out, left, right, start, stop, **kw):
    for n, (a, b) in enumerate(((0, 0), (0, 1), (1, 0))):
        last = nc.tensor.matmul(out, left[a], right[b], start=start and n == 0, stop=stop and n == 2, **kw)
    return last


def reciprocal_root(nc, chain, rs):
    chain.all(nc.vector.reciprocal(rs[:, 2], rs[:, 1]))
    chain.all(nc.vector.tensor_tensor(rs[:, 4], rs[:, 2], rs[:, 2], ALU.mult))
    chain.all(nc.vector.tensor_tensor(rs[:, 4], rs[:, 4], rs[:, 0], ALU.mult))
    chain.all(nc.vector.tensor_scalar(rs[:, 4], rs[:, 4], -0.5, 1.5, ALU.mult, ALU.add))
    chain.all(nc.vector.tensor_tensor(rs[:, 3], rs[:, 2], rs[:, 4], ALU.mult))


def prepare(m):
    nc, dram = m.nc, m.dram
    with ExitStack() as local_ctx:
        sb = m.local(local_ctx)
        lru_in = sb("lru_in", [2 * STATES, 2])
        lru_sign = sb("lru_sign", [2 * STATES, 4])
        lru_fold = sb("lru_fold", [2 * STATES, STATES])
        lru = sb("lru", [2 * STATES, 24])
        turns = sb("turns", [2 * STATES, 1], INT32)
        power = sb("power", [2 * STATES, 2, 9])
        blend = sb("blend", [2 * STATES, 4, 9])
        loaded = m.sig("constants_loaded")
        dve_chain, act_chain = m.sig("dve_chain"), m.sig("act_chain")
        lru_act, lru_dve = m.sig("lru_act"), m.sig("lru_dve")
        constants = [
            (m.ident[:], dram["ident"]), (m.ident_bf[:], dram["ident_bf"]), (m.mask_bf[:], dram["mask_bf"]),
            (m.bo_row[:, 0, :], dram["bo"]), (m.bo_row[:, 1, :], dram["bo"]),
            (lru_in[:], dram["lru_in"]), (lru_sign[:], dram["lru_sign"]), (lru_fold[:], dram["lru_fold"]),
        ]

        with nc.Block() as block:
            @block.sync
            def _(sp):
                for dst, src in constants:
                    sp.dma_start(dst, src).then_inc(loaded.sem, 16)

            @block.scalar
            def _(act):
                act.wait_ge(loaded.sem, loaded.at(16 * len(constants)))
                chain = Chain(act, act_chain)
                chain.all(nc.scalar.activation(lru[:, 0:1], lru_in[:, 0:1], ACT.Abs))
                chain.all(nc.scalar.activation(lru[:, 1:2], lru[:, 0:1], ACT.Exp, scale=-1.0))
                nc.scalar.activation(lru[:, 3:4], lru_in[:, 1:2], ACT.Exp).then_inc(lru_act.sem, 1)
                chain.all(nc.scalar.activation(lru[:, 2:3], lru[:, 1:2], ACT.Ln, bias=1.0))
                act.wait_ge(lru_dve.sem, lru_dve.at(1))
                chain.all(nc.scalar.activation(lru[:, 5:6], lru[:, 4:5], ACT.Identity, bias=lru[:, 2:3]))
                chain.all(nc.scalar.activation(lru[:, 6:7], lru[:, 5:6], ACT.Exp))
                nc.scalar.activation(lru[:, 7:8], lru[:, 6:7], ACT.Exp, scale=-1.0).then_inc(lru_act.sem, 1)
                act.wait_ge(lru_dve.sem, lru_dve.at(2))
                nc.scalar.activation(lru[:, 14:15], lru[:, 12:13], ACT.Sin)
                nc.scalar.activation(lru[:, 15:16], lru[:, 13:14], ACT.Sin).then_inc(lru_act.sem, 1)
                act.wait_ge(lru_dve.sem, lru_dve.at(3))
                nc.scalar.activation(m.lru_gamma[:], lru[:, 17:18], ACT.Sqrt)
                act_chain.close(chain.n)

            @block.vector
            def _(dve):
                chain = Chain(dve, dve_chain)
                nc.vector.memset(m.zero_row[:], 0.0)
                nc.vector.memset(m.one_row[:], 1.0)
                dve.wait_ge(loaded.sem, loaded.at(16 * len(constants)))
                nc.vector.tensor_scalar(lru[:, 4:5], lru_in[:, 0:1], 0.0, None, ALU.max).then_inc(lru_dve.sem, 1)
                dve.wait_ge(lru_act.sem, lru_act.at(1))
                chain.all(nc.vector.tensor_scalar(turns[:], lru[:, 3:4], float(1.0 / TWO_PI), None, ALU.mult))
                chain.all(nc.vector.tensor_copy(lru[:, 8:9], turns[:]))
                c1 = 6.28125
                c2 = float(np.float32(TWO_PI - c1))
                c2 = float(np.frombuffer(np.uint32(np.float32(c2).view(np.uint32) & 0xFFFFF000).tobytes(), np.float32)[0])
                c3 = float(TWO_PI - c1 - c2)
                chain.all(nc.vector.scalar_tensor_tensor(lru[:, 9:10], lru[:, 8:9], -c1, lru[:, 3:4], ALU.mult, ALU.add))
                chain.all(nc.vector.scalar_tensor_tensor(lru[:, 10:11], lru[:, 8:9], -c2, lru[:, 9:10], ALU.mult, ALU.add))
                chain.all(nc.vector.scalar_tensor_tensor(lru[:, 11:12], lru[:, 8:9], -c3, lru[:, 10:11], ALU.mult, ALU.add))
                fold_turn(nc, chain, lru, 11, 16, 18)
                chain.all(nc.vector.tensor_scalar(lru[:, 19:20], lru[:, 16:17], float(np.pi / 2), None, ALU.add))
                fold_turn(nc, chain, lru, 19, 20, 18)
                limit = float(np.nextafter(np.float32(np.pi), np.float32(0)))
                chain.all(nc.vector.tensor_scalar(lru[:, 12:13], lru[:, 16:17], -limit, limit, ALU.max, ALU.min))
                nc.vector.tensor_scalar(lru[:, 13:14], lru[:, 20:21], -limit, limit, ALU.max, ALU.min)\
                  .then_inc(lru_dve.sem, 1)
                dve.wait_ge(lru_act.sem, lru_act.at(3))
                chain.all(nc.vector.tensor_tensor(lru[:, 21:22], lru[:, 7:8], lru[:, 7:8], ALU.mult))
                chain.all(nc.vector.tensor_scalar(lru[:, 22:23], lru[:, 21:22], -1.0, 1.0, ALU.mult, ALU.add))
                nc.vector.tensor_scalar(lru[:, 17:18], lru[:, 22:23], 0.0, None, ALU.max).then_inc(lru_dve.sem, 1)
                nc.vector.tensor_tensor(power[:, 0, 0:1], lru[:, 7:8], lru[:, 15:16], ALU.mult)
                chain.all(nc.vector.tensor_tensor(power[:, 1, 0:1], lru[:, 7:8], lru[:, 14:15], ALU.mult))
                for s in range(1, 9):
                    re, im = power[:, 0, s - 1:s], power[:, 1, s - 1:s]
                    nc.vector.tensor_tensor(blend[:, 0, 0:1], re, re, ALU.mult)
                    nc.vector.tensor_tensor(blend[:, 1, 0:1], im, im, ALU.mult)
                    chain.all(nc.vector.scalar_tensor_tensor(power[:, 1, s:s + 1], re, 2.0, im, ALU.mult, ALU.mult))
                    chain.all(nc.vector.tensor_tensor(power[:, 0, s:s + 1], blend[:, 0, 0:1], blend[:, 1, 0:1],
                                                      ALU.subtract))
                for c in range(2):
                    nc.vector.tensor_scalar(blend[:, 0], power[:, 0], lru_sign[:, 2 * c:2 * c + 1], None, ALU.mult)
                    chain.all(nc.vector.tensor_scalar(blend[:, 1], power[:, 1], lru_sign[:, 2 * c + 1:2 * c + 2],
                                                      None, ALU.mult))
                    chain.all(nc.vector.tensor_tensor(blend[:, 2 + c], blend[:, 0], blend[:, 1], ALU.add))
                for s in range(9):
                    for c in range(2):
                        nc.vector.tensor_scalar(m.lru_step[:, s, c * STATES:(c + 1) * STATES], lru_fold[:],
                                                blend[:, 2 + c, s:s + 1], None, ALU.mult)
                dve_chain.close(chain.n)

        for s, n in ((loaded, 16 * len(constants)), (lru_act, 3), (lru_dve, 3)):
            s.close(n)


class SplineRows:

    def __init__(self, m, ctx):
        sb = m.local(ctx)
        self.m = m
        self.rows = sb("spline_rows", [P, 8, 3, D])
        self.loaded, self.chain = m.sig("points_loaded"), m.sig("pool_chain")
        self.coef_loaded = [m.sig(f"coef_loaded{i}") for i in range(2)]

    def allocate(self, sb):
        self.coef = sb("coef", [P, 2, WINDOW, D])
        self.term = sb("term", [P, 2, 3, D])
        self.points = sb("points", [P, 8, 3, WINDOW])

    def make(self, pool, interlude):
        m, nc = self.m, self.m.nc
        load = lambda n: pool.dma_start(self.coef[:, n % 2], m.dram["spline_coef"][n])\
            .then_inc(self.coef_loaded[n % 2].sem, 16)
        pool.dma_start(self.points[:], m.dram["spline_points"]).then_inc(self.loaded.sem, 16)
        load(0)
        load(1)
        pool.wait_ge(self.loaded.sem, self.loaded.at(16))
        chain = Chain(pool, self.chain)
        for n in range(8):
            pool.wait_ge(self.coef_loaded[n % 2].sem, self.coef_loaded[n % 2].at(16 * (n // 2 + 1)))
            rows = self.rows[:, n]
            for j in range(WINDOW):
                for w in range(3):
                    out = self.term[:, j % 2, w] if j else rows[:, w]
                    chain.link(nc.gpsimd.tensor_scalar(out, self.coef[:, n % 2, j], self.points[:, n, w, j:j + 1],
                                                       1.0, ALU.mult, ALU.mult))
                chain.wait()
                if j == WINDOW // 2:
                    interlude(2 * n)
                if j:
                    chain.link(nc.gpsimd.tensor_tensor(rows, rows, self.term[:, j % 2], ALU.add))
            chain.wait()
            if n + 2 < 8:
                load(n + 2)
            interlude(2 * n + 1)
        self.chain.close(chain.n)
        self.loaded.close(16)
        for s in self.coef_loaded:
            s.close(64)

    def turn(self):
        m, nc = self.m, self.m.nc
        turned, stored = m.sig("rows_turned"), m.sig("turned_stored")
        with nc.Block() as block:
            @block.tensor
            def _(pe):
                for n in range(8):
                    if n >= 2:
                        pe.wait_ge(stored.sem, stored.at(n - 1))
                    for w in range(3):
                        for k in range(KD):
                            at = ((w % 2) * 2 + k) * P
                            last = nc.tensor.transpose(m.banks[:, 2 * (n % 2) + w // 2, at:at + P],
                                                       self.rows[:, n, w, k * P:(k + 1) * P], m.ident[:])
                    last.then_inc(turned.sem, 1)

            @block.scalar
            def _(act):
                for n in range(8):
                    act.wait_ge(turned.sem, turned.at(n + 1))
                    half, q = divmod(n, 4)
                    b = 2 * (n % 2)
                    for w in range(2):
                        out = m.spline_gu[:, :, w, half * 512:(half + 1) * 512]
                        out = out.rearrange("p k (c q) -> p k q c", q=4)[:, :, q, :]
                        src = m.banks[:, b, w * 2 * P:(w + 1) * 2 * P].rearrange("p (k c) -> p k c", k=KD)
                        nc.scalar.activation(out, src, ACT.Copy)
                    src = m.banks[:, b + 1, 0:2 * P].rearrange("p (k c) -> p k c", k=KD)
                    nc.scalar.activation(m.spline_down[:, 2 * q:2 * q + 2, half * P:(half + 1) * P], src, ACT.Copy)\
                      .then_inc(stored.sem, 1)
        turned.close(8)
        stored.close(8)


class TableWeights:
    LINKS = 4 + LUT // 2 + 7 + 1

    def __init__(self, m, ctx):
        sb = m.local(ctx)
        self.m = m
        self.idx = sb("idx", [P, 2, LUT_CHUNK], INT32)
        self.bits = sb("bits", [P, 4, LUT_CHUNK], INT32)
        self.leaves = sb("leaves", [P, LUT // 2, LUT_CHUNK])
        self.table, self.delta = sb("table", [P, LUT]), sb("delta", [P, LUT // 2])
        self.carrier = sb("carrier", [P, 3])
        self.loaded, self.chain = m.sig("table_loaded"), m.sig("table_chain")
        self.idx_loaded = [m.sig(f"idx_loaded{i}") for i in range(2)]
        self.read = m.sig("chunk_read")

    def load(self, sp, g, par):
        src = self.m.dram["lut_idx"][bass.ds(g, 1)].rearrange("a p f -> (a p) f")
        sp.dma_start(self.idx[:, par], src).then_inc(self.idx_loaded[par].sem, 16)

    def start(self, sp):
        sp.dma_start(self.table[:], self.m.dram["lut"].broadcast_to([P, LUT])).then_inc(self.loaded.sem, 16)

    def first(self, dve):
        dve.wait_ge(self.loaded.sem, self.loaded.at(16))
        low, high = (self.table[:].rearrange("p (j e) -> p e j", e=2)[:, e] for e in range(2))
        self.m.nc.vector.tensor_tensor(self.delta[:], high, low, ALU.subtract).then_inc(self.loaded.sem, 1)

    def part(self, dve, g, par, pair, quarter):
        nc, chain = self.m.nc, Chain(dve, self.chain, self.LINKS * g)
        carry = lambda n: nc.vector.memset(self.carrier[:, n:n + 1], 0.0)
        done = (0, 4, 4 + LUT // 2, 8 + LUT // 2)[quarter]
        chain.n = done
        tree, bits = self.leaves, self.bits
        if quarter == 0:
            dve.wait_ge(self.idx_loaded[par].sem, self.idx_loaded[par].at(16 * (pair + 1)))
            for b in range(4):
                ins = nc.vector.tensor_scalar(bits[:, b], self.idx[:, par], 1 << b, None, ALU.bitwise_and)
                chain.link(ins)
        if quarter == 1:
            chain.wait()
            dve.sem_inc(self.read.sem, 1)
            for j in range(LUT // 2):
                chain.link(nc.vector.tensor_scalar(tree[:, j], bits[:, 0], self.delta[:, j:j + 1],
                                                   self.table[:, 2 * j:2 * j + 1], ALU.mult, ALU.add))
        if quarter == 2:
            chain.wait()
            carry(0)
            for a in (0, 2, 4, 6):
                chain.link(nc.vector.copy_predicated(tree[:, a], bits[:, 1], tree[:, a + 1]))
        if quarter == 3:
            chain.wait()
            carry(1)
            for a in (0, 4):
                chain.link(nc.vector.copy_predicated(tree[:, a], bits[:, 2], tree[:, a + 2]))
            chain.wait()
            carry(2)
            chain.link(nc.vector.copy_predicated(tree[:, 0], bits[:, 3], tree[:, 4]))
            chain.wait()
            chain.link(nc.vector.tensor_copy(self.m.lut_w[:, bass.ds(g * LUT_CHUNK, LUT_CHUNK)], tree[:, 0]))

    def close(self):
        self.loaded.close(17)
        self.chain.close(GROUPS * self.LINKS)
        self.read.close(GROUPS)
        for s in self.idx_loaded:
            s.close(16 * GROUPS // 2)


def fold_turn(nc, chain, v, src, dst, tmp):
    chain.all(nc.vector.tensor_scalar(v[:, tmp:tmp + 1], v[:, src:src + 1], float(np.pi), -TWO_PI,
                                      ALU.is_gt, ALU.mult))
    chain.all(nc.vector.tensor_tensor(v[:, dst:dst + 1], v[:, src:src + 1], v[:, tmp:tmp + 1], ALU.add))
    chain.all(nc.vector.tensor_scalar(v[:, tmp:tmp + 1], v[:, dst:dst + 1], -float(np.pi), TWO_PI,
                                      ALU.is_lt, ALU.mult))
    chain.all(nc.vector.tensor_tensor(v[:, dst:dst + 1], v[:, dst:dst + 1], v[:, tmp:tmp + 1], ALU.add))


def normalise(m, b, layer):
    nc = m.nc
    stepped, rooted, normed = m.sig("ln_var"), m.sig("ln_root"), m.sig("ln_normed")
    turned, loaded = m.sig("ln_turned"), m.sig("x_loaded")
    dve_chain, high_ready = m.sig("dve_chain"), m.sig("xnT_high")
    with ExitStack() as local_ctx:
        sb = m.local(local_ctx)
        extra = sb("extra", [P, NT, D])
        skip = sb("skip", [P, D])
        with nc.Block() as block:
            @block.sync
            def _(sp):
                if layer == 0:
                    sp.dma_start(m.x[:], m.dram["x"][b].rearrange("(t p) d -> p t d", p=P)).then_inc(loaded.sem, 16)
                if layer == 3:
                    sp.dma_start(skip[:], m.dram["lru_d"].broadcast_to([P, D])).then_inc(loaded.sem, 16)

            @block.vector
            def _(dve):
                chain = Chain(dve, dve_chain)
                if layer in (0, 3):
                    dve.wait_ge(loaded.sem, loaded.at(16))
                if layer:
                    for h in range(2):
                        x_pair = m.x[:, 2 * h:2 * h + 2].rearrange("p t d -> p (t d)")
                        chain.link(nc.vector.tensor_tensor(x_pair, x_pair, m.acc[:, h, :], ALU.add))
                    if layer == 2:
                        chain.wait()
                        chain.link(nc.vector.tensor_tensor(m.x[:], m.x[:], m.xn[:], ALU.add))
                    if layer == 3:
                        chain.link(nc.vector.tensor_tensor(extra[:], m.xn[:],
                                                           skip[:].unsqueeze(1).broadcast_to([P, NT, D]), ALU.mult))
                        chain.wait()
                        chain.link(nc.vector.tensor_tensor(m.x[:], m.x[:], extra[:], ALU.add))
                    chain.wait()
                for t in range(NT):
                    chain.link(nc.vector.bn_stats(m.stats[:, t], m.x[:, t]))
                chain.wait()
                for t in range(NT):
                    chain.link(nc.vector.bn_aggr(m.mv[:, t], m.stats[:, t]))
                chain.wait()
                nc.vector.tensor_scalar(m.rs[:, 0], m.mv[:, :, 1], 1e-5, None, ALU.add).then_inc(stepped.sem, 1)
                dve.wait_ge(stepped.sem, stepped.at(1))
                dve.wait_ge(rooted.sem, rooted.at(1))
                reciprocal_root(nc, chain, m.rs)
                for t in range(NT):
                    last = nc.vector.tensor_scalar(m.xn[:, t], m.x[:, t], m.mv[:, t, 0:1], m.rs[:, 3, t:t + 1],
                                                   ALU.subtract, ALU.mult)
                    last.then_inc(normed.sem, 1)
                for k in range(KD):
                    dve.wait_ge(high_ready.sem, high_ready.at(k + 1))
                    high, low = (part[:, k] for part in m.xnT_parts)
                    nc.vector.tensor_tensor(low, m.banks[:, k, :], high.bitcast(FP32), ALU.subtract)
                dve_chain.close(chain.n)

            @block.scalar
            def _(act):
                act.wait_ge(stepped.sem, stepped.at(1))
                nc.scalar.activation(m.rs[:, 1], m.rs[:, 0], ACT.Sqrt).then_inc(rooted.sem, 1)
                for k in range(KD):
                    act.wait_ge(turned.sem, turned.at(k + 1))
                    nc.scalar.activation(m.xnT[:, k], m.banks[:, k, :], ACT.Copy)
                    nc.scalar.activation(m.xnT_parts[0][:, k], m.banks[:, k, :], ACT.Copy)\
                      .then_inc(high_ready.sem, 1)

            @block.tensor
            def _(pe):
                for k in range(KD):
                    for t in range(NT):
                        pe.wait_ge(normed.sem, normed.at(t + 1))
                        last = nc.tensor.transpose(m.banks[:, k, t * P:(t + 1) * P],
                                                   m.xn[:, t, k * P:(k + 1) * P], m.ident[:])
                    last.then_inc(turned.sem, 1)
        for s, n in ((stepped, 1), (rooted, 1), (normed, NT), (turned, KD), (high_ready, KD)):
            s.close(n)
        if layer in (0, 3):
            loaded.close(16)


SCORE_AT = {3: (0, 0), 2: (1, 0), 1: (2, 0), 0: (2, 2 * P)}
PROB_AT = {3: 0, 2: T, 1: T + 3 * P, 0: T + 5 * P}
PROB_COLS = 10 * P
TURNED_BANKS = ((0, 4 * P), (T, 3 * P), (T + 3 * P, 3 * P))


def attention(m, layer, spline=None):
    nc = m.nc
    rotary = layer == 0
    heads_dram = m.dram[f"heads{layer}"]
    loaded = [m.sig(f"head_loaded{i}") for i in range(2)]
    qkv_high, qkv_split, wo_high, wo_split = m.sig("qkv_high"), m.sig("qkv_split"), m.sig("wo_high"), m.sig("wo_split")
    qk_high, v_low, probsT_low, y_low = m.sig("qk_high"), m.sig("v_low"), m.sig("probsT_low"), m.sig("y_low")
    qk_projected, v_projected, scored = m.sig("qk_projected"), m.sig("v_projected"), m.sig("scored")
    turned, attended, added = m.sig("turned"), m.sig("attended"), m.sig("head_added")
    qk_ready, qk_rest_ready, max_ready = m.sig("qk_ready"), m.sig("qk_rest_ready"), m.sig("max_ready")
    exp_ready, probs_ready, v_ready = m.sig("exp_ready"), m.sig("probs_ready"), m.sig("v_ready")
    probsT_ready, y_ready, dve_chain = m.sig("probsT_ready"), m.sig("y_ready"), m.sig("dve_chain")
    rope_loaded = m.sig("rope_loaded")
    CHAIN_QK = 3 if rotary else 0
    CHAIN_SOFTMAX = 5

    with ExitStack() as local_ctx:
        sb = m.local(local_ctx)
        QKV = 3 * KD * HD
        raw = [sb(f"head{i}", [P, QKV + D]) for i in range(2)]
        parts = [[sb(f"head_{part}{i}", [P, QKV + D], FP32R) for part in ("high", "low")] for i in range(2)]
        qkT = sb("qkT", [P, 2, T], FP32 if rotary else FP32R)
        v = [sb(f"v{i}", [P, NT, HD], FP32 if rotary else FP32R) for i in range(2)]
        if not rotary:
            qkT_low = sb("qkT_low", [P, 2, T], FP32R)
            v_lows = [sb(f"v_low{i}", [P, NT, HD], FP32R) for i in range(2)]
            probsT_lows = sb("probsT_low", [P, PROB_COLS], FP32R)
            biases = sb("biases", [P, HEADS, 3])
        if rotary:
            rot = sb("rot", [64, 2, 2, T])
            rope_cos, rope_sin = sb("rope_cos", [64, T]), sb("rope_sin", [64, T])
        probs = sb("probs", [P, PROB_COLS])
        probsT = sb("probsT", [P, PROB_COLS], FP32 if rotary else FP32R)
        yT, yT_low = sb("yT", [P, T], FP32R), sb("yT_low", [P, T], FP32R)
        row_max, neg_max = sb("row_max", [P, NT]), sb("neg_max", [P, NT])
        row_sum, row_inv = sb("row_sum", [P, NT]), sb("row_inv", [P, NT])
        if spline:
            spline.allocate(sb)
        bias_of = lambda h, which: biases[:, bass.ds(h, 1), which:which + 1].rearrange("p a n -> p (a n)")
        qk_psum, v_psum = m.banks[:, 3:5, :], m.banks[:, 5, :]

        def score_tile(i):
            b, at = SCORE_AT[i]
            return m.banks[:, b, at:at + (i + 1) * P]

        def prob_tile(i):
            return probs[:, PROB_AT[i]:PROB_AT[i] + (i + 1) * P]

        def turned_tile(k, of=None):
            return (probsT if of is None else of)[:, PROB_AT[3 - k]:PROB_AT[3 - k] + (NT - k) * P]

        with nc.Block() as block:
            @block.sync
            def _(sp):
                def load(h, par):
                    sp.dma_start(raw[par][:], head_rows(heads_dram, h)).then_inc(loaded[par].sem, 16)

                load(0, 0)
                if rotary:
                    sp.dma_start(rope_cos[:], m.dram["rope_cos"]).then_inc(rope_loaded.sem, 16)
                    sp.dma_start(rope_sin[:], m.dram["rope_sin"]).then_inc(rope_loaded.sem, 16)
                else:
                    sp.dma_start(biases[:], m.dram["biases3"]).then_inc(rope_loaded.sem, 16)
                load(1, 1)
                with sp.Fori(0, HEADS // 2 - 1) as i:
                    for par in range(2):
                        h = 2 * i + par
                        sp.wait_ge(qkv_split.sem, qkv_split.at(h + 1))
                        sp.wait_ge(wo_split.sem, wo_split.at(h + 1))
                        load(h + 2, par)

            @block.tensor
            def _(pe):
                def project_qk(par):
                    for which in range(2):
                        for k in range(KD):
                            at = (which * KD + k) * HD
                            last = exact_product(nc, qk_psum[:, which], [a[:, at:at + HD] for a in parts[par]],
                                                 [a[:, k] for a in m.xnT_parts], k == 0, k == KD - 1)
                    last.then_inc(qk_projected.sem, 1)

                def project_v(par):
                    for t in range(NT):
                        for k in range(KD):
                            at = (2 * KD + k) * HD
                            last = exact_product(nc, v_psum[:, t * P:(t + 1) * P],
                                                 [a[:, k, t * P:(t + 1) * P] for a in m.xnT_parts],
                                                 [a[:, at:at + HD] for a in parts[par]], k == 0, k == KD - 1)
                    last.then_inc(v_projected.sem, 1)

                def project(h, par):
                    pe.wait_ge(qkv_split.sem, qkv_split.at(h + 1))
                    project_qk(par)

                def score():
                    for i in (3, 2, 1, 0):
                        out = score_tile(i)
                        q, key = slice(i * P, (i + 1) * P), slice(0, (i + 1) * P)
                        if rotary:
                            nc.tensor.matmul(out, qkT[:, 0, q], qkT[:, 1, key], start=True, stop=False)
                        else:
                            exact_product(nc, out, [a[:, 0, q] for a in (qkT, qkT_low)],
                                          [a[:, 1, key] for a in (qkT, qkT_low)], True, False)
                        last = nc.tensor.matmul(out[:, i * P:(i + 1) * P], m.ident_bf[:], m.mask_bf[:],
                                                start=False, stop=True)
                        if i != 1:
                            last.then_inc(scored.sem, 1)

                def turn():
                    for k in range(NT):
                        out = score_tile(3 - k)
                        for i in range(k, NT):
                            last = nc.tensor.transpose(out[:, (i - k) * P:(i - k + 1) * P],
                                                       prob_tile(i)[:, k * P:(k + 1) * P], m.ident[:])
                        if k != 2:
                            last.then_inc(turned.sem, 1)

                def add_head(par):
                    for t in range(NT):
                        last = exact_product(nc, m.acc_tile(t), [a[:, t * P:(t + 1) * P] for a in (yT, yT_low)],
                                             [a[:, QKV:] for a in parts[par]], False, False, skip_group_check=True)
                    last.then_inc(added.sem, 1)

                def attend(h, par):
                    for k in range(NT):
                        if k < 3:
                            pe.wait_ge(probsT_ready.sem, probsT_ready.at(3 * h + k + 1))
                            if not rotary:
                                pe.wait_ge(probsT_low.sem, probsT_low.at(3 * h + k + 1))
                        if rotary:
                            last = nc.tensor.matmul(v_psum[:, k * P:T], v[par][:, k], turned_tile(k),
                                                    start=k == 0, stop=k == NT - 1)
                        else:
                            last = exact_product(nc, v_psum[:, k * P:T], [v[par][:, k], v_lows[par][:, k]],
                                                 [turned_tile(k), turned_tile(k, probsT_lows)], k == 0, k == NT - 1)
                    last.then_inc(attended.sem, 1)

                def step(h, par, first=False, final=False):
                    pe.wait_ge(qk_ready.sem, qk_ready.at(h + 1))
                    if rotary:
                        pe.wait_ge(qk_rest_ready.sem, qk_rest_ready.at(h + 1))
                    if not first:
                        pe.wait_ge(probsT_ready.sem, probsT_ready.at(3 * h))
                        if not rotary:
                            pe.wait_ge(probsT_low.sem, probsT_low.at(3 * h))
                    score()
                    if not final:
                        project(h + 1, 1 - par)
                    if first:
                        pe.wait_ge(v_ready.sem, v_ready.at(1))
                        if not rotary:
                            pe.wait_ge(v_low.sem, v_low.at(1))
                    else:
                        pe.wait_ge(y_ready.sem, y_ready.at(h))
                        pe.wait_ge(y_low.sem, y_low.at(h))
                    if not final:
                        project_v(1 - par)
                    pe.wait_ge(probs_ready.sem, probs_ready.at(h + 1))
                    turn()
                    if not first:
                        pe.wait_ge(wo_split.sem, wo_split.at(h))
                        add_head(1 - par)
                    pe.wait_ge(v_ready.sem, v_ready.at(h + (1 if final else 2)))
                    if not rotary:
                        pe.wait_ge(v_low.sem, v_low.at(h + (1 if final else 2)))
                    attend(h, par)

                pe.sem_inc(added.sem, 1)
                seed = m.bo_row[:].rearrange("o a d -> o (a d)") if not rotary else m.zero_row[:]
                for h in range(2):
                    nc.tensor.matmul(m.acc[:, h, :], m.one_row[:], seed, start=True, stop=False,
                                     skip_group_check=True)
                project(0, 0)
                project_v(0)
                step(0, 0, first=True)
                with pe.Fori(0, HEADS // 2 - 1) as i:
                    step(2 * i + 1, 1)
                    step(2 * i + 2, 0)
                step(HEADS - 1, 1, final=True)
                pe.wait_ge(y_ready.sem, y_ready.at(HEADS))
                pe.wait_ge(y_low.sem, y_low.at(HEADS))
                pe.wait_ge(wo_split.sem, wo_split.at(HEADS))
                add_head(1)

            @block.vector
            def _(dve):
                def spread_qk(h, par, at):
                    if not rotary:
                        for which in range(2):
                            dve.wait_ge(qk_high.sem, qk_high.at(2 * h + which + 1))
                            last = nc.vector.scalar_tensor_tensor(
                                qkT_low[:, which], qk_psum[:, which], bias_of(h, which),
                                qkT[:, which].bitcast(FP32), ALU.add, ALU.subtract)
                        last.then_inc(qk_ready.sem, 1)
                        dve.wait_ge(v_ready.sem, v_ready.at(h + 1))
                        flat = lambda a: a[:].rearrange("p t c -> p (t c)")
                        nc.vector.tensor_tensor(flat(v_lows[par]), v_psum, flat(v[par]).bitcast(FP32), ALU.subtract)\
                          .then_inc(v_low.sem, 1)
                        return
                    dve.wait_ge(qk_projected.sem, qk_projected.at(h + 1))
                    chain = Chain(dve, dve_chain, at)
                    sin = lambda a: rope_sin[a:a + 32].unsqueeze(1).broadcast_to([32, 2, T])
                    chain.link(nc.vector.tensor_tensor(rot[0:32, 0], qk_psum[32:64], sin(32), ALU.mult))
                    chain.link(nc.vector.tensor_tensor(rot[32:64, 0], qk_psum[0:32], sin(0), ALU.mult))
                    cos = rope_cos[:].unsqueeze(1).broadcast_to([64, 2, T])
                    chain.link(nc.vector.tensor_tensor(rot[:, 1], qk_psum[0:64], cos, ALU.mult))
                    chain.wait()
                    nc.vector.tensor_tensor(qkT[0:64], rot[:, 0], rot[:, 1], ALU.add).then_inc(qk_ready.sem, 1)

                def softmax(h, at):
                    chain = Chain(dve, dve_chain, at)
                    for n, i in enumerate((3, 2, 1, 0)):
                        if n < 3:
                            dve.wait_ge(scored.sem, scored.at(3 * h + n + 1))
                        chain.link(nc.vector.reduce_max(row_max[:, i:i + 1], score_tile(i), AXIS.X))
                    chain.wait()
                    nc.vector.tensor_scalar(neg_max[:], row_max[:], -QK_SCALE, None, ALU.mult)\
                      .then_inc(max_ready.sem, 1)
                    dve.wait_ge(exp_ready.sem, exp_ready.at(h + 1))
                    chain.all(nc.vector.reciprocal(row_inv[:], row_sum[:]))
                    for i in (3, 2, 1, 0):
                        last = nc.vector.tensor_scalar(prob_tile(i), prob_tile(i), row_inv[:, i:i + 1], None,
                                                       ALU.mult)
                    last.then_inc(probs_ready.sem, 1)

                def store_low(h):
                    if not rotary:
                        for k, (at, cols) in enumerate(TURNED_BANKS):
                            dve.wait_ge(probsT_ready.sem, probsT_ready.at(3 * h + k + 1))
                            nc.vector.tensor_tensor(probsT_lows[:, at:at + cols], m.banks[:, k, 0:cols],
                                                    probsT[:, at:at + cols].bitcast(FP32), ALU.subtract)\
                              .then_inc(probsT_low.sem, 1)
                    dve.wait_ge(y_ready.sem, y_ready.at(h + 1))
                    if rotary:
                        last = nc.vector.scalar_tensor_tensor(yT_low[:], v_psum, 1.0 / 3.0, yT[:].bitcast(FP32),
                                                              ALU.mult, ALU.subtract)
                    else:
                        last = nc.vector.scalar_tensor_tensor(yT_low[:], v_psum, bias_of(h, 2), yT[:].bitcast(FP32),
                                                              ALU.add, ALU.subtract)
                    last.then_inc(y_low.sem, 1)

                per = CHAIN_QK + CHAIN_SOFTMAX
                dve.wait_ge(rope_loaded.sem, rope_loaded.at(32 if rotary else 16))
                spread_qk(0, 0, 0)
                with dve.Fori(0, HEADS // 2 - 1) as i:
                    for par in range(2):
                        h = 2 * i + par
                        at = CHAIN_QK + per * h
                        softmax(h, at)
                        spread_qk(h + 1, 1 - par, at + CHAIN_SOFTMAX)
                        store_low(h)
                softmax(HEADS - 2, CHAIN_QK + per * (HEADS - 2))
                spread_qk(HEADS - 1, 1, CHAIN_QK + per * (HEADS - 2) + CHAIN_SOFTMAX)
                store_low(HEADS - 2)
                softmax(HEADS - 1, CHAIN_QK + per * (HEADS - 1))
                store_low(HEADS - 1)

            @block.scalar
            def _(act):
                def spread_rest(h, par):
                    if rotary:
                        act.wait_ge(qk_projected.sem, qk_projected.at(h + 1))
                        nc.scalar.activation(qkT[64:P], qk_psum[64:P], ACT.Copy).then_inc(qk_rest_ready.sem, 1)
                    else:
                        act.wait_ge(qk_projected.sem, qk_projected.at(h + 1))
                        for which in range(2):
                            nc.scalar.activation(qkT[:, which], qk_psum[:, which], ACT.Identity,
                                                 bias=bias_of(h, which)).then_inc(qk_high.sem, 1)
                    act.wait_ge(v_projected.sem, v_projected.at(h + 1))
                    nc.scalar.activation(v[par][:].rearrange("p t c -> p (t c)"), v_psum, ACT.Copy)\
                      .then_inc(v_ready.sem, 1)

                def exponentials(h):
                    act.wait_ge(max_ready.sem, max_ready.at(h + 1))
                    for i in (3, 2, 1, 0):
                        last = nc.scalar.activation(prob_tile(i), score_tile(i), ACT.Exp, bias=neg_max[:, i:i + 1],
                                                    scale=QK_SCALE, accum_out=row_sum[:, i:i + 1])
                    last.then_inc(exp_ready.sem, 1)

                def store_turned(h):
                    for k, (at, cols) in enumerate(TURNED_BANKS):
                        act.wait_ge(turned.sem, turned.at(3 * h + k + 1))
                        nc.scalar.activation(probsT[:, at:at + cols], m.banks[:, k, 0:cols], ACT.Copy)\
                          .then_inc(probsT_ready.sem, 1)

                def store_y(h):
                    act.wait_ge(attended.sem, attended.at(h + 1))
                    if rotary:
                        nc.scalar.activation(yT[:], v_psum, ACT.Copy, scale=1.0 / 3.0).then_inc(y_ready.sem, 1)
                    else:
                        nc.scalar.activation(yT[:], v_psum, ACT.Identity, bias=bias_of(h, 2)).then_inc(y_ready.sem, 1)

                def high_qkv(h, par, use):
                    act.wait_ge(loaded[par].sem, loaded[par].at(16 * use))
                    nc.scalar.activation(parts[par][0][:, 0:QKV], raw[par][:, 0:QKV], ACT.Copy)\
                      .then_inc(qkv_high.sem, 1)

                def high_wo(h, par):
                    act.wait_ge(added.sem, added.at(h))
                    nc.scalar.activation(parts[par][0][:, QKV:], raw[par][:, QKV:], ACT.Copy).then_inc(wo_high.sem, 1)

                def head(h, par, use=None):
                    exponentials(h)
                    spread_rest(h + 1, 1 - par)
                    store_turned(h)
                    if use is not None:
                        high_qkv(h + 2, par, use)
                    store_y(h)
                    high_wo(h + 1, 1 - par)

                high_qkv(0, 0, 1)
                nc.scalar.activation(parts[0][0][:, QKV:], raw[0][:, QKV:], ACT.Copy).then_inc(wo_high.sem, 1)
                high_qkv(1, 1, 1)
                if not rotary:
                    act.wait_ge(rope_loaded.sem, rope_loaded.at(16))
                spread_rest(0, 0)
                with act.Fori(0, HEADS // 2 - 1) as i:
                    for par in range(2):
                        head(2 * i + par, par, i + 2)
                head(HEADS - 2, 0)
                exponentials(HEADS - 1)
                store_turned(HEADS - 1)
                store_y(HEADS - 1)

            @block.gpsimd
            def _(pool):
                def low(columns, high, split, h, par):
                    pool.wait_ge(high.sem, high.at(h + 1))
                    nc.gpsimd.tensor_tensor(parts[par][1][:, columns], raw[par][:, columns],
                                            parts[par][0][:, columns].bitcast(FP32), ALU.subtract)                      .then_inc(split.sem, 1)

                low_qkv = lambda h, par: low(slice(0, QKV), qkv_high, qkv_split, h, par)
                low_wo = lambda h, par: low(slice(QKV, QKV + D), wo_high, wo_split, h, par)

                def lows(h, par):
                    low_qkv(h + 2, par)
                    low_wo(h + 1, 1 - par)

                low_qkv(0, 0)
                low_wo(0, 0)
                low_qkv(1, 1)
                if spline:
                    spline.make(pool, lambda h: lows(h, h % 2) if h < HEADS - 2 else None)
                else:
                    with pool.Fori(0, HEADS // 2 - 1) as i:
                        for par in range(2):
                            lows(2 * i + par, par)
                low_wo(HEADS - 1, 1)

        for s, n in ((qk_projected, HEADS), (v_projected, HEADS), (scored, 3 * HEADS), (turned, 3 * HEADS),
                     (attended, HEADS), (added, HEADS + 1), (qk_ready, HEADS), (max_ready, HEADS), (exp_ready, HEADS),
                     (probs_ready, HEADS), (v_ready, HEADS), (probsT_ready, 3 * HEADS), (y_ready, HEADS),
                     (dve_chain, HEADS * (CHAIN_QK + CHAIN_SOFTMAX))):
            s.close(n)
        for s in (qkv_high, qkv_split, wo_high, wo_split, y_low):
            s.close(HEADS)
        if rotary:
            qk_rest_ready.close(HEADS)
            rope_loaded.close(32)
        else:
            rope_loaded.close(16)
            qk_high.close(2 * HEADS)
            v_low.close(HEADS)
            probsT_low.close(3 * HEADS)
        for s in loaded:
            s.close(16 * HEADS // 2)


def head_rows(dram, h):
    return dram[bass.ds(h, 1)].rearrange("a p f -> (a p) f")


class Hidden:

    def __init__(self, groups, cols, rows, experts, act):
        self.groups, self.cols, self.rows, self.experts, self.act = groups, cols, rows, experts, act
        self.one_bank = 2 * cols <= 512


def gated_mlp_engines(m, shape, sb, first_bank, gate_up, down, scale_of, split):
    nc = m.nc
    gate_done, gated, hidden_ready = m.sig("gate_up_done"), m.sig("gated"), m.sig("hidden_ready")
    hidden_turned, hiddenT_ready, added = m.sig("hidden_turned"), m.sig("hiddenT_ready"), m.sig("group_added")
    F, R = shape.cols, len(shape.rows)
    act_out = [sb(f"act_out{i}", [P, F]) for i in range(2)]
    hidden = [sb(f"hidden{i}", [P, F]) for i in range(2)]
    hiddenT = [sb(f"hiddenT{i}", [P, R, P], FP32R if split else FP32) for i in range(2)]
    hiddenT_low = [sb(f"hiddenT_low{i}", [P, R, P], FP32R) for i in range(2)] if split else None
    low_ready = m.sig("hiddenT_low_ready")
    per_item = 1 if shape.one_bank else 2
    m.last_mlp = act_out, hidden

    def gate_up_psum(par):
        if shape.one_bank:
            b = m.banks[:, first_bank + par, :]
            return b[:, 0:F], b[:, F:2 * F], b[:, 0:2 * F].rearrange("p (w f) -> p w f", w=2)
        b = first_bank + 2 * par
        return m.banks[:, b, 0:F], m.banks[:, b + 1, 0:F], None

    def turned_psum(par):
        return m.banks[:, first_bank + 2 * per_item + par, 0:R * P].rearrange("p (r c) -> p r c", r=R)

    def multiply(t, par, gpar):
        gate, up, both = gate_up_psum(par)
        if split:
            outs = [both] if both is not None else [gate, up]
            for w, out in enumerate(outs):
                for k in range(KD):
                    left = [part[:, k, t * P:(t + 1) * P] for part in m.xnT_parts]
                    right = [part if both is not None else part[:, w] for part in gate_up(gpar, k)]
                    last = exact_product(nc, out, left, right, k == 0, k == KD - 1)
            last.then_inc(gate_done.sem, 1)
            return
        if both is not None:
            for k in range(KD):
                last = nc.tensor.matmul(both, m.xnT[:, k, t * P:(t + 1) * P], gate_up(gpar, k),
                                        start=k == 0, stop=k == KD - 1)
        else:
            for w, out in enumerate((gate, up)):
                for k in range(KD):
                    last = nc.tensor.matmul(out, m.xnT[:, k, t * P:(t + 1) * P], gate_up(gpar, k)[:, w],
                                            start=k == 0, stop=k == KD - 1)
        last.then_inc(gate_done.sem, 1)

    def turn(pe, n, par):
        pe.wait_ge(hidden_ready.sem, hidden_ready.at(n + 1))
        for r, rows in enumerate(shape.rows):
            last = nc.tensor.transpose(turned_psum(par)[0:rows, r], hidden[par][:, r * P:r * P + rows], m.ident[:])
        last.then_inc(hidden_turned.sem, 1)

    def add(pe, n, t, par, gpar):
        pe.wait_ge(hiddenT_ready.sem, hiddenT_ready.at(n + 1))
        if split:
            pe.wait_ge(low_ready.sem, low_ready.at(n + 1))
            for r, rows in enumerate(shape.rows):
                left = [hiddenT[par][0:rows, r], hiddenT_low[par][0:rows, r]]
                last = exact_product(nc, m.acc_tile(t), left, [part[0:rows] for part in down(gpar, r)],
                                     False, False, skip_group_check=True)
            last.then_inc(added.sem, 1)
            return
        for r, rows in enumerate(shape.rows):
            last = nc.tensor.matmul(m.acc_tile(t), hiddenT[par][0:rows, r], down(gpar, r)[0:rows],
                                    start=False, stop=False, skip_group_check=True)
        last.then_inc(added.sem, 1)

    def activate(act, n, par):
        act.wait_ge(gate_done.sem, gate_done.at(n + 1))
        nc.scalar.activation(act_out[par][:], gate_up_psum(par)[0], shape.act).then_inc(gated.sem, 1)

    def store_turned(act, n, par):
        act.wait_ge(hidden_turned.sem, hidden_turned.at(n + 1))
        whole = sum(r == P for r in shape.rows)
        last = nc.scalar.activation(hiddenT[par][:, 0:whole], turned_psum(par)[:, 0:whole], ACT.Copy)
        if whole < R:
            rows = shape.rows[-1]
            last = nc.scalar.activation(hiddenT[par][0:rows, whole], turned_psum(par)[0:rows, whole], ACT.Copy)
        last.then_inc(hiddenT_ready.sem, 1)

    def store_low(dve, n, par):
        dve.wait_ge(hiddenT_ready.sem, hiddenT_ready.at(n + 1))
        whole = sum(r == P for r in shape.rows)
        for rows, r in [(P, slice(0, whole))] + [(rows, slice(whole, R)) for rows in shape.rows[whole:]]:
            last = nc.vector.tensor_tensor(hiddenT_low[par][0:rows, r], turned_psum(par)[0:rows, r],
                                           hiddenT[par][0:rows, r].bitcast(FP32), ALU.subtract)
        last.then_inc(low_ready.sem, 1)

    def gate(dve, n, g, t, par):
        dve.wait_ge(gated.sem, gated.at(n + 1))
        up = gate_up_psum(par)[1]
        if scale_of is None:
            last = nc.vector.tensor_tensor(hidden[par][:], act_out[par][:], up, ALU.mult)
        else:
            cols = F // shape.experts
            for e in range(shape.experts):
                at = slice(e * cols, (e + 1) * cols)
                last = nc.vector.scalar_tensor_tensor(hidden[par][:, at], up[:, at], scale_of(g, t, e),
                                                      act_out[par][:, at], ALU.mult, ALU.mult)
        last.then_inc(hidden_ready.sem, 1)

    def close():
        n = NT * shape.groups
        for s in (gate_done, gated, hidden_ready, hidden_turned, hiddenT_ready, added):
            s.close(n)
        if split:
            low_ready.close(n)

    m.store_low = store_low
    return multiply, turn, add, activate, store_turned, gate, close, gate_done, added


def mixture(m, layer, with_table=False):
    nc = m.nc
    E, TOP = (E0, TOP0) if layer == 0 else (E3, TOP3)
    shape = Hidden(GROUPS, F0, (P, P, P), 4, ACT.Silu) if layer == 0 else Hidden(GROUPS, F3, (P, P), 1, ACT.Gelu)
    F, R = shape.cols, len(shape.rows)
    experts_dram, router_dram = m.dram[f"experts{layer}"], m.dram[f"router{layer}"]
    experts_loaded = [m.sig(f"experts_loaded{i}") for i in range(2)]
    gu_high, gu_split, down_high, down_split = (m.sig("gu_high"), m.sig("gu_split"), m.sig("down_high"),
                                                m.sig("down_split"))
    loaded, routed, logits_in, exp_in = m.sig("router_loaded"), m.sig("routed"), m.sig("logits_in"), m.sig("route_exp")
    stepped, rooted = m.sig("ln_var"), m.sig("ln_root")
    scaled_router, square_step = m.sig("scaled_router"), m.sig("square_step")
    dve_chain = m.sig("dve_chain")
    ITEMS = NT * GROUPS
    UNROLL = 2 * NT
    EP = E + 8 - TOP

    with ExitStack() as local_ctx:
        sb = m.local(local_ctx)
        GU = KD * 2 * F
        raw = [sb(f"experts{i}", [P, GU + R * D]) for i in range(2)]
        parts = [[sb(f"experts_{part}{i}", [P, GU + R * D], FP32R) for part in ("high", "low")] for i in range(2)]
        gu = [[a[:, 0:GU].rearrange("p (k w f) -> p k w f", k=KD, w=2) for a in pair] for pair in parts]
        dn = [[a[:, GU:].rearrange("p (r d) -> p r d", d=D) for a in pair] for pair in parts]
        router = sb("router", [P, KD, E])
        router_scale = sb("router_scale", [P, KD])
        per_expert = sb("per_expert", [P, E])
        logits, replaced = sb("logits", [P, NT, EP]), sb("replaced", [P, NT, EP])
        top = sb("top", [P, NT, 8])
        chosen, expd = sb("chosen", [P, NT, E]), sb("expd", [P, NT, E])
        weight = sb("weight", [P, NT, E])
        sums = sb("sums", [P, 4, NT])
        squares, square_sum = sb("squares", [P, D]), sb("square_sum", [P, NT])
        scale_of = lambda g, t, e: weight[:, t, bass.ds(g * shape.experts + e, 1)]
        multiply, turn, add, activate, store_turned, gate, close, gate_done, added = gated_mlp_engines(
            m, shape, sb, 0, lambda gpar, k: [a[:, k] for a in gu[gpar]], lambda gpar, r: [a[:, r] for a in dn[gpar]],
            scale_of, True)
        store_low = m.store_low
        table = TableWeights(m, local_ctx) if with_table else None
        per_token = lambda a: a.unsqueeze(2).broadcast_to([P, NT, E])
        n_loads = 1 if layer == 0 else 3

        with nc.Block() as block:
            @block.sync
            def _(sp):
                def load(g, gpar):
                    sp.dma_start(raw[gpar][:], head_rows(experts_dram, g)).then_inc(experts_loaded[gpar].sem, 16)

                sp.dma_start(router[:], router_dram).then_inc(loaded.sem, 16)
                if layer == 3:
                    sp.dma_start(router_scale[:], m.dram["router_scale"]).then_inc(loaded.sem, 16)
                    sp.dma_start(per_expert[:], m.dram["per_expert"].broadcast_to([P, E])).then_inc(loaded.sem, 16)
                if table:
                    table.start(sp)
                for g in range(2):
                    load(g, g)
                    if table:
                        table.load(sp, g, g)
                with sp.Fori(0, GROUPS // 2 - 1) as i:
                    for gpar in range(2):
                        g = 2 * i + gpar
                        sp.wait_ge(gu_split.sem, gu_split.at(g + 1))
                        sp.wait_ge(down_split.sem, down_split.at(g + 1))
                        load(g + 2, gpar)
                        if table:
                            sp.wait_ge(table.read.sem, table.read.at(g + 1))
                            table.load(sp, g + 2, gpar)

            @block.tensor
            def _(pe):
                pe.sem_inc(added.sem, 1)
                if layer == 0:
                    pe.wait_ge(loaded.sem, loaded.at(16))
                else:
                    pe.wait_ge(scaled_router.sem, scaled_router.at(1))
                for t in range(NT):
                    for k in range(KD):
                        last = nc.tensor.matmul(m.banks[:, 5, t * E:(t + 1) * E], m.xnT[:, k, t * P:(t + 1) * P],
                                                router[:, k], start=k == 0, stop=k == KD - 1)
                last.then_inc(routed.sem, 1)

                def step(n, c, pair):
                    if c < UNROLL:
                        gpar, t, nxt = c // NT, c % NT, (c + 1) % UNROLL
                    if n is not None and not (isinstance(n, int) and n == ITEMS - 1):
                        if nxt % NT == 0:
                            pe.wait_ge(gu_split.sem, gu_split.at(2 * pair + (3 if nxt == 0 else 2)))
                        multiply(nxt % NT, nxt % 2, nxt // NT)
                    turn(pe, n, c % 2)
                    if not (isinstance(n, int) and n == 0):
                        prev = (c - 1) % UNROLL
                        if prev % NT == 0:
                            pe.wait_ge(down_split.sem, down_split.at(2 * pair + 1 + prev // NT))
                        add(pe, n - 1, prev % NT, prev % 2, prev // NT)

                pe.wait_ge(gu_split.sem, gu_split.at(1))
                multiply(0, 0, 0)
                step(0, 0, 0)
                with pe.Fori(0, GROUPS // 2 - 1) as i:
                    for c in range(1, UNROLL + 1):
                        step(UNROLL * i + c, c % UNROLL, i + c // UNROLL)
                for n in range(ITEMS - UNROLL + 1, ITEMS):
                    step(n, n % UNROLL, n // UNROLL)
                add(pe, ITEMS - 1, NT - 1, 1, 1)

            @block.vector
            def _(dve):
                chain = Chain(dve, dve_chain)
                chain.link(nc.vector.memset(logits[:, :, E:], -3e38))
                dve.wait_ge(loaded.sem, loaded.at(16 * n_loads))
                if layer == 3:
                    for k in range(KD):
                        last = nc.vector.tensor_scalar(router[:, k], router[:, k], router_scale[:, k:k + 1],
                                                       float(D) ** -0.5, ALU.mult, ALU.mult)
                    last.then_inc(scaled_router.sem, 1)
                    dve.wait_ge(square_step.sem, square_step.at(NT))
                    nc.vector.tensor_scalar(m.rs[:, 0], square_sum[:], 1.0 / D, 1e-6, ALU.mult, ALU.add)\
                      .then_inc(stepped.sem, 1)
                    dve.wait_ge(stepped.sem, stepped.at(1))
                    dve.wait_ge(rooted.sem, rooted.at(1))
                    reciprocal_root(nc, chain, m.rs)
                dve.wait_ge(routed.sem, routed.at(1))
                src = m.banks[:, 5, 0:NT * E].rearrange("p (t e) -> p t e", t=NT)
                if layer == 0:
                    chain.all(nc.vector.tensor_copy(logits[:, :, 0:E], src))
                else:
                    chain.all(nc.vector.tensor_tensor(logits[:, :, 0:E], src, per_token(m.rs[:, 3]), ALU.mult))
                for t in range(NT):
                    chain.link(nc.vector.max(top[:, t], logits[:, t]))
                chain.wait()
                chain.link(nc.vector.tensor_tensor(expd[:], logits[:, :, 0:E],
                                                   top[:, :, 0:1].broadcast_to([P, NT, E]), ALU.subtract))
                chain.wait()
                chain.all(nc.vector.memset(top[:, :, TOP:], -3e38))
                for t in range(NT):
                    chain.link(nc.vector.match_replace(replaced[:, t], top[:, t], logits[:, t], 3e38))
                chain.wait()
                nc.vector.tensor_tensor(chosen[:], replaced[:, :, 0:E], logits[:, :, 0:E], ALU.not_equal)\
                  .then_inc(logits_in.sem, 1)
                dve.wait_ge(exp_in.sem, exp_in.at(1))
                dve.wait_ge(logits_in.sem, logits_in.at(1))
                if layer == 3:
                    chain.all(nc.vector.reduce_sum(sums[:, 0], expd[:], AXIS.X))
                    chain.all(nc.vector.reciprocal(sums[:, 1], sums[:, 0]))
                    chain.all(nc.vector.tensor_tensor(expd[:], expd[:], per_token(sums[:, 1]), ALU.mult))
                chain.all(nc.vector.tensor_tensor(chosen[:], chosen[:], expd[:], ALU.mult))
                chain.all(nc.vector.reduce_sum(sums[:, 0], chosen[:], AXIS.X))
                if layer == 3:
                    chain.all(nc.vector.tensor_scalar(sums[:, 0], sums[:, 0], 1e-12, None, ALU.max))
                chain.all(nc.vector.reciprocal(sums[:, 1], sums[:, 0]))
                chain.all(nc.vector.tensor_tensor(weight[:], chosen[:], per_token(sums[:, 1]), ALU.mult))
                if layer == 3:
                    chain.all(nc.vector.tensor_tensor(weight[:], weight[:],
                                                      per_expert[:].unsqueeze(1).broadcast_to([P, NT, E]), ALU.mult))
                if table:
                    table.first(dve)

                def step(n, c, pair):
                    nxt, nxt_pair = (c + 1) % UNROLL, pair + (c + 1) // UNROLL
                    if not (isinstance(n, int) and n == ITEMS - 1):
                        gate(dve, n + 1, 2 * nxt_pair + nxt // NT, nxt % NT, nxt % 2)
                    store_low(dve, n, c % 2)
                    if table:
                        table.part(dve, 2 * pair + c // NT, c // NT, pair, c % NT)

                gate(dve, 0, 0, 0, 0)
                with dve.Fori(0, GROUPS // 2 - 1) as i:
                    for c in range(UNROLL):
                        step(UNROLL * i + c, c, i)
                for n in range(ITEMS - UNROLL, ITEMS):
                    step(n, n % UNROLL, n // UNROLL)
                dve_chain.close(chain.n)

            @block.scalar
            def _(act):
                def high_gu(act, g, gpar, use):
                    act.wait_ge(experts_loaded[gpar].sem, experts_loaded[gpar].at(use))
                    nc.scalar.activation(parts[gpar][0][:, 0:GU], raw[gpar][:, 0:GU], ACT.Copy)\
                      .then_inc(gu_high.sem, 1)

                def high_down(act, g, gpar):
                    if not (isinstance(g, int) and g < 2):
                        act.wait_ge(added.sem, added.at(NT * (g - 1) + 1))
                    nc.scalar.activation(parts[gpar][0][:, GU:], raw[gpar][:, GU:], ACT.Copy)\
                      .then_inc(down_high.sem, 1)

                def step_act(n, c, pair, final=False):
                    if not (final and n == ITEMS - 1):
                        activate(act, n + 1, (c + 1) % 2)
                    store_turned(act, n, c % 2)
                    if c == 1:
                        high_down(act, 2 * pair + 1, 1)
                    if not final:
                        if c == 3:
                            high_gu(act, 2 * pair + 2, 0, 16 * (pair + 2))
                        if c == 5:
                            high_down(act, 2 * pair + 2, 0)
                        if c == 7:
                            high_gu(act, 2 * pair + 3, 1, 16 * (pair + 2))

                if layer == 3:
                    for t in range(NT):
                        last = nc.scalar.activation(squares[:], m.xn[:, t], ACT.Square,
                                                    accum_out=square_sum[:, t:t + 1])
                        last.then_inc(square_step.sem, 1)
                        act.wait_ge(square_step.sem, square_step.at(t + 1))
                    act.wait_ge(stepped.sem, stepped.at(1))
                    nc.scalar.activation(m.rs[:, 1], m.rs[:, 0], ACT.Sqrt).then_inc(rooted.sem, 1)
                act.wait_ge(logits_in.sem, logits_in.at(1))
                nc.scalar.activation(expd[:], expd[:], ACT.Exp).then_inc(exp_in.sem, 1)

                for g in range(2):
                    high_gu(act, g, g, 16)
                    if g == 0:
                        high_down(act, 0, 0)
                activate(act, 0, 0)
                with act.Fori(0, GROUPS // 2 - 1) as i:
                    for c in range(UNROLL):
                        step_act(UNROLL * i + c, c, i)
                for n in range(ITEMS - UNROLL, ITEMS):
                    step_act(n, n % UNROLL, n // UNROLL, final=True)

            @block.gpsimd
            def _(pool):
                def low(columns, high, split, g, gpar):
                    pool.wait_ge(high.sem, high.at(g + 1))
                    nc.gpsimd.tensor_tensor(parts[gpar][1][:, columns], raw[gpar][:, columns],
                                            parts[gpar][0][:, columns].bitcast(FP32), ALU.subtract)\
                      .then_inc(split.sem, 1)

                low_gu = lambda g, gpar: low(slice(0, GU), gu_high, gu_split, g, gpar)
                low_down = lambda g, gpar: low(slice(GU, GU + R * D), down_high, down_split, g, gpar)
                low_gu(0, 0)
                low_down(0, 0)
                low_gu(1, 1)
                with pool.Fori(0, GROUPS // 2 - 1) as i:
                    low_down(2 * i + 1, 1)
                    low_gu(2 * i + 2, 0)
                    low_down(2 * i + 2, 0)
                    low_gu(2 * i + 3, 1)
                low_down(GROUPS - 1, 1)

        close()
        added.close(1)
        if table:
            table.close()
        loaded.close(16 * n_loads)
        for s in (routed, logits_in, exp_in):
            s.close(1)
        if layer == 3:
            stepped.close(1)
            rooted.close(1)
            scaled_router.close(1)
            square_step.close(NT)
        for s in experts_loaded:
            s.close(16 * GROUPS // 2)
        for s in (gu_high, gu_split, down_high, down_split):
            s.close(GROUPS)


def state_space(m):
    nc, dram = m.nc, m.dram
    loaded, in_weights = m.sig("ss_loaded"), m.sig("ss_in_loaded")
    square_step, stepped, rooted = m.sig("square_step"), m.sig("ln_var"), m.sig("ln_root")
    scaled, turned, xmT_ready = m.sig("ln_normed"), m.sig("ln_turned"), m.sig("xmT_ready")
    projected, xs_ready, z_ready = m.sig("ss_projected"), m.sig("xs_ready"), m.sig("z_ready")
    conv_ready, u_ready = m.sig("conv_ready"), m.sig("u_ready")
    low_rank, dt_in, bc_split = m.sig("low_rank"), m.sig("dt_in"), m.sig("bc_split")
    spread, b_stored, c_stored = m.sig("bc_spread"), m.sig("b_stored"), m.sig("c_stored")
    dt_done, dt_parts = m.sig("dt_done"), m.sig("dt_parts")
    softplus_step, delta_ready = m.sig("softplus_step"), m.sig("delta_ready")
    decay_ready, scanned, product_ready, summed = (m.sig("decay_ready"), m.sig("scanned"), m.sig("product_ready"),
                                                   m.sig("summed"))
    y_taken, gated_y, joined = m.sig("y_taken"), m.sig("gated_y"), m.sig("joined")
    dve_chain = m.sig("dve_chain")
    shape = Hidden(KC, D, (P, P), 1, ACT.Tanh)
    DECAYS, INFLOWS, PRODUCTS = 4, 4, 2
    MULTIPLY, GATE, TURN, ADD = (0, 3, 6, 9), (3, 6, 9, 12), (4, 7, 10, 13), (6, 9, 12, 15)
    TANH, STORE = (5, 8, 11, 14), (8, 11, 14, 15)
    CHAIN_TILE = NT
    inflow_ready = m.sig("inflow_ready")

    with ExitStack() as local_ctx:
        sb = m.local(local_ctx)
        xp = sb("xp", [P, KC, T + TAPS - 1])
        u, silu_z, delta = sb("u", [P, KC, T]), sb("silu_z", [P, KC, T]), sb("delta", [P, KC, T])
        Bs, Cs = sb("Bs", [P, NS, T]), sb("Cs", [P, NS, T])
        rings = sb("rings", [P, DECAYS + INFLOWS + PRODUCTS, T])
        decay, inflow, product = rings[:, 0:DECAYS], rings[:, DECAYS:DECAYS + INFLOWS], rings[:, DECAYS + INFLOWS:]
        state = sb("state", [P, 2, T])
        yg, carrier = sb("yg", [P, T]), sb("carrier", [P, NS])
        w_out = sb("w_out", [P, KC, D])
        split = sb("split", [3 * 2 * NS, T], BF16)
        mid = sb("mid", [2 * NS, T], BF16)
        vec = sb("vec", [P, KC, 7])
        w_norm, A = sb("w_norm", [P, KD]), sb("A", [P, KC, NS])
        square_sum = sb("square_sum", [P, NT])
        blended = [sb(f"blended{i}", [P, D]) for i in range(2)]
        xm = decay[:, 0:2].rearrange("p a t -> p (a t)").rearrange("p (t d) -> p t d", t=NT)
        xmT, rank_in = decay[:, 2:4], yg
        w_xp = product.rearrange("p a t -> p (a t)")[:, 0:KC * (RANK + 2 * NS)]
        w_xp, w_dt = w_xp.rearrange("p (k c) -> p k c", k=KC), Bs[:, NS - 1]
        squares, rest = state[:, 0, 0:D], state[0:2 * NS, 1]
        select = inflow[0:6 * NS].rearrange("p a t -> p (a t)").bitcast(BF16).rearrange("p (r c) -> p r c", c=P)
        w_in = Cs[:, NS - 4:].rearrange("p a t -> p (a t)").rearrange("p (k c) -> p k c", k=KD)
        du = xp[:, :, 0:T]
        multiply, turn, add, activate, store_turned, _, close, gate_done, _ = gated_mlp_engines(
            m, shape, sb, 0, lambda g, k: m.spline_gu[:, k, :, bass.ds(g * D, D)],
            lambda g, r: m.spline_down[:, bass.ds(2 * g + r, 1), :].rearrange("p a d -> p (a d)"), None, False)
        gated, hidden_ready = m.sig("gated"), m.sig("hidden_ready")
        act_out, hidden = m.last_mlp
        y_psum = m.banks[:, 4, :]
        loads = [(w_xp, dram["w_xp"]), (w_dt, dram["w_dt"]), (w_out[:], dram["w_out"]),
                 (select, dram["select"]), (vec[:], dram["ss_vec"]), (w_norm[:], dram["w_norm"]),
                 (A[:], dram["a_log"])]

        with nc.Block() as block:
            @block.sync
            def _(sp):
                sp.dma_start(w_in, dram["w_in"]).then_inc(in_weights.sem, 16)
                for dst, src in loads:
                    sp.dma_start(dst, src).then_inc(loaded.sem, 16)

            @block.tensor
            def _(pe):
                for k in range(KD):
                    for t in range(NT):
                        pe.wait_ge(scaled.sem, scaled.at(t + 1))
                        last = nc.tensor.transpose(m.banks[:, k, t * P:(t + 1) * P], xm[:, t, k * P:(k + 1) * P],
                                                   m.ident[:])
                    last.then_inc(turned.sem, 1)
                pe.wait_ge(in_weights.sem, in_weights.at(16))
                pe.wait_ge(xmT_ready.sem, xmT_ready.at(KD))
                for c in range(2 * KC):
                    if c >= 2:
                        if c - 2 < KC:
                            pe.wait_ge(xs_ready.sem, xs_ready.at(c - 1))
                        else:
                            pe.wait_ge(z_ready.sem, z_ready.at(c - 1 - KC))
                    for k in range(KD):
                        last = nc.tensor.matmul(m.banks[:, 4 + c % 2, :], w_in[:, k, c * P:(c + 1) * P], xmT[:, k],
                                                start=k == 0, stop=k == KD - 1)
                    last.then_inc(projected.sem, 1)
                pe.wait_ge(loaded.sem, loaded.at(16 * len(loads)))
                for k in range(KC):
                    pe.wait_ge(u_ready.sem, u_ready.at(k + 1))
                    nc.tensor.matmul(m.banks[:, 0, :], w_xp[:, k, 0:RANK], u[:, k], start=k == 0, stop=k == KC - 1)
                    last = nc.tensor.matmul(m.banks[0:2 * NS, 1, :], w_xp[:, k, RANK:], u[:, k],
                                            start=k == 0, stop=k == KC - 1)
                last.then_inc(low_rank.sem, 1)
                pe.wait_ge(dt_in.sem, dt_in.at(1))
                pe.wait_ge(z_ready.sem, z_ready.at(KC))
                for c in range(KC):
                    if c >= 2:
                        pe.wait_ge(dt_parts.sem, dt_parts.at(c - 1))
                    nc.tensor.matmul(m.banks[:, 4 + c % 2, :], w_dt[:, c * P:(c + 1) * P], rank_in[:],
                                     start=True, stop=True).then_inc(dt_done.sem, 1)
                pe.wait_ge(bc_split.sem, bc_split.at(1))
                for n in range(NS):
                    for which, stored in ((0, b_stored), (1, c_stored)):
                        if n >= 2:
                            pe.wait_ge(stored.sem, stored.at(n - 1))
                        nc.tensor.matmul(m.banks[:, 2 * which + n % 2, :], select[:, which * NS + n, :], split[:],
                                         start=True, stop=True).then_inc(spread.sem, 1)
                pe.wait_ge(b_stored.sem, b_stored.at(NS))
                pe.wait_ge(c_stored.sem, c_stored.at(NS))
                pe.wait_ge(dt_parts.sem, dt_parts.at(KC))
                pe.sem_inc(summed.sem, PRODUCTS)
                with pe.Fori(0, KC) as c:
                    pe.wait_ge(y_taken.sem, y_taken.at(c + 1))
                    for n in range(NS):
                        pe.wait_ge(product_ready.sem, product_ready.at(NS * c + n + 1))
                        nc.tensor.matmul(y_psum, m.ident[:], product[:, n % PRODUCTS], start=n == 0, stop=n == NS - 1)\
                          .then_inc(summed.sem, 1)
                        item = NT * c
                        if n in MULTIPLY:
                            t = MULTIPLY.index(n)
                            multiply(t, t % 2, c)
                        if n in TURN:
                            t = TURN.index(n)
                            turn(pe, item + t, t % 2)
                        if n in ADD:
                            t = ADD.index(n)
                            add(pe, item + t, t, t % 2, c)
                    pe.wait_ge(gated_y.sem, gated_y.at(c + 1))
                    for t in range(NT):
                        last = nc.tensor.matmul(m.acc_tile(t), yg[:, t * P:(t + 1) * P],
                                                w_out[:, bass.ds(c, 1), :].rearrange("p a d -> p (a d)"),
                                                start=False, stop=False, skip_group_check=True)
                    last.then_inc(joined.sem, 1)

            @block.scalar
            def _(act):
                for t in range(NT):
                    nc.scalar.activation(squares, m.xn[:, t], ACT.Square, accum_out=square_sum[:, t:t + 1])\
                      .then_inc(square_step.sem, 1)
                    act.wait_ge(square_step.sem, square_step.at(t + 1))
                act.wait_ge(stepped.sem, stepped.at(1))
                nc.scalar.activation(m.rs[:, 1], m.rs[:, 0], ACT.Sqrt).then_inc(rooted.sem, 1)
                act.wait_ge(loaded.sem, loaded.at(16 * len(loads)))
                for k in range(KD):
                    act.wait_ge(turned.sem, turned.at(k + 1))
                    nc.scalar.activation(xmT[:, k], m.banks[:, k, :], ACT.Copy, scale=w_norm[:, k:k + 1])\
                      .then_inc(xmT_ready.sem, 1)
                for c in range(KC):
                    act.wait_ge(projected.sem, projected.at(c + 1))
                    nc.scalar.activation(xp[:, c, TAPS - 1:], m.banks[:, 4 + c % 2, :], ACT.Copy)\
                      .then_inc(xs_ready.sem, 1)
                for c in range(KC):
                    act.wait_ge(projected.sem, projected.at(KC + c + 1))
                    nc.scalar.activation(silu_z[:, c], m.banks[:, 4 + c % 2, :], ACT.Silu).then_inc(z_ready.sem, 1)
                for c in range(KC):
                    act.wait_ge(conv_ready.sem, conv_ready.at(c + 1))
                    nc.scalar.activation(u[:, c], delta[:, c], ACT.Silu).then_inc(u_ready.sem, 1)
                act.wait_ge(low_rank.sem, low_rank.at(1))
                nc.scalar.activation(rank_in[:], m.banks[:, 0, :], ACT.Copy).then_inc(dt_in.sem, 1)
                for c in range(KC):
                    act.wait_ge(dt_done.sem, dt_done.at(c + 1))
                    v = m.banks[:, 4 + c % 2, :]
                    nc.scalar.activation(delta[:, c], v, ACT.Relu, bias=vec[:, c, 5:6])
                    nc.scalar.activation(du[:, c], v, ACT.Abs, bias=vec[:, c, 5:6]).then_inc(dt_parts.sem, 1)
                act.wait_ge(dt_parts.sem, dt_parts.at(KC))
                nc.scalar.activation(du, du, ACT.Exp, scale=-1.0).then_inc(softplus_step.sem, 1)
                nc.scalar.activation(A[:], A[:], ACT.Exp).then_inc(softplus_step.sem, 1)
                act.wait_ge(softplus_step.sem, softplus_step.at(2))
                nc.scalar.activation(du, du, ACT.Ln, bias=1.0).then_inc(softplus_step.sem, 1)
                for n in range(NS):
                    act.wait_ge(spread.sem, spread.at(2 * n + 1))
                    nc.scalar.activation(Bs[:, n], m.banks[:, n % 2, :], ACT.Copy).then_inc(b_stored.sem, 1)
                act.wait_ge(delta_ready.sem, delta_ready.at(1))
                with act.Fori(0, KC) as c:
                    for n in range(NS):
                        act.wait_ge(scanned.sem, scanned.at(NS * c + n + 1))
                        nc.scalar.activation(decay[:, n % DECAYS],
                                             delta[:, bass.ds(c, 1), :].rearrange("p a t -> p (a t)"), ACT.Exp,
                                             scale=A[:, bass.ds(c, 1), n:n + 1].rearrange("p a n -> p (a n)"))\
                          .then_inc(decay_ready.sem, 1)
                        if n in TANH:
                            t = TANH.index(n)
                            act.wait_ge(gate_done.sem, gate_done.at(NT * c + t + 1))
                            nc.scalar.activation(act_out[t % 2][:], m.banks[:, t % 2, 0:D], ACT.Tanh, scale=0.5)\
                              .then_inc(gated.sem, 1)
                        if n in STORE:
                            t = STORE.index(n)
                            store_turned(act, NT * c + t, t % 2)

            @block.vector
            def _(dve):
                chain = Chain(dve, dve_chain)
                dve.wait_ge(square_step.sem, square_step.at(NT))
                nc.vector.tensor_scalar(m.rs[:, 0], square_sum[:], 1.0 / D, 1e-5, ALU.mult, ALU.add)\
                  .then_inc(stepped.sem, 1)
                dve.wait_ge(stepped.sem, stepped.at(1))
                dve.wait_ge(rooted.sem, rooted.at(1))
                reciprocal_root(nc, chain, m.rs)
                for t in range(NT):
                    nc.vector.tensor_scalar(xm[:, t], m.xn[:, t], m.rs[:, 3, t:t + 1], None, ALU.mult)\
                      .then_inc(scaled.sem, 1)
                dve.wait_ge(loaded.sem, loaded.at(16 * len(loads)))
                chain.all(nc.vector.memset(xp[:, :, 0:TAPS - 1], 0.0))
                conv = delta
                for c in range(KC):
                    dve.wait_ge(xs_ready.sem, xs_ready.at(c + 1))
                    chain.all(nc.vector.tensor_scalar(conv[:, c], xp[:, c, 0:T], vec[:, c, 0:1], vec[:, c, 4:5],
                                                      ALU.mult, ALU.add))
                    for j in range(1, TAPS):
                        last = nc.vector.scalar_tensor_tensor(conv[:, c], xp[:, c, j:j + T], vec[:, c, j:j + 1],
                                                              conv[:, c], ALU.mult, ALU.add)
                        if j < TAPS - 1:
                            chain.all(last)
                    last.then_inc(conv_ready.sem, 1)
                dve.wait_ge(low_rank.sem, low_rank.at(1))
                bc = m.banks[0:2 * NS, 1, :]
                chain.all(nc.vector.tensor_copy(split[0:2 * NS], bc))
                chain.all(nc.vector.tensor_tensor(rest, bc, split[0:2 * NS], ALU.subtract))
                chain.all(nc.vector.tensor_copy(mid[:], rest))
                chain.link(nc.vector.tensor_copy(split[2 * NS:4 * NS], mid[:]))
                chain.link(nc.vector.tensor_tensor(split[4 * NS:6 * NS], rest, mid[:], ALU.subtract))
                chain.wait()
                nc.vector.memset(rest[:, 0:1], 0.0).then_inc(bc_split.sem, 1)
                dve.wait_ge(softplus_step.sem, softplus_step.at(3))
                chain.link(nc.vector.tensor_scalar(A[:], A[:], -1.0, None, ALU.mult))
                chain.all(nc.vector.tensor_tensor(delta[:], delta[:], du, ALU.add))
                chain.all(nc.vector.tensor_tensor(du, delta[:], u[:], ALU.mult))
                nc.vector.memset(rest[:, 0:1], 0.0).then_inc(delta_ready.sem, 1)
                for n in range(NS):
                    dve.wait_ge(spread.sem, spread.at(2 * n + 2))
                    nc.vector.tensor_copy(Cs[:, n], m.banks[:, 2 + n % 2, :]).then_inc(c_stored.sem, 1)
                dve.wait_ge(c_stored.sem, c_stored.at(NS))
                dve.wait_ge(b_stored.sem, b_stored.at(NS))
                dve.sem_inc(scanned.sem, DECAYS)
                dve.sem_inc(y_taken.sem, 1)
                ahead = chain.n
                with dve.Fori(0, KC) as c:
                    tile = Chain(dve, dve_chain, ahead + CHAIN_TILE * c)
                    row = lambda a: a[:, bass.ds(c, 1), :].rearrange("p a t -> p (a t)")
                    scalar = lambda j: vec[:, bass.ds(c, 1), j:j + 1].rearrange("p a n -> p (a n)")
                    for n in range(NS):
                        dve.wait_ge(inflow_ready.sem, inflow_ready.at(NS * c + n + 1))
                        dve.wait_ge(decay_ready.sem, decay_ready.at(NS * c + n + 1))
                        nc.vector.tensor_tensor_scan(state[:, n % 2], decay[:, n % DECAYS], inflow[:, n % INFLOWS], 0.0,
                                                     ALU.mult, ALU.add).then_inc(scanned.sem, 1)
                        dve.wait_ge(scanned.sem, scanned.at(NS * c + n + 1 + DECAYS))
                        dve.wait_ge(summed.sem, summed.at(NS * c + n + 1))
                        nc.vector.tensor_tensor(product[:, n % PRODUCTS], state[:, n % 2], Cs[:, n], ALU.mult)\
                          .then_inc(product_ready.sem, 1)
                        if n in GATE:
                            t = GATE.index(n)
                            dve.wait_ge(gated.sem, gated.at(NT * c + t + 1))
                            tile.all(nc.vector.scalar_tensor_tensor(blended[t % 2][:], act_out[t % 2][:], 1.0,
                                                                    m.banks[:, t % 2, D:2 * D], ALU.add, ALU.mult))
                            nc.vector.scalar_tensor_tensor(hidden[t % 2][:], blended[t % 2][:], 0.5,
                                                           m.banks[:, t % 2, 0:D], ALU.mult, ALU.mult)\
                              .then_inc(hidden_ready.sem, 1)
                    dve.wait_ge(summed.sem, summed.at(NS * c + NS + PRODUCTS))
                    nc.vector.scalar_tensor_tensor(yg[:], row(u), scalar(6), y_psum, ALU.mult, ALU.add)\
                      .then_inc(y_taken.sem, 1)
                    dve.wait_ge(y_taken.sem, y_taken.at(c + 2))
                    nc.vector.tensor_tensor(yg[:], yg[:], row(silu_z), ALU.mult).then_inc(gated_y.sem, 1)
                dve_chain.close(ahead + KC * CHAIN_TILE)

            @block.gpsimd
            def _(pool):
                pool.wait_ge(delta_ready.sem, delta_ready.at(1))
                pool.wait_ge(b_stored.sem, b_stored.at(NS))
                pool.wait_ge(c_stored.sem, c_stored.at(NS))
                with pool.Fori(0, KC) as c:
                    for n in range(NS):
                        pool.wait_ge(scanned.sem, scanned.at(NS * c + n + 1))
                        nc.gpsimd.tensor_tensor(carrier[:, n:n + 1], m.ident[:, 0:1], m.ident[:, 0:1], ALU.mult)
                        nc.gpsimd.tensor_tensor(inflow[:, n % INFLOWS],
                                                xp[:, bass.ds(c, 1), 0:T].rearrange("p a t -> p (a t)"),
                                                Bs[:, n], ALU.mult).then_inc(inflow_ready.sem, 1)

        inflow_ready.close(KC * NS)
        close()
        for s, n in ((in_weights, 16), (loaded, 16 * len(loads)), (square_step, NT), (stepped, 1), (rooted, 1),
                     (scaled, NT), (turned, KD), (xmT_ready, KD), (projected, 2 * KC), (xs_ready, KC),
                     (z_ready, KC), (conv_ready, KC), (u_ready, KC), (low_rank, 1), (dt_in, 1), (bc_split, 1),
                     (spread, 2 * NS), (b_stored, NS), (c_stored, NS), (dt_done, KC), (dt_parts, KC),
                     (softplus_step, 3), (delta_ready, 1), (decay_ready, KC * NS), (scanned, KC * NS + DECAYS),
                     (product_ready, KC * NS), (summed, KC * NS + PRODUCTS), (y_taken, KC + 1), (gated_y, KC),
                     (joined, KC)):
            s.close(n)


def clear_acc(m, pe):
    for h in range(2):
        m.nc.tensor.matmul(m.acc[:, h, :], m.one_row[:], m.zero_row[:], start=True, stop=False,
                           skip_group_check=True)


def linear_recurrence(m):
    nc, dram = m.nc, m.dram
    loaded, projected, h_ready, stepped = m.sig("lru_loaded"), m.sig("lru_projected"), m.sig("h_ready"), m.sig("lru_stepped")
    shape = Hidden(2, F2, F2_ROWS, 1, ACT.Silu)
    ITEMS = 2 * NT
    N2 = 2 * STATES
    STEPS = 9
    with ExitStack() as local_ctx:
        sb = m.local(local_ctx)
        w_b, w_c = sb("w_b", [P, KD, N2]), sb("w_c", [N2, D])
        h = sb("h", [N2, T])
        gu_w = m.lut_w[:, 0:KD * 2 * INTER2].rearrange("p (k w f) -> p k w f", k=KD, w=2)
        down_w = m.lut_w[:, KD * 2 * INTER2:].rearrange("p (r d) -> p r d", d=D)
        multiply, turn, add, activate, store_turned, gate, close, gate_done, _ = gated_mlp_engines(
            m, shape, sb, 0, lambda g, k: gu_w[:, k, :, g * F2:(g + 1) * F2],
            lambda g, r: down_w[:, 3 * g + r], None, False)
        lru_psum = m.banks[0:N2, 4 + 1, :]

        with nc.Block() as block:
            @block.sync
            def _(sp):
                sp.dma_start(w_b[:], dram["lru_b"]).then_inc(loaded.sem, 16)
                sp.dma_start(w_c[:], dram["lru_c"]).then_inc(loaded.sem, 16)

            @block.tensor
            def _(pe):
                clear_acc(m, pe)
                pe.wait_ge(loaded.sem, loaded.at(32))
                for k in range(KD):
                    last = nc.tensor.matmul(lru_psum, w_b[:, k], m.xnT[:, k], start=k == 0, stop=k == KD - 1)
                last.then_inc(projected.sem, 1)
                for s in range(STEPS):
                    pe.wait_ge(h_ready.sem, h_ready.at(s + 1))
                    shift = 1 << s
                    nc.tensor.matmul(lru_psum[:, shift:], m.lru_step[:, s], h[:, 0:T - shift], start=True, stop=True)\
                      .then_inc(stepped.sem, 1)
                pe.wait_ge(h_ready.sem, h_ready.at(STEPS + 1))
                for t in range(NT):
                    nc.tensor.matmul(m.acc_tile(t), h[:, t * P:(t + 1) * P], w_c[:], start=False, stop=False,
                                     skip_group_check=True)
                multiply(0, 0, 0)
                for n in range(ITEMS):
                    if n + 1 < ITEMS:
                        multiply((n + 1) % NT, (n + 1) % 2, (n + 1) // NT)
                    turn(pe, n, n % 2)
                    if n:
                        add(pe, n - 1, (n - 1) % NT, (n - 1) % 2, (n - 1) // NT)
                add(pe, ITEMS - 1, NT - 1, 1, 1)

            @block.vector
            def _(dve):
                dve.wait_ge(loaded.sem, loaded.at(32))
                dve.wait_ge(projected.sem, projected.at(1))
                nc.vector.tensor_scalar(w_c[STATES:], w_c[STATES:], -1.0, None, ALU.mult)
                nc.vector.tensor_scalar(h[:], lru_psum, m.lru_gamma[:], None, ALU.mult).then_inc(h_ready.sem, 1)
                for s in range(STEPS):
                    dve.wait_ge(h_ready.sem, h_ready.at(s + 1))
                    dve.wait_ge(stepped.sem, stepped.at(s + 1))
                    shift = 1 << s
                    nc.vector.tensor_tensor(h[:, shift:], h[:, shift:], lru_psum[:, shift:], ALU.add)\
                      .then_inc(h_ready.sem, 1)
                for n in range(ITEMS):
                    gate(dve, n, None, n % NT, n % 2)

            @block.scalar
            def _(act):
                for n in range(ITEMS):
                    activate(act, n, n % 2)
                    if n:
                        store_turned(act, n - 1, (n - 1) % 2)
                store_turned(act, ITEMS - 1, 1)
        close()
        loaded.close(32)
        for s, n in ((projected, 1), (h_ready, STEPS + 1), (stepped, STEPS)):
            s.close(n)


def finish(m, b, out, add_mixer=True):
    nc = m.nc
    joined, stored = m.sig("sequence_joined"), m.sig("sequence_stored")
    with nc.Block() as block:
        @block.vector
        def _(dve):
            for h in range(2):
                x_pair = m.x[:, 2 * h:2 * h + 2].rearrange("p t d -> p (t d)")
                nc.vector.tensor_tensor(x_pair, x_pair, m.acc[:, h, :], ALU.add).then_inc(joined.sem, 1)

        @block.sync
        def _(sp):
            for h in range(2):
                sp.wait_ge(joined.sem, joined.at(h + 1))
                sp.dma_start(out[b, h * 2 * P:(h + 1) * 2 * P].rearrange("(t p) d -> p t d", p=P),
                             m.x[:, 2 * h:2 * h + 2]).then_inc(stored.sem, 16)
            sp.wait_ge(stored.sem, stored.at(32))
    joined.close(2)
    stored.close(32)


def clear_stage(m):
    with m.nc.Block() as block:
        @block.tensor
        def _(pe):
            clear_acc(m, pe)


STOP = 4


def hybrid_stack_kernel(nc, dram, out):
    with ExitStack() as ctx:
        m = Machine(nc, ctx, dram)
        prepare(m)
        for b in range(BATCH):
            with ExitStack() as rows_ctx:
                spline = SplineRows(m, rows_ctx) if b == 0 else None
                normalise(m, b, 0)
                attention(m, 0, spline)
                mixture(m, 0, with_table=b == 0)
                if spline:
                    spline.turn()
            if STOP >= 2:
                normalise(m, b, 1)
                clear_stage(m)
                state_space(m)
            if STOP >= 3:
                normalise(m, b, 2)
                linear_recurrence(m)
            if STOP >= 4:
                normalise(m, b, 3)
                attention(m, 3)
                mixture(m, 3)
            finish(m, b, out)



def shape_constants():
    f32, bf16 = np.float32, np.dtype("bfloat16")
    out = {"ident": np.eye(P, dtype=f32), "ident_bf": np.eye(P).astype(bf16)}
    i = np.arange(P)
    out["mask_bf"] = np.where(i[None, :] > i[:, None], MASKED, 0.0).astype(bf16)
    freq = (f32(1.0 / 1024.0) ** np.linspace(0.0, 1.0, HD // 4, dtype=f32)).astype(f32)
    theta = np.arange(T, dtype=f32)[None, :] * freq[:, None]
    cos, sin = np.cos(theta.astype(np.float64)), np.sin(theta.astype(np.float64))
    out["rope_cos"] = np.concatenate([cos, cos]).astype(f32)
    out["rope_sin"] = np.concatenate([-sin, sin]).astype(f32)
    rows = np.arange(6 * NS)[:, None, None] % (2 * NS) == np.arange(2 * NS)[None, :, None]
    out["select"] = np.broadcast_to(rows, (6 * NS, 2 * NS, P)).astype(bf16)
    p = np.arange(2 * STATES)
    out["lru_fold"] = (p[:, None] % STATES == np.arange(STATES)[None, :]).astype(f32)
    re, im = (p < STATES).astype(f32), (p >= STATES).astype(f32)
    out["lru_sign"] = np.stack([re, -im, im, re], 1)
    base, frac, at = spline_grid()
    coef = np.zeros((P * 8, WINDOW, D), np.float64)
    f = frac.astype(np.float64)
    blend = (0.5 * (-f + 2 * f ** 2 - f ** 3), 0.5 * (2 - 5 * f ** 2 + 3 * f ** 3),
             0.5 * (f + 4 * f ** 2 - 3 * f ** 3), 0.5 * (-f ** 2 + f ** 3))
    r, c = np.arange(P * 8)[:, None], np.arange(D)[None, :]
    for k in range(4):
        coef[r, at + k, c] += blend[k]
    out["spline_coef"] = coef.astype(f32)[spline_rows_of()]
    return out


def spline_grid():
    n = INTER1 * D
    t = np.linspace(0.0, NCTRL - 1.0, n, dtype=np.float64)
    i = np.clip(np.floor(t).astype(np.int64), 0, NCTRL - 2)
    frac = (t - i).astype(np.float32).reshape(P * 8, D)
    i = i.reshape(P * 8, D)
    base = i[:, 0] - 1
    at = i - 1 - base[:, None]
    assert at.max() + 3 < WINDOW
    return base, frac, at


def spline_rows_of():
    half, q, p = np.meshgrid(np.arange(2), np.arange(4), np.arange(P), indexing="ij")
    return (4 * (half * P + p) + q).reshape(8, P)


def by_rows(w, rows=P):
    return np.ascontiguousarray(w.reshape(-1, rows, w.shape[-1]).transpose(1, 0, 2))


def laid_out(v):
    out = {"x": v["L0_attn_x"]}
    order = np.concatenate([np.arange(0, 32), np.arange(64, 96), np.arange(32, 64), np.arange(96, 128)])

    def heads(mats, wo):
        parts = [w.reshape(KD, P, HEADS, HD).transpose(2, 1, 0, 3).reshape(HEADS, P, KD * HD) for w in mats]
        return np.ascontiguousarray(np.concatenate(parts + [wo.reshape(HEADS, HD, D)], 2))

    q, k, w = (v[f"L0_attn_W{c}"].T.reshape(D, HEADS, HD) for c in "qkv")
    out["heads0"] = heads([q[..., order], k[..., order], w], v["L0_attn_Wo"].T)
    q, k, w = (v[f"L3_attn_w_{c}"].reshape(D, HEADS, HD) for c in "qkv")
    out["heads3"] = heads([q, k, w], v["L3_attn_w_o"])
    out["biases3"] = np.ascontiguousarray(np.stack([v[f"L3_attn_b_{c}"].reshape(HEADS, HD).T for c in "qkv"], 2))
    out["bo"] = v["L3_attn_b_o"].reshape(1, D)

    def gate_up(gate, up):
        both = np.stack([gate, up], 1).reshape(KD, P, 2, GROUPS, -1)
        return np.ascontiguousarray(both.transpose(3, 1, 0, 2, 4).reshape(GROUPS, P, -1))

    def down(w):
        w = w.reshape(GROUPS, -1, P, D)
        return np.ascontiguousarray(w.transpose(0, 2, 1, 3).reshape(GROUPS, P, -1))

    experts = lambda gate_up, down: np.ascontiguousarray(np.concatenate([gate_up, down], 2))
    out["router0"] = by_rows(v["L0_ffn_router_w"].T)
    out["experts0"] = experts(gate_up(*(v[f"L0_ffn_{c}_w"].transpose(2, 0, 1).reshape(D, -1) for c in ("gate", "up"))),
                              down(v["L0_ffn_down_w"].transpose(0, 2, 1).reshape(E0 * I0, D)))
    gu = v["L3_ffn_gate_up"].transpose(1, 0, 2).reshape(D, E3, 2, I3)
    out["router3"] = by_rows(v["L3_ffn_gate_w"])
    out["experts3"] = experts(gate_up(gu[:, :, 0].reshape(D, -1), gu[:, :, 1].reshape(D, -1)),
                              down(v["L3_ffn_down"].reshape(E3 * I3, D)))
    out["router_scale"] = np.ascontiguousarray(v["L3_ffn_router_scale"].reshape(KD, P).T)
    out["per_expert"] = v["L3_ffn_per_expert_scale"].reshape(1, E3)

    out["w_norm"] = np.ascontiguousarray(v["L1_attn_w_norm"].reshape(KD, P).T)
    out["w_in"] = by_rows(v["L1_attn_W_in"])
    out["w_xp"] = by_rows(v["L1_attn_W_xp"])
    out["w_dt"] = v["L1_attn_W_dt"]
    out["w_out"] = by_rows(v["L1_attn_W_out"])
    vec = np.concatenate([v["L1_attn_conv_w"], v["L1_attn_conv_b"][None], v["L1_attn_b_dt"][None],
                          v["L1_attn_D"][None]])
    out["ss_vec"] = np.ascontiguousarray(vec.reshape(7, KC, P).transpose(2, 1, 0))
    out["a_log"] = by_rows(v["L1_attn_A_log"])
    base, _, _ = spline_grid()
    window = np.clip(base[:, None] + np.arange(WINDOW), 0, NCTRL - 1)[spline_rows_of()]
    points = np.stack([v[f"L1_ffn_{c}_cp"][window] for c in ("gate", "up", "down")], 2)
    out["spline_points"] = np.ascontiguousarray(points.transpose(1, 0, 2, 3))

    out["lru_in"] = np.stack([np.tile(v["L2_attn_nu_log"], 2), np.tile(v["L2_attn_theta_log"], 2)], 1)
    out["lru_b"] = by_rows(np.concatenate([v["L2_attn_B_re"], v["L2_attn_B_im"]]).T)
    out["lru_c"] = np.ascontiguousarray(np.concatenate([v["L2_attn_C_re"].T, v["L2_attn_C_im"].T]))
    out["lru_d"] = v["L2_attn_D"].reshape(1, D)
    out["lut"] = v["L2_ffn_lut"].reshape(1, LUT)
    gu = np.stack([v["L2_ffn_gate_idx"].T, v["L2_ffn_up_idx"].T], 1)
    gu = gu.reshape(KD, P, 2 * INTER2).transpose(1, 0, 2).reshape(P, -1)
    dn = np.zeros((2, 3 * P, D), v["L2_ffn_down_idx"].dtype)
    dn[:, :F2] = v["L2_ffn_down_idx"].T.reshape(2, F2, D)
    dn = dn.reshape(6, P, D).transpose(1, 0, 2).reshape(P, -1)
    idx = np.concatenate([gu, dn], 1).reshape(P, GROUPS, LUT_CHUNK)
    out["lut_idx"] = np.ascontiguousarray(idx.transpose(1, 0, 2))
    return out


def kernel(**inputs):
    import concourse.bacc as bacc
    from concourse.bass_utils import run_bass_kernel_spmd

    arrays = laid_out({name: np.asarray(a) for name, a in inputs.items()})
    arrays.update(shape_constants())
    arrays = {f"in_{name}": np.ascontiguousarray(a) for name, a in arrays.items()}
    nc = bacc.Bacc("TRN2", target_bir_lowering=False, num_devices=1)
    dram = {name[3:]: nc.dram_tensor(name, a.shape, mybir.dt.from_np(a.dtype), kind="ExternalInput").ap()
            for name, a in arrays.items()}
    out = nc.dram_tensor("out", (BATCH, T, D), FP32, kind="ExternalOutput").ap()
    hybrid_stack_kernel(nc, dram, out)
    result = run_bass_kernel_spmd(nc, [arrays], core_ids=[0])
    return result.results[0]["out"]
```

```python
from contextlib import ExitStack

import numpy as np

import concourse.bass as bass
from concourse import mybir

FP32 = mybir.dt.float32
FP32R = mybir.dt.float32r
BF16 = mybir.dt.bfloat16
INT32 = mybir.dt.int32
ACT = mybir.ActivationFunctionType
ALU = mybir.AluOpType
AXIS = mybir.AxisListType

P = 128
BATCH, T, D = 2, 512, 256
NT = T // P
KD = D // P
HEADS, HD = 16, 128
QK_SCALE = float(HD) ** -0.5
MASKED = -1e30

E0, TOP0, I0 = 32, 4, 96
E3, TOP3, I3 = 8, 2, 256
GROUPS = 8
F0 = E0 * I0 // GROUPS
F3 = E3 * I3 // GROUPS

CH, NS, RANK, TAPS = 512, 16, 128, 4
KC = CH // P
INTER1 = 1024
NCTRL = max(16, int(INTER1 * D / 128.9))
WINDOW = 6
STATES = 32
INTER2 = 688
F2 = INTER2 // 2
F2_ROWS = (P, P, F2 - 2 * P)
LUT = 16
LUT_COLS = KD * 2 * INTER2 + 6 * D
LUT_CHUNK = LUT_COLS // GROUPS
TWO_PI = 2.0 * np.pi


class Signal:

    def __init__(self, nc, ctx, name):
        self.sem = ctx.enter_context(nc.semaphore(name))
        self.base = 0

    def at(self, n):
        return self.base + n

    def close(self, n):
        self.base = self.base + n


class Chain:

    def __init__(self, eng, count, start=0):
        self.eng, self.count, self.start, self.n = eng, count, start, 0

    def link(self, instruction):
        instruction.then_inc(self.count.sem, 1)
        self.n += 1

    def wait(self):
        self.eng.wait_ge(self.count.sem, self.count.at(self.start + self.n))

    def all(self, instruction):
        self.link(instruction)
        self.wait()


class Machine:

    def __init__(self, nc, ctx, dram):
        self.nc, self.ctx, self.dram = nc, ctx, dram
        self.signals, self.n_local = {}, 0
        sb = lambda name, shape, dt=FP32: ctx.enter_context(nc.sbuf_tensor(name, shape, dt))
        self.x_of = [sb(f"x{b}", [P, NT, D]) for b in range(BATCH)]
        self.xn = sb("xn", [P, NT, D])
        self.xnT = sb("xnT", [P, KD, T])
        self.xnT_parts = [sb(f"xnT_{part}", [P, KD, T], FP32R) for part in ("high", "low")]
        self.stats = sb("stats", [P, NT, 6])
        self.mv = sb("mv", [P, NT, 2])
        self.rs = sb("rs", [P, 6, NT])
        self.ident = sb("ident", [P, P])
        self.ident_bf = sb("ident_bf", [P, P], BF16)
        self.mask_bf = sb("mask_bf", [P, P], BF16)
        self.zero_row = sb("zero_row", [1, T], BF16)
        self.spline_gu = sb("spline_gu", [P, KD, 2, INTER1])
        self.spline_down = sb("spline_down", [P, INTER1 // P, D])
        self.lut_w = sb("lut_w", [P, LUT_COLS])
        self.lru_step = sb("lru_step", [2 * STATES, 9, 2 * STATES])
        self.lru_gamma = sb("lru_gamma", [2 * STATES, 1])
        self.acc = ctx.enter_context(nc.psum_tensor("acc", [P, 2, 512], FP32))
        self.banks = ctx.enter_context(nc.psum_tensor("banks", [P, 6, 512], FP32))

    def sig(self, name):
        if name not in self.signals:
            self.signals[name] = Signal(self.nc, self.ctx, name)
        return self.signals[name]

    def local(self, stage_ctx):
        self.n_local += 1
        tag = self.n_local
        return lambda name, shape, dt=FP32: stage_ctx.enter_context(
            self.nc.sbuf_tensor(f"{name}_{tag}", shape, dt))

    def acc_tile(self, t):
        return self.acc[:, t // 2, (t % 2) * D:(t % 2 + 1) * D]


class Stage:

    def __init__(self, close=lambda: None, sync=None, tensor=None, vector=None, scalar=None, gpsimd=None):
        self.close, self.sync, self.tensor, self.vector, self.scalar, self.gpsimd = (
            close, sync, tensor, vector, scalar, gpsimd)


def run(m, *stages):
    with m.nc.Block() as block:
        @block.sync
        def _(sp):
            for s in stages:
                if s.sync:
                    s.sync(sp)

        @block.tensor
        def _(pe):
            for s in stages:
                if s.tensor:
                    s.tensor(pe)

        @block.vector
        def _(dve):
            for s in stages:
                if s.vector:
                    s.vector(dve)

        @block.scalar
        def _(act):
            for s in stages:
                if s.scalar:
                    s.scalar(act)

        @block.gpsimd
        def _(pool):
            for s in stages:
                if s.gpsimd:
                    s.gpsimd(pool)
    for s in stages:
        s.close()


def exact_product(nc, out, left, right, start, stop, **kw):
    for n, (a, b) in enumerate(((0, 0), (0, 1), (1, 0))):
        last = nc.tensor.matmul(out, left[a], right[b], start=start and n == 0, stop=stop and n == 2, **kw)
    return last


def reciprocal_root(nc, chain, rs):
    chain.all(nc.vector.reciprocal(rs[:, 2], rs[:, 1]))
    chain.all(nc.vector.tensor_tensor(rs[:, 4], rs[:, 2], rs[:, 2], ALU.mult))
    chain.all(nc.vector.tensor_tensor(rs[:, 4], rs[:, 4], rs[:, 0], ALU.mult))
    chain.all(nc.vector.tensor_scalar(rs[:, 4], rs[:, 4], -0.5, 1.5, ALU.mult, ALU.add))
    chain.all(nc.vector.tensor_tensor(rs[:, 3], rs[:, 2], rs[:, 4], ALU.mult))


def transition(m, ctx):
    nc, dram = m.nc, m.dram
    sb = m.local(ctx)
    lru_in = sb("lru_in", [2 * STATES, 2])
    lru_sign = sb("lru_sign", [2 * STATES, 4])
    lru_fold = sb("lru_fold", [2 * STATES, STATES])
    lru = sb("lru", [2 * STATES, 24])
    turns = sb("turns", [2 * STATES, 1], INT32)
    power = sb("power", [2 * STATES, 2, 9])
    blend = sb("blend", [2 * STATES, 4, 9])
    loaded, zeroed = m.sig("constants_loaded"), m.sig("zeroed")
    act_chain, lru_chain = m.sig("act_chain"), m.sig("lru_chain")
    lru_act, lru_dve = m.sig("lru_act"), m.sig("lru_dve")
    constants = [
        (m.ident[:], dram["ident"]), (m.ident_bf[:], dram["ident_bf"]), (m.mask_bf[:], dram["mask_bf"]),
        (lru_in[:], dram["lru_in"]), (lru_sign[:], dram["lru_sign"]), (lru_fold[:], dram["lru_fold"]),
    ]

    def load(sp):
        for b in range(BATCH):
            sp.dma_start(m.x_of[b][:], dram["x"][b].rearrange("(t p) d -> p t d", p=P))\
              .then_inc(m.sig(f"x_loaded{b}").sem, 16)
        for dst, src in constants:
            sp.dma_start(dst, src).then_inc(loaded.sem, 16)

    def zero(dve):
        nc.vector.memset(m.zero_row[:], 0.0).then_inc(zeroed.sem, 1)

    def wait_constants(pe):
        pe.wait_ge(loaded.sem, loaded.at(16 * len(constants)))
        pe.wait_ge(zeroed.sem, zeroed.at(1))

    def scalar(act):
        act.wait_ge(loaded.sem, loaded.at(16 * len(constants)))
        chain = Chain(act, act_chain)
        chain.all(nc.scalar.activation(lru[:, 0:1], lru_in[:, 0:1], ACT.Abs))
        chain.all(nc.scalar.activation(lru[:, 1:2], lru[:, 0:1], ACT.Exp, scale=-1.0))
        nc.scalar.activation(lru[:, 3:4], lru_in[:, 1:2], ACT.Exp).then_inc(lru_act.sem, 1)
        chain.all(nc.scalar.activation(lru[:, 2:3], lru[:, 1:2], ACT.Ln, bias=1.0))
        act.wait_ge(lru_dve.sem, lru_dve.at(1))
        chain.all(nc.scalar.activation(lru[:, 5:6], lru[:, 4:5], ACT.Identity, bias=lru[:, 2:3]))
        chain.all(nc.scalar.activation(lru[:, 6:7], lru[:, 5:6], ACT.Exp))
        nc.scalar.activation(lru[:, 7:8], lru[:, 6:7], ACT.Exp, scale=-1.0).then_inc(lru_act.sem, 1)
        act.wait_ge(lru_dve.sem, lru_dve.at(2))
        nc.scalar.activation(lru[:, 14:15], lru[:, 12:13], ACT.Sin)
        nc.scalar.activation(lru[:, 15:16], lru[:, 13:14], ACT.Sin).then_inc(lru_act.sem, 1)
        act.wait_ge(lru_dve.sem, lru_dve.at(3))
        nc.scalar.activation(m.lru_gamma[:], lru[:, 17:18], ACT.Sqrt)
        act_chain.close(chain.n)

    def vector(dve):
        chain = Chain(dve, lru_chain)
        dve.wait_ge(loaded.sem, loaded.at(16 * len(constants)))
        nc.vector.tensor_scalar(lru[:, 4:5], lru_in[:, 0:1], 0.0, None, ALU.max).then_inc(lru_dve.sem, 1)
        dve.wait_ge(lru_act.sem, lru_act.at(1))
        chain.all(nc.vector.tensor_scalar(turns[:], lru[:, 3:4], float(1.0 / TWO_PI), None, ALU.mult))
        chain.all(nc.vector.tensor_copy(lru[:, 8:9], turns[:]))
        c1 = 6.28125
        c2 = float(np.float32(TWO_PI - c1))
        c2 = float(np.frombuffer(np.uint32(np.float32(c2).view(np.uint32) & 0xFFFFF000).tobytes(), np.float32)[0])
        c3 = float(TWO_PI - c1 - c2)
        chain.all(nc.vector.scalar_tensor_tensor(lru[:, 9:10], lru[:, 8:9], -c1, lru[:, 3:4], ALU.mult, ALU.add))
        chain.all(nc.vector.scalar_tensor_tensor(lru[:, 10:11], lru[:, 8:9], -c2, lru[:, 9:10], ALU.mult, ALU.add))
        chain.all(nc.vector.scalar_tensor_tensor(lru[:, 11:12], lru[:, 8:9], -c3, lru[:, 10:11], ALU.mult, ALU.add))
        fold_turn(nc, chain, lru, 11, 16, 18)
        chain.all(nc.vector.tensor_scalar(lru[:, 19:20], lru[:, 16:17], float(np.pi / 2), None, ALU.add))
        fold_turn(nc, chain, lru, 19, 20, 18)
        limit = float(np.nextafter(np.float32(np.pi), np.float32(0)))
        chain.all(nc.vector.tensor_scalar(lru[:, 12:13], lru[:, 16:17], -limit, limit, ALU.max, ALU.min))
        nc.vector.tensor_scalar(lru[:, 13:14], lru[:, 20:21], -limit, limit, ALU.max, ALU.min)\
          .then_inc(lru_dve.sem, 1)
        dve.wait_ge(lru_act.sem, lru_act.at(3))
        chain.all(nc.vector.tensor_tensor(lru[:, 21:22], lru[:, 7:8], lru[:, 7:8], ALU.mult))
        chain.all(nc.vector.tensor_scalar(lru[:, 22:23], lru[:, 21:22], -1.0, 1.0, ALU.mult, ALU.add))
        nc.vector.tensor_scalar(lru[:, 17:18], lru[:, 22:23], 0.0, None, ALU.max).then_inc(lru_dve.sem, 1)
        lru_chain.close(chain.n)

    def powers(dve):
        chain = Chain(dve, lru_chain)
        nc.vector.tensor_tensor(power[:, 0, 0:1], lru[:, 7:8], lru[:, 15:16], ALU.mult)
        chain.all(nc.vector.tensor_tensor(power[:, 1, 0:1], lru[:, 7:8], lru[:, 14:15], ALU.mult))
        for s in range(1, 9):
            re, im = power[:, 0, s - 1:s], power[:, 1, s - 1:s]
            nc.vector.tensor_tensor(blend[:, 0, 0:1], re, re, ALU.mult)
            nc.vector.tensor_tensor(blend[:, 1, 0:1], im, im, ALU.mult)
            chain.all(nc.vector.scalar_tensor_tensor(power[:, 1, s:s + 1], re, 2.0, im, ALU.mult, ALU.mult))
            chain.all(nc.vector.tensor_tensor(power[:, 0, s:s + 1], blend[:, 0, 0:1], blend[:, 1, 0:1],
                                              ALU.subtract))
        for c in range(2):
            nc.vector.tensor_scalar(blend[:, 0], power[:, 0], lru_sign[:, 2 * c:2 * c + 1], None, ALU.mult)
            chain.all(nc.vector.tensor_scalar(blend[:, 1], power[:, 1], lru_sign[:, 2 * c + 1:2 * c + 2],
                                              None, ALU.mult))
            chain.all(nc.vector.tensor_tensor(blend[:, 2 + c], blend[:, 0], blend[:, 1], ALU.add))
        for s in range(9):
            for c in range(2):
                nc.vector.tensor_scalar(m.lru_step[:, s, c * STATES:(c + 1) * STATES], lru_fold[:],
                                        blend[:, 2 + c, s:s + 1], None, ALU.mult)
        lru_chain.close(chain.n)

    def close():
        for s, n in ((loaded, 16 * len(constants)), (lru_act, 3), (lru_dve, 3), (zeroed, 1)):
            s.close(n)

    return (Stage(sync=load, vector=zero, tensor=wait_constants), Stage(close, vector=vector, scalar=scalar),
            Stage(vector=powers))


class SplineRows:

    def __init__(self, m, ctx):
        sb = m.local(ctx)
        self.m = m
        self.rows = sb("spline_rows", [P, 8, 3, D])
        self.loaded, self.chain = m.sig("points_loaded"), m.sig("pool_chain")
        self.coef_loaded = [m.sig(f"coef_loaded{i}") for i in range(2)]

    def allocate(self, sb):
        self.coef = sb("coef", [P, 2, WINDOW, D])
        self.term = sb("term", [P, 2, 3, D])
        self.points = sb("points", [P, 8, 3, WINDOW])

    def make(self, pool, interlude):
        m, nc = self.m, self.m.nc
        load = lambda n: pool.dma_start(self.coef[:, n % 2], m.dram["spline_coef"][n])\
            .then_inc(self.coef_loaded[n % 2].sem, 16)
        pool.dma_start(self.points[:], m.dram["spline_points"]).then_inc(self.loaded.sem, 16)
        load(0)
        load(1)
        pool.wait_ge(self.loaded.sem, self.loaded.at(16))
        chain = Chain(pool, self.chain)
        for n in range(8):
            pool.wait_ge(self.coef_loaded[n % 2].sem, self.coef_loaded[n % 2].at(16 * (n // 2 + 1)))
            rows = self.rows[:, n]
            for j in range(WINDOW):
                for w in range(3):
                    out = self.term[:, j % 2, w] if j else rows[:, w]
                    chain.link(nc.gpsimd.tensor_scalar(out, self.coef[:, n % 2, j], self.points[:, n, w, j:j + 1],
                                                       1.0, ALU.mult, ALU.mult))
                chain.wait()
                if j == WINDOW // 2:
                    interlude(2 * n)
                if j:
                    chain.link(nc.gpsimd.tensor_tensor(rows, rows, self.term[:, j % 2], ALU.add))
            chain.wait()
            if n + 2 < 8:
                load(n + 2)
            interlude(2 * n + 1)
        self.chain.close(chain.n)
        self.loaded.close(16)
        for s in self.coef_loaded:
            s.close(64)

    def turn(self):
        m, nc = self.m, self.m.nc
        turned, stored = m.sig("rows_turned"), m.sig("turned_stored")
        def tensor(pe):
            for n in range(8):
                if n >= 2:
                    pe.wait_ge(stored.sem, stored.at(n - 1))
                for w in range(3):
                    for k in range(KD):
                        at = ((w % 2) * 2 + k) * P
                        last = nc.tensor.transpose(m.banks[:, 2 * (n % 2) + w // 2, at:at + P],
                                                   self.rows[:, n, w, k * P:(k + 1) * P], m.ident[:])
                last.then_inc(turned.sem, 1)

        def scalar(act):
            for n in range(8):
                act.wait_ge(turned.sem, turned.at(n + 1))
                half, q = divmod(n, 4)
                b = 2 * (n % 2)
                for w in range(2):
                    out = m.spline_gu[:, :, w, half * 512:(half + 1) * 512]
                    out = out.rearrange("p k (c q) -> p k q c", q=4)[:, :, q, :]
                    src = m.banks[:, b, w * 2 * P:(w + 1) * 2 * P].rearrange("p (k c) -> p k c", k=KD)
                    nc.scalar.activation(out, src, ACT.Copy)
                src = m.banks[:, b + 1, 0:2 * P].rearrange("p (k c) -> p k c", k=KD)
                nc.scalar.activation(m.spline_down[:, 2 * q:2 * q + 2, half * P:(half + 1) * P], src, ACT.Copy)\
                  .then_inc(stored.sem, 1)

        def close():
            turned.close(8)
            stored.close(8)

        return Stage(close, tensor=tensor, scalar=scalar)


class TableWeights:
    SPLIT = 3
    LINKS = 4 + SPLIT + 7 + 1

    def __init__(self, m, ctx):
        sb = m.local(ctx)
        self.m = m
        self.idx = sb("idx", [P, 2, LUT_CHUNK], INT32)
        self.bits = sb("bits", [P, 4, LUT_CHUNK], INT32)
        self.leaves = sb("leaves", [P, LUT // 2, LUT_CHUNK])
        self.table, self.delta = sb("table", [P, LUT]), sb("delta", [P, LUT // 2])
        self.carrier, self.pool_carrier = sb("carrier", [P, 3]), sb("pool_carrier", [P, 2])
        self.bits_ready, self.leaves_ready = m.sig("bits_ready"), m.sig("leaves_ready")
        self.loaded, self.chain = m.sig("table_loaded"), m.sig("table_chain")
        self.idx_loaded = [m.sig(f"idx_loaded{i}") for i in range(2)]
        self.read = m.sig("chunk_read")

    def load(self, sp, g, par):
        src = self.m.dram["lut_idx"][bass.ds(g, 1)].rearrange("a p f -> (a p) f")
        sp.dma_start(self.idx[:, par], src).then_inc(self.idx_loaded[par].sem, 16)

    def start(self, sp):
        sp.dma_start(self.table[:], self.m.dram["lut"].broadcast_to([P, LUT])).then_inc(self.loaded.sem, 16)

    def first(self, dve):
        dve.wait_ge(self.loaded.sem, self.loaded.at(16))
        low, high = (self.table[:].rearrange("p (j e) -> p e j", e=2)[:, e] for e in range(2))
        self.m.nc.vector.tensor_tensor(self.delta[:], high, low, ALU.subtract).then_inc(self.loaded.sem, 1)

    def part(self, dve, g, par, pair, quarter):
        nc, chain = self.m.nc, Chain(dve, self.chain, self.LINKS * g)
        carry = lambda n: nc.vector.memset(self.carrier[:, n:n + 1], 0.0)
        done = (0, 4, 4 + self.SPLIT, 8 + self.SPLIT)[quarter]
        chain.n = done
        tree, bits = self.leaves, self.bits
        if quarter == 0:
            dve.wait_ge(self.idx_loaded[par].sem, self.idx_loaded[par].at(16 * (pair + 1)))
            for b in range(4):
                ins = nc.vector.tensor_scalar(bits[:, b], self.idx[:, par], 1 << b, None, ALU.bitwise_and)
                chain.link(ins)
        if quarter == 1:
            chain.wait()
            dve.sem_inc(self.read.sem, 1)
            dve.sem_inc(self.bits_ready.sem, 1)
            for j in range(self.SPLIT):
                chain.link(nc.vector.tensor_scalar(tree[:, j], bits[:, 0], self.delta[:, j:j + 1],
                                                   self.table[:, 2 * j:2 * j + 1], ALU.mult, ALU.add))
        if quarter == 2:
            dve.wait_ge(self.leaves_ready.sem, self.leaves_ready.at(g + 1))
            chain.wait()
            carry(0)
            for a in (0, 2, 4, 6):
                chain.link(nc.vector.copy_predicated(tree[:, a], bits[:, 1], tree[:, a + 1]))
        if quarter == 3:
            chain.wait()
            carry(1)
            for a in (0, 4):
                chain.link(nc.vector.copy_predicated(tree[:, a], bits[:, 2], tree[:, a + 2]))
            chain.wait()
            carry(2)
            chain.link(nc.vector.copy_predicated(tree[:, 0], bits[:, 3], tree[:, 4]))
            chain.wait()
            chain.link(nc.vector.tensor_copy(self.m.lut_w[:, bass.ds(g * LUT_CHUNK, LUT_CHUNK)], tree[:, 0]))

    def leaves_of(self, pool, g, par):
        nc = self.m.nc
        pool.wait_ge(self.bits_ready.sem, self.bits_ready.at(g + 1))
        nc.gpsimd.tensor_tensor(self.pool_carrier[:, par:par + 1], self.m.ident[:, 0:1], self.m.ident[:, 0:1],
                                ALU.mult)
        for j in range(self.SPLIT, LUT // 2):
            last = nc.gpsimd.tensor_scalar(self.leaves[:, j], self.bits[:, 0], self.delta[:, j:j + 1],
                                           self.table[:, 2 * j:2 * j + 1], ALU.mult, ALU.add)
        last.then_inc(self.leaves_ready.sem, 1)

    def close(self):
        self.bits_ready.close(GROUPS)
        self.leaves_ready.close(GROUPS)
        self.loaded.close(17)
        self.chain.close(GROUPS * self.LINKS)
        self.read.close(GROUPS)
        for s in self.idx_loaded:
            s.close(16 * GROUPS // 2)


def fold_turn(nc, chain, v, src, dst, tmp):
    chain.all(nc.vector.tensor_scalar(v[:, tmp:tmp + 1], v[:, src:src + 1], float(np.pi), -TWO_PI,
                                      ALU.is_gt, ALU.mult))
    chain.all(nc.vector.tensor_tensor(v[:, dst:dst + 1], v[:, src:src + 1], v[:, tmp:tmp + 1], ALU.add))
    chain.all(nc.vector.tensor_scalar(v[:, tmp:tmp + 1], v[:, dst:dst + 1], -float(np.pi), TWO_PI,
                                      ALU.is_lt, ALU.mult))
    chain.all(nc.vector.tensor_tensor(v[:, dst:dst + 1], v[:, dst:dst + 1], v[:, tmp:tmp + 1], ALU.add))


def normalise(m, b, layer, scalar_between=None, vector_between=None):
    nc, x = m.nc, m.x_of[b]
    stepped, rooted, normed = m.sig("ln_var"), m.sig("ln_root"), m.sig("ln_normed")
    turned = m.sig("ln_turned")
    ln_chain, high_ready, low_ready = m.sig("ln_chain"), m.sig("xnT_high"), m.sig("xnT_low")
    def vector(dve):
        chain = Chain(dve, ln_chain)
        if layer == 0:
            dve.wait_ge(m.sig(f"x_loaded{b}").sem, 16)
        if layer:
            for h in range(2):
                x_pair = x[:, 2 * h:2 * h + 2].rearrange("p t d -> p (t d)")
                chain.link(nc.vector.tensor_tensor(x_pair, x_pair, m.acc[:, h, :], ALU.add))
            chain.wait()
        for t in range(NT):
            chain.link(nc.vector.bn_stats(m.stats[:, t], x[:, t]))
        chain.wait()
        for t in range(NT):
            chain.link(nc.vector.bn_aggr(m.mv[:, t], m.stats[:, t]))
        chain.wait()
        nc.vector.tensor_scalar(m.rs[:, 0], m.mv[:, :, 1], 1e-5, None, ALU.add).then_inc(stepped.sem, 1)
        dve.wait_ge(stepped.sem, stepped.at(1))
        dve.wait_ge(rooted.sem, rooted.at(1))
        reciprocal_root(nc, chain, m.rs)
        for t in range(NT):
            last = nc.vector.tensor_scalar(m.xn[:, t], x[:, t], m.mv[:, t, 0:1], m.rs[:, 3, t:t + 1],
                                           ALU.subtract, ALU.mult)
            last.then_inc(normed.sem, 1)
        if vector_between:
            vector_between(dve)
        for k in range(KD):
            dve.wait_ge(high_ready.sem, high_ready.at(k + 1))
            high, low = (part[:, k] for part in m.xnT_parts)
            nc.vector.tensor_tensor(low, m.banks[:, k, :], high.bitcast(FP32), ALU.subtract)\
              .then_inc(low_ready.sem, 1)
        ln_chain.close(chain.n)

    def scalar(act):
        act.wait_ge(stepped.sem, stepped.at(1))
        nc.scalar.activation(m.rs[:, 1], m.rs[:, 0], ACT.Sqrt).then_inc(rooted.sem, 1)
        if scalar_between:
            scalar_between(act)
        for k in range(KD):
            act.wait_ge(turned.sem, turned.at(k + 1))
            nc.scalar.activation(m.xnT[:, k], m.banks[:, k, :], ACT.Copy)
            nc.scalar.activation(m.xnT_parts[0][:, k], m.banks[:, k, :], ACT.Copy)\
              .then_inc(high_ready.sem, 1)

    def tensor(pe):
        for k in range(KD):
            for t in range(NT):
                pe.wait_ge(normed.sem, normed.at(t + 1))
                last = nc.tensor.transpose(m.banks[:, k, t * P:(t + 1) * P],
                                           m.xn[:, t, k * P:(k + 1) * P], m.ident[:])
            last.then_inc(turned.sem, 1)

    def close():
        for s, n in ((stepped, 1), (rooted, 1), (normed, NT), (turned, KD), (high_ready, KD), (low_ready, KD)):
            s.close(n)

    return Stage(close, vector=vector, scalar=scalar, tensor=tensor)


def wait_xnT(m, eng):
    for part in (m.sig("xnT_high"), m.sig("xnT_low")):
        eng.wait_ge(part.sem, part.at(KD))


SCORE_AT = {3: (0, 0), 2: (1, 0), 1: (2, 0), 0: (2, 2 * P)}
PROB_AT = {3: 0, 2: T, 1: T + 3 * P, 0: T + 5 * P}
PROB_COLS = 10 * P
TURNED_BANKS = ((0, 4 * P), (T, 3 * P), (T + 3 * P, 3 * P))


def attention(m, layer, ctx, spline=None, ahead=None):
    nc = m.nc
    rotary = layer == 0
    heads_dram = m.dram[f"heads{layer}"]
    loaded = [m.sig(f"head_loaded{i}") for i in range(2)]
    qkv_high, qkv_split, wo_high, wo_split = m.sig("qkv_high"), m.sig("qkv_split"), m.sig("wo_high"), m.sig("wo_split")
    qk_high, v_low, probsT_low, y_low = m.sig("qk_high"), m.sig("v_low"), m.sig("probsT_low"), m.sig("y_low")
    qk_projected, v_projected, scored = m.sig("qk_projected"), m.sig("v_projected"), m.sig("scored")
    turned, attended, added = m.sig("turned"), m.sig("attended"), m.sig("head_added")
    qk_ready, qk_rest_ready, max_ready = m.sig("qk_ready"), m.sig("qk_rest_ready"), m.sig("max_ready")
    exp_ready, probs_ready, v_ready = m.sig("exp_ready"), m.sig("probs_ready"), m.sig("v_ready")
    probsT_ready, y_ready, dve_chain = m.sig("probsT_ready"), m.sig("y_ready"), m.sig("dve_chain")
    rope_loaded = m.sig("rope_loaded")
    CHAIN_QK = 3 if rotary else 0
    CHAIN_SOFTMAX = 5

    sb = m.local(ctx)
    QKV = 3 * KD * HD
    raw = [sb(f"head{i}", [P, QKV + D]) for i in range(2)]
    parts = [[sb(f"head_{part}{i}", [P, QKV + D], FP32R) for part in ("high", "low")] for i in range(2)]
    qkT = sb("qkT", [P, 2, T], FP32 if rotary else FP32R)
    v = [sb(f"v{i}", [P, NT, HD], FP32 if rotary else FP32R) for i in range(2)]
    if not rotary:
        qkT_low = sb("qkT_low", [P, 2, T], FP32R)
        v_lows = [sb(f"v_low{i}", [P, NT, HD], FP32R) for i in range(2)]
        probsT_lows = sb("probsT_low", [P, PROB_COLS], FP32R)
        biases = sb("biases", [P, HEADS, 3])
        bo_row, one_row = sb("bo_row", [1, 2, D]), sb("one_row", [1, P])
    if rotary:
        rot = sb("rot", [64, 2, 2, T])
        rope_cos, rope_sin = sb("rope_cos", [64, T]), sb("rope_sin", [64, T])
    probs = sb("probs", [P, PROB_COLS])
    probsT = sb("probsT", [P, PROB_COLS], FP32 if rotary else FP32R)
    yT, yT_low = sb("yT", [P, T], FP32R), sb("yT_low", [P, T], FP32R)
    row_max, neg_max = sb("row_max", [P, NT]), sb("neg_max", [P, NT])
    row_sum, row_inv = sb("row_sum", [P, NT]), sb("row_inv", [P, NT])
    if spline:
        spline.allocate(sb)
    bias_of = lambda h, which: biases[:, bass.ds(h, 1), which:which + 1].rearrange("p a n -> p (a n)")
    qk_psum, v_psum = m.banks[:, 3:5, :], m.banks[:, 5, :]

    def score_tile(i):
        b, at = SCORE_AT[i]
        return m.banks[:, b, at:at + (i + 1) * P]

    def prob_tile(i):
        return probs[:, PROB_AT[i]:PROB_AT[i] + (i + 1) * P]

    def turned_tile(k, of=None):
        return (probsT if of is None else of)[:, PROB_AT[3 - k]:PROB_AT[3 - k] + (NT - k) * P]

    def load(sp, h, par):
        sp.dma_start(raw[par][:], head_rows(heads_dram, h)).then_inc(loaded[par].sem, 16)

    def high_qkv(act, h, par, use):
        act.wait_ge(loaded[par].sem, loaded[par].at(16 * use))
        nc.scalar.activation(parts[par][0][:, 0:QKV], raw[par][:, 0:QKV], ACT.Copy).then_inc(qkv_high.sem, 1)

    def low(pool, columns, high, split, h, par):
        pool.wait_ge(high.sem, high.at(h + 1))
        nc.gpsimd.tensor_tensor(parts[par][1][:, columns], raw[par][:, columns],
                                parts[par][0][:, columns].bitcast(FP32), ALU.subtract).then_inc(split.sem, 1)

    low_qkv = lambda pool, h, par: low(pool, slice(0, QKV), qkv_high, qkv_split, h, par)
    low_wo = lambda pool, h, par: low(pool, slice(QKV, QKV + D), wo_high, wo_split, h, par)

    def first_sync(sp):
        load(sp, 0, 0)
        load(sp, 1, 1)
        if rotary:
            sp.dma_start(rope_cos[:], m.dram["rope_cos"]).then_inc(rope_loaded.sem, 16)
            sp.dma_start(rope_sin[:], m.dram["rope_sin"]).then_inc(rope_loaded.sem, 16)
        else:
            sp.dma_start(biases[:], m.dram["biases3"]).then_inc(rope_loaded.sem, 16)
            sp.dma_start(one_row[:], m.dram["ones"]).then_inc(rope_loaded.sem, 16)
            for half in range(2):
                sp.dma_start(bo_row[:, half, :], m.dram["bo"]).then_inc(rope_loaded.sem, 16)
        if ahead:
            ahead.load(sp)

    def first_scalar(act):
        high_qkv(act, 0, 0, 1)
        nc.scalar.activation(parts[0][0][:, QKV:], raw[0][:, QKV:], ACT.Copy).then_inc(wo_high.sem, 1)
        high_qkv(act, 1, 1, 1)

    def first_gpsimd(pool):
        low_qkv(pool, 0, 0)
        low_wo(pool, 0, 0)
        low_qkv(pool, 1, 1)

    def sync(sp):
        with sp.Fori(0, HEADS // 2 - 1) as i:
            for par in range(2):
                h = 2 * i + par
                sp.wait_ge(qkv_split.sem, qkv_split.at(h + 1))
                sp.wait_ge(wo_split.sem, wo_split.at(h + 1))
                load(sp, h + 2, par)

    def tensor(pe):
        def project_qk(par):
            for which in range(2):
                for k in range(KD):
                    at = (which * KD + k) * HD
                    last = exact_product(nc, qk_psum[:, which], [a[:, at:at + HD] for a in parts[par]],
                                         [a[:, k] for a in m.xnT_parts], k == 0, k == KD - 1)
            last.then_inc(qk_projected.sem, 1)

        def project_v(par):
            for t in range(NT):
                for k in range(KD):
                    at = (2 * KD + k) * HD
                    last = exact_product(nc, v_psum[:, t * P:(t + 1) * P],
                                         [a[:, k, t * P:(t + 1) * P] for a in m.xnT_parts],
                                         [a[:, at:at + HD] for a in parts[par]], k == 0, k == KD - 1)
            last.then_inc(v_projected.sem, 1)

        def project(h, par):
            pe.wait_ge(qkv_split.sem, qkv_split.at(h + 1))
            project_qk(par)

        def score():
            for i in (3, 2, 1, 0):
                out = score_tile(i)
                q, key = slice(i * P, (i + 1) * P), slice(0, (i + 1) * P)
                if rotary:
                    nc.tensor.matmul(out, qkT[:, 0, q], qkT[:, 1, key], start=True, stop=False)
                else:
                    exact_product(nc, out, [a[:, 0, q] for a in (qkT, qkT_low)],
                                  [a[:, 1, key] for a in (qkT, qkT_low)], True, False)
                last = nc.tensor.matmul(out[:, i * P:(i + 1) * P], m.ident_bf[:], m.mask_bf[:],
                                        start=False, stop=True)
                if i != 1:
                    last.then_inc(scored.sem, 1)

        def turn():
            for k in range(NT):
                out = score_tile(3 - k)
                for i in range(k, NT):
                    last = nc.tensor.transpose(out[:, (i - k) * P:(i - k + 1) * P],
                                               prob_tile(i)[:, k * P:(k + 1) * P], m.ident[:])
                if k != 2:
                    last.then_inc(turned.sem, 1)

        def add_head(par):
            for t in range(NT):
                last = exact_product(nc, m.acc_tile(t), [a[:, t * P:(t + 1) * P] for a in (yT, yT_low)],
                                     [a[:, QKV:] for a in parts[par]], False, False, skip_group_check=True)
            last.then_inc(added.sem, 1)

        def attend(h, par):
            for k in range(NT):
                if k < 3:
                    pe.wait_ge(probsT_ready.sem, probsT_ready.at(3 * h + k + 1))
                    if not rotary:
                        pe.wait_ge(probsT_low.sem, probsT_low.at(3 * h + k + 1))
                if rotary:
                    last = nc.tensor.matmul(v_psum[:, k * P:T], v[par][:, k], turned_tile(k),
                                            start=k == 0, stop=k == NT - 1)
                else:
                    last = exact_product(nc, v_psum[:, k * P:T], [v[par][:, k], v_lows[par][:, k]],
                                         [turned_tile(k), turned_tile(k, probsT_lows)], k == 0, k == NT - 1)
            last.then_inc(attended.sem, 1)

        def step(h, par, first=False, final=False):
            pe.wait_ge(qk_ready.sem, qk_ready.at(h + 1))
            if rotary:
                pe.wait_ge(qk_rest_ready.sem, qk_rest_ready.at(h + 1))
            if not first:
                pe.wait_ge(probsT_ready.sem, probsT_ready.at(3 * h))
                if not rotary:
                    pe.wait_ge(probsT_low.sem, probsT_low.at(3 * h))
            score()
            if not final:
                project(h + 1, 1 - par)
            elif ahead:
                ahead.route(pe)
            if first:
                pe.wait_ge(v_ready.sem, v_ready.at(1))
                if not rotary:
                    pe.wait_ge(v_low.sem, v_low.at(1))
            else:
                pe.wait_ge(y_ready.sem, y_ready.at(h))
                pe.wait_ge(y_low.sem, y_low.at(h))
            if not final:
                project_v(1 - par)
            pe.wait_ge(probs_ready.sem, probs_ready.at(h + 1))
            turn()
            if not first:
                pe.wait_ge(wo_split.sem, wo_split.at(h))
                add_head(1 - par)
            pe.wait_ge(v_ready.sem, v_ready.at(h + (1 if final else 2)))
            if not rotary:
                pe.wait_ge(v_low.sem, v_low.at(h + (1 if final else 2)))
            attend(h, par)

        pe.sem_inc(added.sem, 1)
        wait_xnT(m, pe)
        if rotary:
            clear_acc(m, pe)
        else:
            pe.wait_ge(rope_loaded.sem, rope_loaded.at(64))
            for h in range(2):
                nc.tensor.matmul(m.acc[:, h, :], one_row[:], bo_row[:].rearrange("o a d -> o (a d)"), start=True,
                                 stop=False, skip_group_check=True)
        project(0, 0)
        project_v(0)
        step(0, 0, first=True)
        with pe.Fori(0, HEADS // 2 - 1) as i:
            step(2 * i + 1, 1)
            step(2 * i + 2, 0)
        step(HEADS - 1, 1, final=True)
        pe.wait_ge(y_ready.sem, y_ready.at(HEADS))
        pe.wait_ge(y_low.sem, y_low.at(HEADS))
        pe.wait_ge(wo_split.sem, wo_split.at(HEADS))
        add_head(1)

    def vector(dve):
        def spread_qk(h, par, at):
            if not rotary:
                for which in range(2):
                    dve.wait_ge(qk_high.sem, qk_high.at(2 * h + which + 1))
                    last = nc.vector.scalar_tensor_tensor(
                        qkT_low[:, which], qk_psum[:, which], bias_of(h, which),
                        qkT[:, which].bitcast(FP32), ALU.add, ALU.subtract)
                last.then_inc(qk_ready.sem, 1)
                dve.wait_ge(v_ready.sem, v_ready.at(h + 1))
                flat = lambda a: a[:].rearrange("p t c -> p (t c)")
                nc.vector.tensor_tensor(flat(v_lows[par]), v_psum, flat(v[par]).bitcast(FP32), ALU.subtract)\
                  .then_inc(v_low.sem, 1)
                return
            dve.wait_ge(qk_projected.sem, qk_projected.at(h + 1))
            chain = Chain(dve, dve_chain, at)
            sin = lambda a: rope_sin[a:a + 32].unsqueeze(1).broadcast_to([32, 2, T])
            chain.link(nc.vector.tensor_tensor(rot[0:32, 0], qk_psum[32:64], sin(32), ALU.mult))
            chain.link(nc.vector.tensor_tensor(rot[32:64, 0], qk_psum[0:32], sin(0), ALU.mult))
            cos = rope_cos[:].unsqueeze(1).broadcast_to([64, 2, T])
            chain.link(nc.vector.tensor_tensor(rot[:, 1], qk_psum[0:64], cos, ALU.mult))
            chain.wait()
            nc.vector.tensor_tensor(qkT[0:64], rot[:, 0], rot[:, 1], ALU.add).then_inc(qk_ready.sem, 1)

        def softmax(h, at):
            chain = Chain(dve, dve_chain, at)
            for n, i in enumerate((3, 2, 1, 0)):
                if n < 3:
                    dve.wait_ge(scored.sem, scored.at(3 * h + n + 1))
                chain.link(nc.vector.reduce_max(row_max[:, i:i + 1], score_tile(i), AXIS.X))
            chain.wait()
            nc.vector.tensor_scalar(neg_max[:], row_max[:], -QK_SCALE, None, ALU.mult)\
              .then_inc(max_ready.sem, 1)
            dve.wait_ge(exp_ready.sem, exp_ready.at(h + 1))
            chain.all(nc.vector.reciprocal(row_inv[:], row_sum[:]))
            for i in (3, 2, 1, 0):
                last = nc.vector.tensor_scalar(prob_tile(i), prob_tile(i), row_inv[:, i:i + 1], None,
                                               ALU.mult)
            last.then_inc(probs_ready.sem, 1)

        def store_low(h):
            if not rotary:
                for k, (at, cols) in enumerate(TURNED_BANKS):
                    dve.wait_ge(probsT_ready.sem, probsT_ready.at(3 * h + k + 1))
                    nc.vector.tensor_tensor(probsT_lows[:, at:at + cols], m.banks[:, k, 0:cols],
                                            probsT[:, at:at + cols].bitcast(FP32), ALU.subtract)\
                      .then_inc(probsT_low.sem, 1)
            dve.wait_ge(y_ready.sem, y_ready.at(h + 1))
            if rotary:
                last = nc.vector.scalar_tensor_tensor(yT_low[:], v_psum, 1.0 / 3.0, yT[:].bitcast(FP32),
                                                      ALU.mult, ALU.subtract)
            else:
                last = nc.vector.scalar_tensor_tensor(yT_low[:], v_psum, bias_of(h, 2), yT[:].bitcast(FP32),
                                                      ALU.add, ALU.subtract)
            last.then_inc(y_low.sem, 1)

        per = CHAIN_QK + CHAIN_SOFTMAX
        if ahead:
            ahead.begin_vector(dve)
        dve.wait_ge(rope_loaded.sem, rope_loaded.at(32 if rotary else 64))
        spread_qk(0, 0, 0)
        with dve.Fori(0, HEADS // 2 - 1) as i:
            for par in range(2):
                h = 2 * i + par
                at = CHAIN_QK + per * h
                softmax(h, at)
                spread_qk(h + 1, 1 - par, at + CHAIN_SOFTMAX)
                store_low(h)
        softmax(HEADS - 2, CHAIN_QK + per * (HEADS - 2))
        spread_qk(HEADS - 1, 1, CHAIN_QK + per * (HEADS - 2) + CHAIN_SOFTMAX)
        store_low(HEADS - 2)
        softmax(HEADS - 1, CHAIN_QK + per * (HEADS - 1))
        if ahead:
            ahead.choose(dve)
        store_low(HEADS - 1)

    def scalar(act):
        def spread_rest(h, par):
            if rotary:
                act.wait_ge(qk_projected.sem, qk_projected.at(h + 1))
                nc.scalar.activation(qkT[64:P], qk_psum[64:P], ACT.Copy).then_inc(qk_rest_ready.sem, 1)
            else:
                act.wait_ge(qk_projected.sem, qk_projected.at(h + 1))
                for which in range(2):
                    nc.scalar.activation(qkT[:, which], qk_psum[:, which], ACT.Identity,
                                         bias=bias_of(h, which)).then_inc(qk_high.sem, 1)
            act.wait_ge(v_projected.sem, v_projected.at(h + 1))
            nc.scalar.activation(v[par][:].rearrange("p t c -> p (t c)"), v_psum, ACT.Copy)\
              .then_inc(v_ready.sem, 1)

        def exponentials(h):
            act.wait_ge(max_ready.sem, max_ready.at(h + 1))
            for i in (3, 2, 1, 0):
                last = nc.scalar.activation(prob_tile(i), score_tile(i), ACT.Exp, bias=neg_max[:, i:i + 1],
                                            scale=QK_SCALE, accum_out=row_sum[:, i:i + 1])
            last.then_inc(exp_ready.sem, 1)

        def store_turned(h):
            for k, (at, cols) in enumerate(TURNED_BANKS):
                act.wait_ge(turned.sem, turned.at(3 * h + k + 1))
                nc.scalar.activation(probsT[:, at:at + cols], m.banks[:, k, 0:cols], ACT.Copy)\
                  .then_inc(probsT_ready.sem, 1)

        def store_y(h):
            act.wait_ge(attended.sem, attended.at(h + 1))
            if rotary:
                nc.scalar.activation(yT[:], v_psum, ACT.Copy, scale=1.0 / 3.0).then_inc(y_ready.sem, 1)
            else:
                nc.scalar.activation(yT[:], v_psum, ACT.Identity, bias=bias_of(h, 2)).then_inc(y_ready.sem, 1)

        def high_wo(h, par):
            act.wait_ge(added.sem, added.at(h))
            nc.scalar.activation(parts[par][0][:, QKV:], raw[par][:, QKV:], ACT.Copy).then_inc(wo_high.sem, 1)

        def head(h, par, use=None):
            exponentials(h)
            spread_rest(h + 1, 1 - par)
            store_turned(h)
            if use is not None:
                high_qkv(act, h + 2, par, use)
            store_y(h)
            high_wo(h + 1, 1 - par)

        if ahead:
            ahead.begin_scalar(act)
        if not rotary:
            act.wait_ge(rope_loaded.sem, rope_loaded.at(64))
        spread_rest(0, 0)
        with act.Fori(0, HEADS // 2 - 1) as i:
            for par in range(2):
                head(2 * i + par, par, i + 2)
        head(HEADS - 2, 0)
        if ahead:
            ahead.first_high(act)
        exponentials(HEADS - 1)
        if ahead:
            ahead.second_high(act)
        store_turned(HEADS - 1)
        store_y(HEADS - 1)

    def gpsimd(pool):
        def lows(h, par):
            low_qkv(pool, h + 2, par)
            low_wo(pool, h + 1, 1 - par)

        if spline:
            spline.make(pool, lambda h: lows(h, h % 2) if h < HEADS - 2 else None)
        else:
            with pool.Fori(0, HEADS // 2 - 1) as i:
                for par in range(2):
                    lows(2 * i + par, par)
        low_wo(pool, HEADS - 1, 1)

    def close():
        for s, n in ((qk_projected, HEADS), (v_projected, HEADS), (scored, 3 * HEADS), (turned, 3 * HEADS),
                     (attended, HEADS), (added, HEADS + 1), (qk_ready, HEADS), (max_ready, HEADS), (exp_ready, HEADS),
                     (probs_ready, HEADS), (v_ready, HEADS), (probsT_ready, 3 * HEADS), (y_ready, HEADS),
                     (dve_chain, HEADS * (CHAIN_QK + CHAIN_SOFTMAX))):
            s.close(n)
        for s in (qkv_high, qkv_split, wo_high, wo_split, y_low):
            s.close(HEADS)
        if rotary:
            qk_rest_ready.close(HEADS)
            rope_loaded.close(32)
        else:
            rope_loaded.close(64)
            qk_high.close(2 * HEADS)
            v_low.close(HEADS)
            probsT_low.close(3 * HEADS)
        for s in loaded:
            s.close(16 * HEADS // 2)

    return (Stage(sync=first_sync, gpsimd=first_gpsimd), first_scalar,
            Stage(close, sync, tensor, vector, scalar, gpsimd))


def head_rows(dram, h):
    return dram[bass.ds(h, 1)].rearrange("a p f -> (a p) f")


class Hidden:

    def __init__(self, groups, cols, rows, experts, act):
        self.groups, self.cols, self.rows, self.experts, self.act = groups, cols, rows, experts, act
        self.one_bank = 2 * cols <= 512


class MlpSteps:

    def __init__(self, multiply, turn, add, activate, store_turned, store_low, gate, close, act_out, hidden):
        self.multiply, self.turn, self.add, self.activate = multiply, turn, add, activate
        self.store_turned, self.store_low, self.gate, self.close = store_turned, store_low, gate, close
        self.act_out, self.hidden = act_out, hidden


def gated_mlp_engines(m, shape, sb, first_bank, gate_up, down, scale_of, split, turned_banks=2):
    nc = m.nc
    gate_done, gated, hidden_ready = m.sig("gate_up_done"), m.sig("gated"), m.sig("hidden_ready")
    hidden_turned, hiddenT_ready, added = m.sig("hidden_turned"), m.sig("hiddenT_ready"), m.sig("group_added")
    F, R = shape.cols, len(shape.rows)
    act_out = [sb(f"act_out{i}", [P, F]) for i in range(2)]
    hidden = [sb(f"hidden{i}", [P, F]) for i in range(2)]
    hiddenT = [sb(f"hiddenT{i}", [P, R, P], FP32R if split else FP32) for i in range(2)]
    hiddenT_low = [sb(f"hiddenT_low{i}", [P, R, P], FP32R) for i in range(2)] if split else None
    low_ready = m.sig("hiddenT_low_ready")
    per_item = 1 if shape.one_bank else 2

    def gate_up_psum(par):
        if shape.one_bank:
            b = m.banks[:, first_bank + par, :]
            return b[:, 0:F], b[:, F:2 * F], b[:, 0:2 * F].rearrange("p (w f) -> p w f", w=2)
        b = first_bank + 2 * par
        return m.banks[:, b, 0:F], m.banks[:, b + 1, 0:F], None

    def turned_psum(par):
        return m.banks[:, first_bank + 2 * per_item + par % turned_banks, 0:R * P].rearrange("p (r c) -> p r c", r=R)

    def multiply(t, par, gpar):
        gate, up, both = gate_up_psum(par)
        if split:
            outs = [both] if both is not None else [gate, up]
            for w, out in enumerate(outs):
                for k in range(KD):
                    left = [part[:, k, t * P:(t + 1) * P] for part in m.xnT_parts]
                    right = [part if both is not None else part[:, w] for part in gate_up(gpar, k)]
                    last = exact_product(nc, out, left, right, k == 0, k == KD - 1)
            last.then_inc(gate_done.sem, 1)
            return
        if both is not None:
            for k in range(KD):
                last = nc.tensor.matmul(both, m.xnT[:, k, t * P:(t + 1) * P], gate_up(gpar, k),
                                        start=k == 0, stop=k == KD - 1)
        else:
            for w, out in enumerate((gate, up)):
                for k in range(KD):
                    last = nc.tensor.matmul(out, m.xnT[:, k, t * P:(t + 1) * P], gate_up(gpar, k)[:, w],
                                            start=k == 0, stop=k == KD - 1)
        last.then_inc(gate_done.sem, 1)

    def turn(pe, n, par):
        pe.wait_ge(hidden_ready.sem, hidden_ready.at(n + 1))
        if turned_banks == 1 and n:
            pe.wait_ge(hiddenT_ready.sem, hiddenT_ready.at(n))
            pe.wait_ge(low_ready.sem, low_ready.at(n))
        for r, rows in enumerate(shape.rows):
            last = nc.tensor.transpose(turned_psum(par)[0:rows, r], hidden[par][:, r * P:r * P + rows], m.ident[:])
        last.then_inc(hidden_turned.sem, 1)

    def add(pe, n, t, par, gpar):
        pe.wait_ge(hiddenT_ready.sem, hiddenT_ready.at(n + 1))
        if split:
            pe.wait_ge(low_ready.sem, low_ready.at(n + 1))
            for r, rows in enumerate(shape.rows):
                left = [hiddenT[par][0:rows, r], hiddenT_low[par][0:rows, r]]
                last = exact_product(nc, m.acc_tile(t), left, [part[0:rows] for part in down(gpar, r)],
                                     False, False, skip_group_check=True)
            last.then_inc(added.sem, 1)
            return
        for r, rows in enumerate(shape.rows):
            last = nc.tensor.matmul(m.acc_tile(t), hiddenT[par][0:rows, r], down(gpar, r)[0:rows],
                                    start=False, stop=False, skip_group_check=True)
        last.then_inc(added.sem, 1)

    def activate(act, n, par):
        act.wait_ge(gate_done.sem, gate_done.at(n + 1))
        nc.scalar.activation(act_out[par][:], gate_up_psum(par)[0], shape.act).then_inc(gated.sem, 1)

    def store_turned(act, n, par):
        act.wait_ge(hidden_turned.sem, hidden_turned.at(n + 1))
        whole = sum(r == P for r in shape.rows)
        last = nc.scalar.activation(hiddenT[par][:, 0:whole], turned_psum(par)[:, 0:whole], ACT.Copy)
        if whole < R:
            rows = shape.rows[-1]
            last = nc.scalar.activation(hiddenT[par][0:rows, whole], turned_psum(par)[0:rows, whole], ACT.Copy)
        last.then_inc(hiddenT_ready.sem, 1)

    def store_low(dve, n, par):
        dve.wait_ge(hiddenT_ready.sem, hiddenT_ready.at(n + 1))
        whole = sum(r == P for r in shape.rows)
        for rows, r in [(P, slice(0, whole))] + [(rows, slice(whole, R)) for rows in shape.rows[whole:]]:
            last = nc.vector.tensor_tensor(hiddenT_low[par][0:rows, r], turned_psum(par)[0:rows, r],
                                           hiddenT[par][0:rows, r].bitcast(FP32), ALU.subtract)
        last.then_inc(low_ready.sem, 1)

    def gate(dve, n, g, t, par):
        dve.wait_ge(gated.sem, gated.at(n + 1))
        up = gate_up_psum(par)[1]
        if scale_of is None:
            last = nc.vector.tensor_tensor(hidden[par][:], act_out[par][:], up, ALU.mult)
        else:
            cols = F // shape.experts
            for e in range(shape.experts):
                at = slice(e * cols, (e + 1) * cols)
                last = nc.vector.scalar_tensor_tensor(hidden[par][:, at], up[:, at], scale_of(g, t, e),
                                                      act_out[par][:, at], ALU.mult, ALU.mult)
        last.then_inc(hidden_ready.sem, 1)

    def close():
        n = NT * shape.groups
        for s in (gate_done, gated, hidden_ready, hidden_turned, hiddenT_ready, added):
            s.close(n)
        if split:
            low_ready.close(n)

    return MlpSteps(multiply, turn, add, activate, store_turned, store_low, gate, close, act_out, hidden)


class Ahead:

    def __init__(self, load, route, begin_vector, choose, begin_scalar, first_high, second_high):
        self.load, self.route, self.begin_vector, self.choose = load, route, begin_vector, choose
        self.begin_scalar, self.first_high, self.second_high = begin_scalar, first_high, second_high


def mixture(m, layer, ctx, with_table=False, merged=True):
    nc = m.nc
    E, TOP = (E0, TOP0) if layer == 0 else (E3, TOP3)
    shape = Hidden(GROUPS, F0, (P, P, P), 4, ACT.Silu) if layer == 0 else Hidden(GROUPS, F3, (P, P), 1, ACT.Gelu)
    F, R = shape.cols, len(shape.rows)
    experts_dram, router_dram = m.dram[f"experts{layer}"], m.dram[f"router{layer}"]
    experts_loaded = [m.sig(f"experts_loaded{i}") for i in range(2)]
    gu_high, gu_split, down_high, down_split = (m.sig("gu_high"), m.sig("gu_split"), m.sig("down_high"),
                                                m.sig("down_split"))
    loaded, routed, logits_in, exp_in = m.sig("router_loaded"), m.sig("routed"), m.sig("logits_in"), m.sig("route_exp")
    stepped, rooted = m.sig("route_var"), m.sig("route_root")
    scaled_router, square_step = m.sig("scaled_router"), m.sig("square_step")
    dve_chain = m.sig("route_chain")
    ITEMS = NT * GROUPS
    UNROLL = 2 * NT
    EP = E + 8 - TOP

    sb = m.local(ctx)
    GU = KD * 2 * F
    raw = [sb(f"experts{i}", [P, GU + R * D]) for i in range(2)]
    parts = [[sb(f"experts_{part}{i}", [P, GU + R * D], FP32R) for part in ("high", "low")] for i in range(2)]
    gu = [[a[:, 0:GU].rearrange("p (k w f) -> p k w f", k=KD, w=2) for a in pair] for pair in parts]
    dn = [[a[:, GU:].rearrange("p (r d) -> p r d", d=D) for a in pair] for pair in parts]
    router = sb("router", [P, KD, E])
    router_scale = sb("router_scale", [P, KD])
    per_expert = sb("per_expert", [P, E])
    logits, replaced = sb("logits", [P, NT, EP]), sb("replaced", [P, NT, EP])
    top = sb("top", [P, NT, 8])
    chosen, expd = sb("chosen", [P, NT, E]), sb("expd", [P, NT, E])
    weight = sb("weight", [P, NT, E])
    sums = sb("sums", [P, 4, NT])
    squares, square_sum = sb("squares", [P, D]), sb("square_sum", [P, NT])
    scale_of = lambda g, t, e: weight[:, t, bass.ds(g * shape.experts + e, 1)]
    mlp = gated_mlp_engines(
        m, shape, sb, 0, lambda gpar, k: [a[:, k] for a in gu[gpar]], lambda gpar, r: [a[:, r] for a in dn[gpar]],
        scale_of, True)
    multiply, turn, add = mlp.multiply, mlp.turn, mlp.add
    activate, store_turned, store_low, gate = mlp.activate, mlp.store_turned, mlp.store_low, mlp.gate
    added = m.sig("group_added")
    table = TableWeights(m, ctx) if with_table else None
    per_token = lambda a: a.unsqueeze(2).broadcast_to([P, NT, E])
    n_loads = 1 if layer == 0 else 3

    def load_router(sp):
        sp.dma_start(router[:], router_dram).then_inc(loaded.sem, 16)
        if layer == 3:
            sp.dma_start(router_scale[:], m.dram["router_scale"]).then_inc(loaded.sem, 16)
            sp.dma_start(per_expert[:], m.dram["per_expert"].broadcast_to([P, E])).then_inc(loaded.sem, 16)

    def sync(sp):
        def load(g, gpar):
            sp.dma_start(raw[gpar][:], head_rows(experts_dram, g)).then_inc(experts_loaded[gpar].sem, 16)

        if not merged:
            load_router(sp)
        if table:
            table.start(sp)
        for g in range(2):
            load(g, g)
            if table:
                table.load(sp, g, g)
        with sp.Fori(0, GROUPS // 2 - 1) as i:
            for gpar in range(2):
                g = 2 * i + gpar
                sp.wait_ge(gu_split.sem, gu_split.at(g + 1))
                sp.wait_ge(down_split.sem, down_split.at(g + 1))
                load(g + 2, gpar)
                if table:
                    sp.wait_ge(table.read.sem, table.read.at(g + 1))
                    table.load(sp, g + 2, gpar)

    def route(pe):
        if layer == 0:
            pe.wait_ge(loaded.sem, loaded.at(16))
        else:
            pe.wait_ge(scaled_router.sem, scaled_router.at(1))
        for t in range(NT):
            for k in range(KD):
                last = nc.tensor.matmul(m.banks[:, 3, t * E:(t + 1) * E], m.xnT[:, k, t * P:(t + 1) * P],
                                        router[:, k], start=k == 0, stop=k == KD - 1)
        last.then_inc(routed.sem, 1)

    def tensor(pe):
        pe.sem_inc(added.sem, 1)
        if not merged:
            route(pe)

        def step(n, c, pair):
            if c < UNROLL:
                gpar, t, nxt = c // NT, c % NT, (c + 1) % UNROLL
            if n is not None and not (isinstance(n, int) and n == ITEMS - 1):
                if nxt % NT == 0:
                    pe.wait_ge(gu_split.sem, gu_split.at(2 * pair + (3 if nxt == 0 else 2)))
                multiply(nxt % NT, nxt % 2, nxt // NT)
            turn(pe, n, c % 2)
            if not (isinstance(n, int) and n == 0):
                prev = (c - 1) % UNROLL
                if prev % NT == 0:
                    pe.wait_ge(down_split.sem, down_split.at(2 * pair + 1 + prev // NT))
                add(pe, n - 1, prev % NT, prev % 2, prev // NT)

        pe.wait_ge(gu_split.sem, gu_split.at(1))
        multiply(0, 0, 0)
        pe.wait_ge(logits_in.sem, logits_in.at(1))
        step(0, 0, 0)
        with pe.Fori(0, GROUPS // 2 - 1) as i:
            for c in range(1, UNROLL + 1):
                step(UNROLL * i + c, c % UNROLL, i + c // UNROLL)
        for n in range(ITEMS - UNROLL + 1, ITEMS):
            step(n, n % UNROLL, n // UNROLL)
        add(pe, ITEMS - 1, NT - 1, 1, 1)

    chains = []

    def begin_vector(dve):
        chain = Chain(dve, dve_chain)
        chains.append(chain)
        chain.link(nc.vector.memset(logits[:, :, E:], -3e38))
        dve.wait_ge(loaded.sem, loaded.at(16 * n_loads))
        if layer == 3:
            for k in range(KD):
                last = nc.vector.tensor_scalar(router[:, k], router[:, k], router_scale[:, k:k + 1],
                                               float(D) ** -0.5, ALU.mult, ALU.mult)
            last.then_inc(scaled_router.sem, 1)
            dve.wait_ge(square_step.sem, square_step.at(NT))
            nc.vector.tensor_scalar(m.rs[:, 0], square_sum[:], 1.0 / D, 1e-6, ALU.mult, ALU.add)\
              .then_inc(stepped.sem, 1)
            dve.wait_ge(stepped.sem, stepped.at(1))
            dve.wait_ge(rooted.sem, rooted.at(1))
            reciprocal_root(nc, chain, m.rs)

    def choose(dve):
        chain = chains[0]
        dve.wait_ge(routed.sem, routed.at(1))
        src = m.banks[:, 3, 0:NT * E].rearrange("p (t e) -> p t e", t=NT)
        if layer == 0:
            chain.all(nc.vector.tensor_copy(logits[:, :, 0:E], src))
        else:
            chain.all(nc.vector.tensor_tensor(logits[:, :, 0:E], src, per_token(m.rs[:, 3]), ALU.mult))
        for t in range(NT):
            chain.link(nc.vector.max(top[:, t], logits[:, t]))
        chain.wait()
        chain.link(nc.vector.tensor_tensor(expd[:], logits[:, :, 0:E],
                                           top[:, :, 0:1].broadcast_to([P, NT, E]), ALU.subtract))
        chain.wait()
        chain.all(nc.vector.memset(top[:, :, TOP:], -3e38))
        for t in range(NT):
            chain.link(nc.vector.match_replace(replaced[:, t], top[:, t], logits[:, t], 3e38))
        chain.wait()
        nc.vector.tensor_tensor(chosen[:], replaced[:, :, 0:E], logits[:, :, 0:E], ALU.not_equal)\
          .then_inc(logits_in.sem, 1)

    def vector(dve):
        if not merged:
            begin_vector(dve)
            choose(dve)
        chain = chains[0]
        dve.wait_ge(exp_in.sem, exp_in.at(1))
        dve.wait_ge(logits_in.sem, logits_in.at(1))
        if layer == 3:
            chain.all(nc.vector.reduce_sum(sums[:, 0], expd[:], AXIS.X))
            chain.all(nc.vector.reciprocal(sums[:, 1], sums[:, 0]))
            chain.all(nc.vector.tensor_tensor(expd[:], expd[:], per_token(sums[:, 1]), ALU.mult))
        chain.all(nc.vector.tensor_tensor(chosen[:], chosen[:], expd[:], ALU.mult))
        chain.all(nc.vector.reduce_sum(sums[:, 0], chosen[:], AXIS.X))
        if layer == 3:
            chain.all(nc.vector.tensor_scalar(sums[:, 0], sums[:, 0], 1e-12, None, ALU.max))
        chain.all(nc.vector.reciprocal(sums[:, 1], sums[:, 0]))
        chain.all(nc.vector.tensor_tensor(weight[:], chosen[:], per_token(sums[:, 1]), ALU.mult))
        if layer == 3:
            chain.all(nc.vector.tensor_tensor(weight[:], weight[:],
                                              per_expert[:].unsqueeze(1).broadcast_to([P, NT, E]), ALU.mult))
        if table:
            table.first(dve)

        def step(n, c, pair):
            nxt, nxt_pair = (c + 1) % UNROLL, pair + (c + 1) // UNROLL
            if not (isinstance(n, int) and n == ITEMS - 1):
                gate(dve, n + 1, 2 * nxt_pair + nxt // NT, nxt % NT, nxt % 2)
            store_low(dve, n, c % 2)
            if table:
                table.part(dve, 2 * pair + c // NT, c // NT, pair, c % NT)

        gate(dve, 0, 0, 0, 0)
        with dve.Fori(0, GROUPS // 2 - 1) as i:
            for c in range(UNROLL):
                step(UNROLL * i + c, c, i)
        for n in range(ITEMS - UNROLL, ITEMS):
            step(n, n % UNROLL, n // UNROLL)
        dve_chain.close(chain.n)

    def high_gu(act, g, gpar, use):
        act.wait_ge(experts_loaded[gpar].sem, experts_loaded[gpar].at(use))
        nc.scalar.activation(parts[gpar][0][:, 0:GU], raw[gpar][:, 0:GU], ACT.Copy)\
          .then_inc(gu_high.sem, 1)

    def high_down(act, g, gpar):
        if not (isinstance(g, int) and g < 2):
            act.wait_ge(added.sem, added.at(NT * (g - 1) + 1))
        nc.scalar.activation(parts[gpar][0][:, GU:], raw[gpar][:, GU:], ACT.Copy)\
          .then_inc(down_high.sem, 1)

    def first_high(act):
        high_gu(act, 0, 0, 16)
        high_down(act, 0, 0)

    def second_high(act):
        high_gu(act, 1, 1, 16)

    def begin_scalar(act):
        if layer == 3:
            act.wait_ge(m.sig("ln_normed").sem, m.sig("ln_normed").at(NT))
            for t in range(NT):
                last = nc.scalar.activation(squares[:], m.xn[:, t], ACT.Square,
                                            accum_out=square_sum[:, t:t + 1])
                last.then_inc(square_step.sem, 1)
                act.wait_ge(square_step.sem, square_step.at(t + 1))
            act.wait_ge(stepped.sem, stepped.at(1))
            nc.scalar.activation(m.rs[:, 1], m.rs[:, 0], ACT.Sqrt).then_inc(rooted.sem, 1)

    def scalar(act):
        def step_act(n, c, pair, final=False):
            if not (final and n == ITEMS - 1):
                activate(act, n + 1, (c + 1) % 2)
            store_turned(act, n, c % 2)
            if c == 1:
                high_down(act, 2 * pair + 1, 1)
            if not final:
                if c == 3:
                    high_gu(act, 2 * pair + 2, 0, 16 * (pair + 2))
                if c == 5:
                    high_down(act, 2 * pair + 2, 0)
                if c == 7:
                    high_gu(act, 2 * pair + 3, 1, 16 * (pair + 2))

        if not merged:
            begin_scalar(act)
            first_high(act)
            second_high(act)
        act.wait_ge(logits_in.sem, logits_in.at(1))
        nc.scalar.activation(expd[:], expd[:], ACT.Exp).then_inc(exp_in.sem, 1)

        activate(act, 0, 0)
        with act.Fori(0, GROUPS // 2 - 1) as i:
            for c in range(UNROLL):
                step_act(UNROLL * i + c, c, i)
        for n in range(ITEMS - UNROLL, ITEMS):
            step_act(n, n % UNROLL, n // UNROLL, final=True)

    def gpsimd(pool):
        def low(columns, high, split, g, gpar):
            pool.wait_ge(high.sem, high.at(g + 1))
            nc.gpsimd.tensor_tensor(parts[gpar][1][:, columns], raw[gpar][:, columns],
                                    parts[gpar][0][:, columns].bitcast(FP32), ALU.subtract)\
              .then_inc(split.sem, 1)

        low_gu = lambda g, gpar: low(slice(0, GU), gu_high, gu_split, g, gpar)
        low_down = lambda g, gpar: low(slice(GU, GU + R * D), down_high, down_split, g, gpar)
        low_gu(0, 0)
        low_down(0, 0)
        low_gu(1, 1)
        with pool.Fori(0, GROUPS // 2 - 1) as i:
            if table:
                table.leaves_of(pool, 2 * i, 0)
            low_down(2 * i + 1, 1)
            low_gu(2 * i + 2, 0)
            if table:
                table.leaves_of(pool, 2 * i + 1, 1)
            low_down(2 * i + 2, 0)
            low_gu(2 * i + 3, 1)
        if table:
            table.leaves_of(pool, GROUPS - 2, 0)
        low_down(GROUPS - 1, 1)
        if table:
            table.leaves_of(pool, GROUPS - 1, 1)

    def close():
        mlp.close()
        added.close(1)
        if table:
            table.close()
        loaded.close(16 * n_loads)
        for s in (routed, logits_in, exp_in):
            s.close(1)
        if layer == 3:
            stepped.close(1)
            rooted.close(1)
            scaled_router.close(1)
            square_step.close(NT)
        for s in experts_loaded:
            s.close(16 * GROUPS // 2)
        for s in (gu_high, gu_split, down_high, down_split):
            s.close(GROUPS)

    ahead = Ahead(load_router, route, begin_vector, choose, begin_scalar, first_high, second_high)
    return Stage(close, sync, tensor, vector, scalar, gpsimd), ahead


def state_space(m, b, ctx):
    nc, dram = m.nc, m.dram
    loaded, in_weights = m.sig("ss_loaded"), m.sig("ss_in_loaded")
    square_step, stepped, rooted = m.sig("square_step"), m.sig("rms_var"), m.sig("rms_root")
    scaled, turned, xmT_ready = m.sig("rms_scaled"), m.sig("rms_turned"), m.sig("xmT_ready")
    projected, xs_ready, z_ready = m.sig("ss_projected"), m.sig("xs_ready"), m.sig("z_ready")
    conv_ready, u_ready = m.sig("conv_ready"), m.sig("u_ready")
    low_rank, dt_in, bc_split = m.sig("low_rank"), m.sig("dt_in"), m.sig("bc_split")
    b_spread, c_spread, b_stored, c_stored = m.sig("b_spread"), m.sig("c_spread"), m.sig("b_stored"), m.sig("c_stored")
    first_tap, padded = m.sig("first_tap"), m.sig("xs_padded")
    dt_done, dt_parts = m.sig("dt_done"), m.sig("dt_parts")
    softplus_step, delta_ready = m.sig("softplus_step"), m.sig("delta_ready")
    decay_ready, scanned, product_ready, summed = (m.sig("decay_ready"), m.sig("scanned"), m.sig("product_ready"),
                                                   m.sig("summed"))
    y_taken, gated_y, joined = m.sig("y_taken"), m.sig("gated_y"), m.sig("joined")
    dve_chain, rms_chain = m.sig("dve_chain"), m.sig("rms_chain")
    shape = Hidden(KC, D, (P, P), 1, ACT.Silu)
    DECAYS, INFLOWS, PRODUCTS = 4, 4, 3
    STEPS, EARLY, BESIDE = KC * NS, KC, (NT - 1) * KC
    step_of = lambda item, after: min(5 * item + after, STEPS - 1)
    items_at = lambda step, after: [item for item in range(BESIDE) if step_of(item, after) == step]
    MULTIPLY, GATE, TURN, ADD, TANH, STORE = 0, 3, 4, 6, 5, 8
    CLOSE = 3
    inflow_ready = m.sig("inflow_ready")

    sb = m.local(ctx)
    xp = sb("xp", [P, KC, T + TAPS - 1])
    u, silu_z, delta = sb("u", [P, KC, T]), sb("silu_z", [P, KC, T]), sb("delta", [P, KC, T])
    Bs, Cs = sb("Bs", [P, NS, T]), sb("Cs", [P, NS, T])
    rings = sb("rings", [P, DECAYS + INFLOWS + PRODUCTS, T])
    decay, inflow, product = rings[:, 0:DECAYS], rings[:, DECAYS:DECAYS + INFLOWS], rings[:, DECAYS + INFLOWS:]
    state = sb("state", [P, 3, T])
    yg = sb("yg", [P, T])
    w_out = sb("w_out", [P, KC, D])
    split = sb("split", [3 * 2 * NS, T], BF16)
    mid = sb("mid", [2 * NS, T], BF16)
    vec = sb("vec", [P, KC, 7])
    w_norm, A = sb("w_norm", [P, KD]), sb("A", [P, KC, NS])
    root = sb("root", [P, 6, NT])
    square_sum = sb("square_sum", [P, NT])
    xm = decay[:, 0:2].rearrange("p a t -> p (a t)").rearrange("p (t d) -> p t d", t=NT)
    xmT, rank_in = decay[:, 2:4], yg
    w_xp = product.rearrange("p a t -> p (a t)")[:, 0:KC * (RANK + 2 * NS)]
    w_xp, w_dt = w_xp.rearrange("p (k c) -> p k c", k=KC), Bs[:, NS - 1]
    squares, rest = state[:, 0, 0:D], state[0:2 * NS, 1]
    select = inflow[0:6 * NS].rearrange("p a t -> p (a t)").bitcast(BF16).rearrange("p (r c) -> p r c", c=P)
    w_in = Cs[:, NS - 4:].rearrange("p a t -> p (a t)").rearrange("p (k c) -> p k c", k=KD)
    du, conv = xp[:, :, 0:T], delta
    mlp = gated_mlp_engines(
        m, shape, sb, 0, lambda g, k: m.spline_gu[:, k, :, bass.ds(g * D, D)],
        lambda g, r: m.spline_down[:, bass.ds(2 * g + r, 1), :].rearrange("p a d -> p (a d)"), None, False)
    multiply, turn, add = mlp.multiply, mlp.turn, mlp.add
    activate, store_turned, gate = mlp.activate, mlp.store_turned, mlp.gate
    act_out, hidden = mlp.act_out, mlp.hidden
    gated, hidden_ready, gate_done = m.sig("gated"), m.sig("hidden_ready"), m.sig("gate_up_done")
    y_psum = lambda c: m.banks[:, 4 + c % 2, :]
    loads = [(w_xp, dram["w_xp"]), (w_dt, dram["w_dt"]), (w_out[:], dram["w_out"]),
             (select, dram["select"]), (vec[:], dram["ss_vec"]), (w_norm[:], dram["w_norm"]),
             (A[:], dram["a_log"])]

    def sync(sp):
        sp.dma_start(w_in, dram["w_in"]).then_inc(in_weights.sem, 16)
        for dst, src in loads:
            sp.dma_start(dst, src).then_inc(loaded.sem, 16)

    def tensor(pe):
        wait_xnT(m, pe)
        clear_acc(m, pe)
        early = NT - 1
        multiply(early, 0, 0)
        for k in range(KD):
            for t in range(NT):
                pe.wait_ge(scaled.sem, scaled.at(t + 1))
                last = nc.tensor.transpose(m.banks[:, 4 + k, t * P:(t + 1) * P], xm[:, t, k * P:(k + 1) * P],
                                           m.ident[:])
            last.then_inc(turned.sem, 1)
        multiply(early, 1, 1)
        pe.wait_ge(in_weights.sem, in_weights.at(16))
        pe.wait_ge(xmT_ready.sem, xmT_ready.at(KD))

        def project(c):
            if c >= 2:
                if c - 2 < KC:
                    pe.wait_ge(xs_ready.sem, xs_ready.at(c - 1))
                else:
                    pe.wait_ge(z_ready.sem, z_ready.at(c - 1 - KC))
            for k in range(KD):
                last = nc.tensor.matmul(m.banks[:, 4 + c % 2, :], w_in[:, k, c * P:(c + 1) * P], xmT[:, k],
                                        start=k == 0, stop=k == KD - 1)
            last.then_inc(projected.sem, 1)

        for c in range(KC):
            project(c)
            turn(pe, c, c % 2)
            if c:
                add(pe, c - 1, early, (c - 1) % 2, c - 1)
            if c + 2 < EARLY:
                multiply(early, c % 2, c + 2)
        add(pe, EARLY - 1, early, (EARLY - 1) % 2, EARLY - 1)
        project(KC)
        project(KC + 1)
        pe.wait_ge(loaded.sem, loaded.at(16 * len(loads)))
        for k in range(KC):
            pe.wait_ge(u_ready.sem, u_ready.at(k + 1))
            nc.tensor.matmul(m.banks[:, 0, :], w_xp[:, k, 0:RANK], u[:, k], start=k == 0, stop=k == KC - 1)
            last = nc.tensor.matmul(m.banks[0:2 * NS, 1, :], w_xp[:, k, RANK:], u[:, k],
                                    start=k == 0, stop=k == KC - 1)
        last.then_inc(low_rank.sem, 1)
        project(KC + 2)
        project(KC + 3)
        pe.wait_ge(dt_in.sem, dt_in.at(1))
        pe.wait_ge(z_ready.sem, z_ready.at(KC))
        for c in range(KC):
            if c >= 2:
                pe.wait_ge(dt_parts.sem, dt_parts.at(c - 1))
            nc.tensor.matmul(m.banks[:, 4 + c % 2, :], w_dt[:, c * P:(c + 1) * P], rank_in[:],
                             start=True, stop=True).then_inc(dt_done.sem, 1)
        pe.wait_ge(bc_split.sem, bc_split.at(1))
        for which, stored, done in ((1, c_stored, c_spread), (0, b_stored, b_spread)):
            for n in range(NS):
                if n >= 2:
                    pe.wait_ge(stored.sem, stored.at(n - 1))
                nc.tensor.matmul(m.banks[:, 2 * which + n % 2, :], select[:, which * NS + n, :], split[:],
                                 start=True, stop=True).then_inc(done.sem, 1)
        pe.wait_ge(b_stored.sem, b_stored.at(NS))
        pe.wait_ge(c_stored.sem, c_stored.at(NS))
        pe.wait_ge(dt_parts.sem, dt_parts.at(KC))
        pe.sem_inc(summed.sem, PRODUCTS)

        def join(c):
            pe.wait_ge(gated_y.sem, gated_y.at(c + 1))
            for t in range(NT):
                last = nc.tensor.matmul(m.acc_tile(t), yg[:, t * P:(t + 1) * P], w_out[:, c],
                                        start=False, stop=False, skip_group_check=True)
            last.then_inc(joined.sem, 1)

        for step in range(STEPS):
            c, n = divmod(step, NS)
            if c >= 2 and n == 0:
                pe.wait_ge(y_taken.sem, y_taken.at(c - 1))
            pe.wait_ge(product_ready.sem, product_ready.at(step + 1))
            nc.tensor.matmul(y_psum(c), m.ident[:], product[:, step % PRODUCTS], start=n == 0, stop=n == NS - 1)\
              .then_inc(summed.sem, 1)
            if c and n == CLOSE + 1:
                join(c - 1)
            for item in items_at(step, TURN):
                turn(pe, EARLY + item, item % 2)
            for item in items_at(step, ADD):
                add(pe, EARLY + item, item % 3, item % 2, item // 3)
            for item in items_at(step, MULTIPLY):
                multiply(item % 3, item % 2, item // 3)
        join(KC - 1)

    def mean_square(act):
        for t in range(NT):
            act.wait_ge(m.sig("ln_normed").sem, m.sig("ln_normed").at(t + 1))
            nc.scalar.activation(squares, m.xn[:, t], ACT.Square, accum_out=square_sum[:, t:t + 1])\
              .then_inc(square_step.sem, 1)
            act.wait_ge(square_step.sem, square_step.at(t + 1))
        act.wait_ge(stepped.sem, stepped.at(1))
        nc.scalar.activation(root[:, 1], root[:, 0], ACT.Sqrt).then_inc(rooted.sem, 1)

    def scalar(act):
        act.wait_ge(loaded.sem, loaded.at(16 * len(loads)))
        for k in range(KD):
            act.wait_ge(turned.sem, turned.at(k + 1))
            nc.scalar.activation(xmT[:, k], m.banks[:, 4 + k, :], ACT.Copy, scale=w_norm[:, k:k + 1])\
              .then_inc(xmT_ready.sem, 1)
        activate(act, 0, 0)
        activate(act, 1, 1)
        act.wait_ge(padded.sem, padded.at(1))
        for c in range(KC):
            act.wait_ge(projected.sem, projected.at(c + 1))
            nc.scalar.activation(xp[:, c, TAPS - 1:], m.banks[:, 4 + c % 2, :], ACT.Copy).then_inc(xs_ready.sem, 1)
            act.wait_ge(xs_ready.sem, xs_ready.at(c + 1))
            nc.scalar.activation(conv[:, c], xp[:, c, 0:T], ACT.Identity, scale=vec[:, c, 0:1], bias=vec[:, c, 4:5])\
              .then_inc(first_tap.sem, 1)
            store_turned(act, c, c % 2)
            if c + 2 < EARLY:
                activate(act, c + 2, c % 2)

        def silu_u(c):
            act.wait_ge(conv_ready.sem, conv_ready.at(c + 1))
            nc.scalar.activation(u[:, c], conv[:, c], ACT.Silu).then_inc(u_ready.sem, 1)

        def gate_z(c):
            act.wait_ge(projected.sem, projected.at(KC + c + 1))
            nc.scalar.activation(silu_z[:, c], m.banks[:, 4 + c % 2, :], ACT.Silu).then_inc(z_ready.sem, 1)

        for c in (0, 1):
            silu_u(c)
        for c in (0, 1):
            gate_z(c)
        for c in (2, 3):
            silu_u(c)
        act.wait_ge(low_rank.sem, low_rank.at(1))
        nc.scalar.activation(rank_in[:], m.banks[:, 0, :], ACT.Copy).then_inc(dt_in.sem, 1)
        for c in (2, 3):
            gate_z(c)
        for c in range(KC):
            act.wait_ge(dt_done.sem, dt_done.at(c + 1))
            v = m.banks[:, 4 + c % 2, :]
            nc.scalar.activation(delta[:, c], v, ACT.Relu, bias=vec[:, c, 5:6])
            nc.scalar.activation(du[:, c], v, ACT.Abs, bias=vec[:, c, 5:6]).then_inc(dt_parts.sem, 1)
        act.wait_ge(dt_parts.sem, dt_parts.at(KC))
        nc.scalar.activation(du, du, ACT.Exp, scale=-1.0).then_inc(softplus_step.sem, 1)
        nc.scalar.activation(A[:], A[:], ACT.Exp).then_inc(softplus_step.sem, 1)
        act.wait_ge(softplus_step.sem, softplus_step.at(2))
        nc.scalar.activation(du, du, ACT.Ln, bias=1.0).then_inc(softplus_step.sem, 1)
        for n in range(NS):
            act.wait_ge(b_spread.sem, b_spread.at(n + 1))
            nc.scalar.activation(Bs[:, n], m.banks[:, n % 2, :], ACT.Copy).then_inc(b_stored.sem, 1)
        act.wait_ge(delta_ready.sem, delta_ready.at(1))
        for step in range(STEPS):
            c, n = divmod(step, NS)
            act.wait_ge(scanned.sem, scanned.at(step + 1))
            nc.scalar.activation(decay[:, step % DECAYS], delta[:, c], ACT.Exp, scale=A[:, c, n:n + 1])\
              .then_inc(decay_ready.sem, 1)
            for item in items_at(step, TANH):
                act.wait_ge(gate_done.sem, gate_done.at(EARLY + item + 1))
                nc.scalar.activation(act_out[item % 2][:], m.banks[:, item % 2, 0:D], ACT.Tanh, scale=0.5)\
                  .then_inc(gated.sem, 1)
            for item in items_at(step, STORE):
                store_turned(act, EARLY + item, item % 2)

    def inverse_root(dve):
        chain = Chain(dve, rms_chain)
        dve.wait_ge(square_step.sem, square_step.at(NT))
        nc.vector.tensor_scalar(root[:, 0], square_sum[:], 1.0 / D, 1e-5, ALU.mult, ALU.add)\
          .then_inc(stepped.sem, 1)
        dve.wait_ge(stepped.sem, stepped.at(1))
        dve.wait_ge(rooted.sem, rooted.at(1))
        reciprocal_root(nc, chain, root)
        rms_chain.close(chain.n)

    def vector(dve):
        chain = Chain(dve, dve_chain)
        nc.vector.memset(xp[:, :, 0:TAPS - 1], 0.0).then_inc(padded.sem, 1)
        for t in range(NT):
            nc.vector.tensor_scalar(xm[:, t], m.xn[:, t], root[:, 3, t:t + 1], None, ALU.mult)\
              .then_inc(scaled.sem, 1)
        gate(dve, 0, None, NT - 1, 0)
        gate(dve, 1, None, NT - 1, 1)
        dve.wait_ge(loaded.sem, loaded.at(16 * len(loads)))
        for c in range(KC):
            dve.wait_ge(first_tap.sem, first_tap.at(c + 1))
            for j in range(1, TAPS):
                last = nc.vector.scalar_tensor_tensor(conv[:, c], xp[:, c, j:j + T], vec[:, c, j:j + 1],
                                                      conv[:, c], ALU.mult, ALU.add)
                if j < TAPS - 1:
                    chain.all(last)
            last.then_inc(conv_ready.sem, 1)
            if c + 2 < EARLY:
                gate(dve, c + 2, None, NT - 1, c % 2)
        dve.wait_ge(low_rank.sem, low_rank.at(1))
        bc = m.banks[0:2 * NS, 1, :]
        chain.all(nc.vector.tensor_copy(split[0:2 * NS], bc))
        chain.all(nc.vector.tensor_tensor(rest, bc, split[0:2 * NS], ALU.subtract))
        chain.all(nc.vector.tensor_copy(mid[:], rest))
        chain.link(nc.vector.tensor_copy(split[2 * NS:4 * NS], mid[:]))
        chain.link(nc.vector.tensor_tensor(split[4 * NS:6 * NS], rest, mid[:], ALU.subtract))
        chain.wait()
        nc.vector.memset(rest[:, 0:1], 0.0).then_inc(bc_split.sem, 1)
        for n in range(NS):
            dve.wait_ge(c_spread.sem, c_spread.at(n + 1))
            nc.vector.tensor_copy(Cs[:, n], m.banks[:, 2 + n % 2, :]).then_inc(c_stored.sem, 1)
        dve.wait_ge(softplus_step.sem, softplus_step.at(3))
        chain.link(nc.vector.tensor_scalar(A[:], A[:], -1.0, None, ALU.mult))
        chain.all(nc.vector.tensor_tensor(delta[:], delta[:], du, ALU.add))
        chain.all(nc.vector.tensor_tensor(du, delta[:], u[:], ALU.mult))
        nc.vector.memset(rest[:, 0:1], 0.0).then_inc(delta_ready.sem, 1)
        dve.wait_ge(c_stored.sem, c_stored.at(NS))
        dve.wait_ge(b_stored.sem, b_stored.at(NS))
        dve.sem_inc(scanned.sem, DECAYS)

        def scan(step):
            dve.wait_ge(inflow_ready.sem, inflow_ready.at(step + 1))
            dve.wait_ge(decay_ready.sem, decay_ready.at(step + 1))
            if step >= 3:
                dve.wait_ge(product_ready.sem, product_ready.at(step - 2))
            nc.vector.tensor_tensor_scan(state[:, step % 3], decay[:, step % DECAYS], inflow[:, step % INFLOWS],
                                         0.0, ALU.mult, ALU.add).then_inc(scanned.sem, 1)

        def take_y(c):
            dve.wait_ge(summed.sem, summed.at(NS * c + NS + PRODUCTS))
            nc.vector.scalar_tensor_tensor(yg[:], u[:, c], vec[:, c, 6:7], y_psum(c), ALU.mult, ALU.add)\
              .then_inc(y_taken.sem, 1)
            dve.wait_ge(y_taken.sem, y_taken.at(c + 1))
            nc.vector.tensor_tensor(yg[:], yg[:], silu_z[:, c], ALU.mult).then_inc(gated_y.sem, 1)

        scan(0)
        for step in range(STEPS):
            c, n = divmod(step, NS)
            if step + 1 < STEPS:
                scan(step + 1)
            dve.wait_ge(scanned.sem, scanned.at(step + 1 + DECAYS))
            dve.wait_ge(summed.sem, summed.at(step + 1))
            nc.vector.tensor_tensor(product[:, step % PRODUCTS], state[:, step % 3], Cs[:, n], ALU.mult)\
              .then_inc(product_ready.sem, 1)
            if c and n == CLOSE:
                take_y(c - 1)
            for item in items_at(step, GATE):
                dve.wait_ge(gated.sem, gated.at(EARLY + item + 1))
                chain.all(nc.vector.scalar_tensor_tensor(act_out[item % 2][:], act_out[item % 2][:], 1.0,
                                                         m.banks[:, item % 2, D:2 * D], ALU.add, ALU.mult))
                nc.vector.scalar_tensor_tensor(hidden[item % 2][:], act_out[item % 2][:], 0.5,
                                               m.banks[:, item % 2, 0:D], ALU.mult, ALU.mult)\
                  .then_inc(hidden_ready.sem, 1)
        take_y(KC - 1)
        dve_chain.close(chain.n)

    def gpsimd(pool):
        pool.wait_ge(m.sig("ln_normed").sem, m.sig("ln_normed").at(NT))
        nc.gpsimd.tensor_tensor(m.x_of[b][:], m.x_of[b][:], m.xn[:], ALU.add)
        pool.wait_ge(delta_ready.sem, delta_ready.at(1))
        pool.wait_ge(b_stored.sem, b_stored.at(NS))
        pool.wait_ge(c_stored.sem, c_stored.at(NS))
        for step in range(STEPS):
            c, n = divmod(step, NS)
            pool.wait_ge(scanned.sem, scanned.at(step + 1))
            nc.gpsimd.tensor_tensor(inflow[:, step % INFLOWS], du[:, c], Bs[:, n], ALU.mult)\
              .then_inc(inflow_ready.sem, 1)

    def close():
        mlp.close()
        inflow_ready.close(KC * NS)
        for s, n in ((in_weights, 16), (loaded, 16 * len(loads)), (square_step, NT), (stepped, 1), (rooted, 1),
                     (scaled, NT), (turned, KD), (xmT_ready, KD), (projected, 2 * KC), (xs_ready, KC),
                     (z_ready, KC), (conv_ready, KC), (u_ready, KC), (low_rank, 1), (dt_in, 1), (bc_split, 1),
                     (b_spread, NS), (c_spread, NS), (first_tap, KC), (padded, 1), (b_stored, NS), (c_stored, NS),
                     (dt_done, KC), (dt_parts, KC),
                     (softplus_step, 3), (delta_ready, 1), (decay_ready, KC * NS), (scanned, KC * NS + DECAYS),
                     (product_ready, KC * NS), (summed, KC * NS + PRODUCTS), (y_taken, KC), (gated_y, KC),
                     (joined, KC)):
            s.close(n)

    return Stage(close, sync, tensor, vector, scalar, gpsimd), mean_square, inverse_root


def clear_acc(m, pe):
    for h in range(2):
        m.nc.tensor.matmul(m.acc[:, h, :], m.ident_bf[0:1], m.zero_row[:], start=True, stop=False,
                           skip_group_check=True)


def linear_recurrence(m, b, ctx):
    nc, dram = m.nc, m.dram
    loaded, projected = m.sig("lru_loaded"), m.sig("lru_projected")
    h_ready, stepped = m.sig("h_ready"), m.sig("lru_stepped")
    shape = Hidden(2, F2, F2_ROWS, 1, ACT.Silu)
    ITEMS = 2 * NT
    N2 = 2 * STATES
    STEPS = 9
    sb = m.local(ctx)
    w_b, w_c = sb("w_b", [P, KD, N2]), sb("w_c", [N2, D])
    h = sb("h", [N2, T])
    GU = KD * 2 * INTER2
    pieces = [(0, GU // 2), (GU // 2, GU), (GU, LUT_COLS)]
    parts = [sb(f"lut_{part}", [P, LUT_COLS], FP32R) for part in ("high", "low")]
    piece_high, piece_split = m.sig("lut_high"), m.sig("lut_split")
    extra, skip = sb("extra", [P, NT, D]), sb("skip", [P, D])
    skip_loaded, skip_step = m.sig("skip_loaded"), m.sig("skip_step")
    gu_w = [a[:, 0:GU].rearrange("p (g k w f) -> p g k w f", g=2, k=KD, w=2) for a in parts]
    down_w = [a[:, GU:].rearrange("p (r d) -> p r d", d=D) for a in parts]
    mlp = gated_mlp_engines(
        m, shape, sb, 0, lambda g, k: [a[:, g, k] for a in gu_w], lambda g, r: [a[:, 3 * g + r] for a in down_w],
        None, True, turned_banks=1)
    multiply, turn, add = mlp.multiply, mlp.turn, mlp.add
    activate, store_turned, gate = mlp.activate, mlp.store_turned, mlp.gate
    store_low = mlp.store_low
    lru_psum = m.banks[0:N2, 4 + 1, :]

    def sync(sp):
        sp.dma_start(w_b[:], dram["lru_b"]).then_inc(loaded.sem, 16)
        sp.dma_start(w_c[:], dram["lru_c"]).then_inc(loaded.sem, 16)
        sp.dma_start(skip[:], dram["lru_d"].broadcast_to([P, D])).then_inc(skip_loaded.sem, 16)

    def tensor(pe):
        wait_xnT(m, pe)
        clear_acc(m, pe)
        pe.wait_ge(loaded.sem, loaded.at(32))
        for k in range(KD):
            last = nc.tensor.matmul(lru_psum, w_b[:, k], m.xnT[:, k], start=k == 0, stop=k == KD - 1)
        last.then_inc(projected.sem, 1)

        def double(s):
            pe.wait_ge(h_ready.sem, h_ready.at(s + 1))
            shift = 1 << s
            nc.tensor.matmul(lru_psum[:, shift:], m.lru_step[:, s], h[:, 0:T - shift], start=True, stop=True)\
              .then_inc(stepped.sem, 1)

        double(0)
        pe.wait_ge(piece_split.sem, piece_split.at(1))
        multiply(0, 0, 0)
        for n in range(ITEMS):
            double(n + 1)
            if n + 1 < ITEMS:
                if n + 1 == NT:
                    pe.wait_ge(piece_split.sem, piece_split.at(3))
                multiply((n + 1) % NT, (n + 1) % 2, (n + 1) // NT)
            turn(pe, n, n % 2)
            if n == 1:
                pe.wait_ge(piece_split.sem, piece_split.at(2))
            if n:
                add(pe, n - 1, (n - 1) % NT, (n - 1) % 2, (n - 1) // NT)
        pe.wait_ge(h_ready.sem, h_ready.at(STEPS + 1))
        for t in range(NT):
            nc.tensor.matmul(m.acc_tile(t), h[:, t * P:(t + 1) * P], w_c[:], start=False, stop=False,
                             skip_group_check=True)
        add(pe, ITEMS - 1, NT - 1, 1, 1)

    def vector(dve):
        dve.wait_ge(loaded.sem, loaded.at(32))
        dve.wait_ge(projected.sem, projected.at(1))
        nc.vector.tensor_scalar(w_c[STATES:], w_c[STATES:], -1.0, None, ALU.mult)
        nc.vector.tensor_scalar(h[:], lru_psum, m.lru_gamma[:], None, ALU.mult).then_inc(h_ready.sem, 1)

        def double(s):
            dve.wait_ge(h_ready.sem, h_ready.at(s + 1))
            dve.wait_ge(stepped.sem, stepped.at(s + 1))
            shift = 1 << s
            nc.vector.tensor_tensor(h[:, shift:], h[:, shift:], lru_psum[:, shift:], ALU.add)\
              .then_inc(h_ready.sem, 1)

        double(0)
        gate(dve, 0, None, 0, 0)
        for n in range(ITEMS):
            double(n + 1)
            if n + 1 < ITEMS:
                gate(dve, n + 1, None, (n + 1) % NT, (n + 1) % 2)
            store_low(dve, n, n % 2)

    def scalar(act):
        def high(piece):
            at = slice(*pieces[piece])
            nc.scalar.activation(parts[0][:, at], m.lut_w[:, at], ACT.Copy).then_inc(piece_high.sem, 1)

        high(0)
        high(2)
        high(1)
        activate(act, 0, 0)
        for n in range(ITEMS):
            if n + 1 < ITEMS:
                activate(act, n + 1, (n + 1) % 2)
            store_turned(act, n, n % 2)

    def gpsimd(pool):
        for n, piece in enumerate((0, 2, 1)):
            at = slice(*pieces[piece])
            pool.wait_ge(piece_high.sem, piece_high.at(n + 1))
            nc.gpsimd.tensor_tensor(parts[1][:, at], m.lut_w[:, at], parts[0][:, at].bitcast(FP32),
                                    ALU.subtract).then_inc(piece_split.sem, 1)
        pool.wait_ge(skip_loaded.sem, skip_loaded.at(16))
        pool.wait_ge(m.sig("ln_normed").sem, m.sig("ln_normed").at(NT))
        nc.gpsimd.tensor_tensor(extra[:], m.xn[:], skip[:].unsqueeze(1).broadcast_to([P, NT, D]), ALU.mult)\
          .then_inc(skip_step.sem, 1)
        pool.wait_ge(skip_step.sem, skip_step.at(1))
        nc.gpsimd.tensor_tensor(m.x_of[b][:], m.x_of[b][:], extra[:], ALU.add)

    def close():
        mlp.close()
        piece_high.close(3)
        piece_split.close(3)
        loaded.close(32)
        skip_loaded.close(16)
        skip_step.close(1)
        for s, n in ((projected, 1), (h_ready, STEPS + 1), (stepped, STEPS)):
            s.close(n)

    return Stage(close, sync, tensor, vector, scalar, gpsimd)


def finish(m, b, out, ctx):
    nc, x = m.nc, m.x_of[b]
    joined, stored = m.sig("sequence_joined"), m.sig("sequence_stored")

    def vector(dve):
        for h in range(2):
            x_pair = x[:, 2 * h:2 * h + 2].rearrange("p t d -> p (t d)")
            nc.vector.tensor_tensor(x_pair, x_pair, m.acc[:, h, :], ALU.add).then_inc(joined.sem, 1)

    def tensor(pe):
        pe.wait_ge(joined.sem, joined.at(2))

    def sync(sp):
        for h in range(2):
            sp.wait_ge(joined.sem, joined.at(h + 1))
            sp.dma_start(out[b, h * 2 * P:(h + 1) * 2 * P].rearrange("(t p) d -> p t d", p=P),
                         x[:, 2 * h:2 * h + 2]).then_inc(stored.sem, 16)

    def last_sync(sp):
        sp.wait_ge(stored.sem, stored.at(32))

    def close():
        joined.close(2)
        stored.close(32)

    return Stage(close, sync=sync, tensor=tensor, vector=vector), Stage(sync=last_sync)


def attention_layer(m, b, layer, ctx, before=()):
    experts, ahead = mixture(m, layer, ctx)
    first, first_scalar, heads = attention(m, layer, ctx, ahead=ahead)
    norm = normalise(m, b, layer, first_scalar)
    run(m, first, *before, norm, heads, experts)


def hybrid_stack_kernel(nc, dram, out):
    with ExitStack() as ctx:
        m = Machine(nc, ctx, dram)
        before = []
        for b in range(BATCH):
            if b == 0:
                with ExitStack() as rows_ctx:
                    spline = SplineRows(m, rows_ctx)
                    constants, decay, powers = transition(m, rows_ctx)
                    with ExitStack() as layer_ctx:
                        first, first_scalar, heads = attention(m, 0, layer_ctx, spline)
                        norm = normalise(m, b, 0, first_scalar)
                        run(m, constants, first, norm, decay, heads)
                    with ExitStack() as layer_ctx:
                        experts, _ = mixture(m, 0, layer_ctx, with_table=True, merged=False)
                        run(m, experts)
                    run(m, spline.turn(), powers)
            else:
                with ExitStack() as layer_ctx:
                    attention_layer(m, b, 0, layer_ctx, before)
            with ExitStack() as layer_ctx:
                scan, mean_square, inverse_root = state_space(m, b, layer_ctx)
                norm = normalise(m, b, 1, mean_square, inverse_root)
                run(m, norm, scan)
            with ExitStack() as layer_ctx:
                run(m, normalise(m, b, 2), linear_recurrence(m, b, layer_ctx))
            with ExitStack() as layer_ctx:
                attention_layer(m, b, 3, layer_ctx)
            before = finish(m, b, out, ctx)
        run(m, *before)



def shape_constants():
    f32, bf16 = np.float32, np.dtype("bfloat16")
    out = {"ident": np.eye(P, dtype=f32), "ident_bf": np.eye(P).astype(bf16)}
    i = np.arange(P)
    out["mask_bf"] = np.where(i[None, :] > i[:, None], MASKED, 0.0).astype(bf16)
    freq = (f32(1.0 / 1024.0) ** np.linspace(0.0, 1.0, HD // 4, dtype=f32)).astype(f32)
    theta = np.arange(T, dtype=f32)[None, :] * freq[:, None]
    cos, sin = np.cos(theta.astype(np.float64)), np.sin(theta.astype(np.float64))
    out["rope_cos"] = np.concatenate([cos, cos]).astype(f32)
    out["rope_sin"] = np.concatenate([-sin, sin]).astype(f32)
    rows = np.arange(6 * NS)[:, None, None] % (2 * NS) == np.arange(2 * NS)[None, :, None]
    out["ones"] = np.ones((1, P), f32)
    out["select"] = np.broadcast_to(rows, (6 * NS, 2 * NS, P)).astype(bf16)
    p = np.arange(2 * STATES)
    out["lru_fold"] = (p[:, None] % STATES == np.arange(STATES)[None, :]).astype(f32)
    re, im = (p < STATES).astype(f32), (p >= STATES).astype(f32)
    out["lru_sign"] = np.stack([re, -im, im, re], 1)
    base, frac, at = spline_grid()
    coef = np.zeros((P * 8, WINDOW, D), np.float64)
    f = frac.astype(np.float64)
    blend = (0.5 * (-f + 2 * f ** 2 - f ** 3), 0.5 * (2 - 5 * f ** 2 + 3 * f ** 3),
             0.5 * (f + 4 * f ** 2 - 3 * f ** 3), 0.5 * (-f ** 2 + f ** 3))
    r, c = np.arange(P * 8)[:, None], np.arange(D)[None, :]
    for k in range(4):
        coef[r, at + k, c] += blend[k]
    out["spline_coef"] = coef.astype(f32)[spline_rows_of()]
    return out


def spline_grid():
    n = INTER1 * D
    t = np.linspace(0.0, NCTRL - 1.0, n, dtype=np.float64)
    i = np.clip(np.floor(t).astype(np.int64), 0, NCTRL - 2)
    frac = (t - i).astype(np.float32).reshape(P * 8, D)
    i = i.reshape(P * 8, D)
    base = i[:, 0] - 1
    at = i - 1 - base[:, None]
    assert at.max() + 3 < WINDOW
    return base, frac, at


def spline_rows_of():
    half, q, p = np.meshgrid(np.arange(2), np.arange(4), np.arange(P), indexing="ij")
    return (4 * (half * P + p) + q).reshape(8, P)


def by_rows(w, rows=P):
    return np.ascontiguousarray(w.reshape(-1, rows, w.shape[-1]).transpose(1, 0, 2))


def laid_out(v):
    out = {"x": v["L0_attn_x"]}
    order = np.concatenate([np.arange(0, 32), np.arange(64, 96), np.arange(32, 64), np.arange(96, 128)])

    def heads(mats, wo):
        parts = [w.reshape(KD, P, HEADS, HD).transpose(2, 1, 0, 3).reshape(HEADS, P, KD * HD) for w in mats]
        return np.ascontiguousarray(np.concatenate(parts + [wo.reshape(HEADS, HD, D)], 2))

    q, k, w = (v[f"L0_attn_W{c}"].T.reshape(D, HEADS, HD) for c in "qkv")
    out["heads0"] = heads([q[..., order], k[..., order], w], v["L0_attn_Wo"].T)
    q, k, w = (v[f"L3_attn_w_{c}"].reshape(D, HEADS, HD) for c in "qkv")
    out["heads3"] = heads([q, k, w], v["L3_attn_w_o"])
    out["biases3"] = np.ascontiguousarray(np.stack([v[f"L3_attn_b_{c}"].reshape(HEADS, HD).T for c in "qkv"], 2))
    out["bo"] = v["L3_attn_b_o"].reshape(1, D)

    def gate_up(gate, up):
        both = np.stack([gate, up], 1).reshape(KD, P, 2, GROUPS, -1)
        return np.ascontiguousarray(both.transpose(3, 1, 0, 2, 4).reshape(GROUPS, P, -1))

    def down(w):
        w = w.reshape(GROUPS, -1, P, D)
        return np.ascontiguousarray(w.transpose(0, 2, 1, 3).reshape(GROUPS, P, -1))

    experts = lambda gate_up, down: np.ascontiguousarray(np.concatenate([gate_up, down], 2))
    out["router0"] = by_rows(v["L0_ffn_router_w"].T)
    out["experts0"] = experts(gate_up(*(v[f"L0_ffn_{c}_w"].transpose(2, 0, 1).reshape(D, -1) for c in ("gate", "up"))),
                              down(v["L0_ffn_down_w"].transpose(0, 2, 1).reshape(E0 * I0, D)))
    gu = v["L3_ffn_gate_up"].transpose(1, 0, 2).reshape(D, E3, 2, I3)
    out["router3"] = by_rows(v["L3_ffn_gate_w"])
    out["experts3"] = experts(gate_up(gu[:, :, 0].reshape(D, -1), gu[:, :, 1].reshape(D, -1)),
                              down(v["L3_ffn_down"].reshape(E3 * I3, D)))
    out["router_scale"] = np.ascontiguousarray(v["L3_ffn_router_scale"].reshape(KD, P).T)
    out["per_expert"] = v["L3_ffn_per_expert_scale"].reshape(1, E3)

    out["w_norm"] = np.ascontiguousarray(v["L1_attn_w_norm"].reshape(KD, P).T)
    out["w_in"] = by_rows(v["L1_attn_W_in"])
    out["w_xp"] = by_rows(v["L1_attn_W_xp"])
    out["w_dt"] = v["L1_attn_W_dt"]
    out["w_out"] = by_rows(v["L1_attn_W_out"])
    vec = np.concatenate([v["L1_attn_conv_w"], v["L1_attn_conv_b"][None], v["L1_attn_b_dt"][None],
                          v["L1_attn_D"][None]])
    out["ss_vec"] = np.ascontiguousarray(vec.reshape(7, KC, P).transpose(2, 1, 0))
    out["a_log"] = by_rows(v["L1_attn_A_log"])
    base, _, _ = spline_grid()
    window = np.clip(base[:, None] + np.arange(WINDOW), 0, NCTRL - 1)[spline_rows_of()]
    points = np.stack([v[f"L1_ffn_{c}_cp"][window] for c in ("gate", "up", "down")], 2)
    out["spline_points"] = np.ascontiguousarray(points.transpose(1, 0, 2, 3))

    out["lru_in"] = np.stack([np.tile(v["L2_attn_nu_log"], 2), np.tile(v["L2_attn_theta_log"], 2)], 1)
    out["lru_b"] = by_rows(np.concatenate([v["L2_attn_B_re"], v["L2_attn_B_im"]]).T)
    out["lru_c"] = np.ascontiguousarray(np.concatenate([v["L2_attn_C_re"].T, v["L2_attn_C_im"].T]))
    out["lru_d"] = v["L2_attn_D"].reshape(1, D)
    out["lut"] = v["L2_ffn_lut"].reshape(1, LUT)
    gu = np.stack([v["L2_ffn_gate_idx"].T, v["L2_ffn_up_idx"].T], 1)
    gu = gu.reshape(KD, P, 2, 2, F2).transpose(1, 3, 0, 2, 4).reshape(P, -1)
    dn = np.zeros((2, 3 * P, D), v["L2_ffn_down_idx"].dtype)
    dn[:, :F2] = v["L2_ffn_down_idx"].T.reshape(2, F2, D)
    dn = dn.reshape(6, P, D).transpose(1, 0, 2).reshape(P, -1)
    idx = np.concatenate([gu, dn], 1).reshape(P, GROUPS, LUT_CHUNK)
    out["lut_idx"] = np.ascontiguousarray(idx.transpose(1, 0, 2))
    return out


def kernel(**inputs):
    import concourse.bacc as bacc
    from concourse.bass_utils import run_bass_kernel_spmd

    arrays = laid_out({name: np.asarray(a) for name, a in inputs.items()})
    arrays.update(shape_constants())
    arrays = {f"in_{name}": np.ascontiguousarray(a) for name, a in arrays.items()}
    nc = bacc.Bacc("TRN2", target_bir_lowering=False, num_devices=1)
    dram = {name[3:]: nc.dram_tensor(name, a.shape, mybir.dt.from_np(a.dtype), kind="ExternalInput").ap()
            for name, a in arrays.items()}
    out = nc.dram_tensor("out", (BATCH, T, D), FP32, kind="ExternalOutput").ap()
    hybrid_stack_kernel(nc, dram, out)
    result = run_bass_kernel_spmd(nc, [arrays], core_ids=[0])
    return result.results[0]["out"]
```
